# Optimizing a Trainium2 kernel written in Bass

```python
import numpy as np
import jax
import jax.numpy as jnp

def _softmax(x, axis=-1):
    return jax.nn.softmax(x, axis=axis)

def _gelu(x):
    return jax.nn.gelu(x, approximate=True)

def _silu(x):
    return jax.nn.silu(x)

def _sigmoid(x):
    return jax.nn.sigmoid(x)

def _layernorm(x, axis=-1, eps=1e-05):
    m = jnp.mean(x, axis=axis, keepdims=True)
    v = jnp.var(x, axis=axis, keepdims=True)
    return (x - m) / jnp.sqrt(v + eps)

def _scatter_add(tgt, idx, src, axis=0):
    return tgt.at[idx].add(src)

def _segment_sum(src, seg, n):
    return jax.ops.segment_sum(src, seg, n)
kernel_name = 'mk_perceiver_d2_seqx_r8_8c9961'

def setup_inputs(seed: int=0):
    np.random.seed(seed)
    _w = jnp.asarray

    def _rec_inputs():
        import jax
        import jax.numpy as jnp
        _rk = jax.random.key(seed)
        x = -0.0002928 + 1 * jax.random.normal(jax.random.fold_in(_rk, 1), (8, 32, 512), jnp.float32)
        _lenS = 32 - jax.random.randint(jax.random.fold_in(_rk, 7), (8,), 0, max(1, 32 // 4) + 1, jnp.int32)
        _lenS2 = 512 - jax.random.randint(jax.random.fold_in(_rk, 8), (8,), 0, max(1, 512 // 4) + 1, jnp.int32)
        _ctx_4096P = jax.random.normal(jax.random.fold_in(_rk, 11), (8, 16, 512), jnp.float32)
        _ctx_4096c = jax.random.dirichlet(jax.random.fold_in(_rk, 511), 0.3 * jnp.ones((16,), jnp.float32), (8, 512))
        _ctx_4096t = jnp.einsum('bsk,bkd->bsd', _ctx_4096c, _ctx_4096P)
        _ctx_4096t = _ctx_4096t * jax.lax.rsqrt(jnp.mean(jnp.square(_ctx_4096t)) + 1e-12) * 0.953939
        ctx_4096 = -2.8382e-05 + 0.999851 * (_ctx_4096t + 0.3 * jax.random.normal(jax.random.fold_in(_rk, 611), (8, 512, 512), jnp.float32))
        _validS = jnp.arange(32)[None, :] < _lenS[:, None]
        _validS2 = jnp.arange(512)[None, :] < _lenS2[:, None]
        _causal = jnp.tril(jnp.ones((32, 32), dtype=bool))
        mask_1x1xSxS2_ff0 = jnp.where(jnp.ones((1, 1, 32, 512), dtype=bool), 0.0, -1000000000.0).astype(jnp.float32)
        return (x, ctx_4096, mask_1x1xSxS2_ff0)
    x, ctx_4096, mask_1x1xSxS2_ff0 = _rec_inputs()

    def _L0_xattn_setup():
        import jax, jax.numpy as jnp
        import numpy as np
        B, Q, K, D = (1, 128, 6404, 512)
        H, KVH, HD = (32, 8, 128)
        GROUPS = H // KVH
        EPS = 1e-05

        def _rmsnorm(x, w):
            xf = x.astype(jnp.float32)
            var = jnp.mean(xf * xf, axis=-1, keepdims=True)
            return (xf * jax.lax.rsqrt(var + EPS)).astype(x.dtype) * w
        key = jax.random.key(seed)
        ks = jax.random.split(key, 8)
        s = 0.02
        return {'hidden_states': jax.random.normal(ks[0], (B, Q, D), jnp.float32), 'cross_attention_states': jax.random.normal(ks[1], (B, K, D), jnp.float32), 'attention_mask': jnp.zeros((B, 1, Q, K), jnp.float32), 'Wq': jax.random.normal(ks[2], (H * HD, D), jnp.float32) * s, 'Wk': jax.random.normal(ks[3], (KVH * HD, D), jnp.float32) * s, 'Wv': jax.random.normal(ks[4], (KVH * HD, D), jnp.float32) * s, 'Wo': jax.random.normal(ks[5], (D, H * HD), jnp.float32) * s, 'q_norm_w': jnp.ones((HD,), jnp.float32), 'k_norm_w': jnp.ones((HD,), jnp.float32)}
    _L0_xattn_all = _L0_xattn_setup()
    _L0_xattn_in = {k: v for k, v in _L0_xattn_all.items() if k in ('Wq', 'Wk', 'Wv', 'Wo', 'q_norm_w', 'k_norm_w')}
    del _L0_xattn_all

    def _L0_attn_setup():
        import jax, jax.numpy as jnp
        import numpy as np
        B, S, D = (2, 256, 512)
        NH, NKV = (32, 8)
        HD = D // NH
        NREP = NH // NKV
        SCALE = HD ** (-0.5)
        key = jax.random.key(seed)
        kx, kq, kk, kv, ko = jax.random.split(key, 5)
        s = 0.02
        return {'x': jax.random.normal(kx, (B, S, D), dtype=jnp.float32), 'wq': jax.random.normal(kq, (D, NH * HD), dtype=jnp.float32) * s, 'wk': jax.random.normal(kk, (D, NKV * HD), dtype=jnp.float32) * s, 'wv': jax.random.normal(kv, (D, NKV * HD), dtype=jnp.float32) * s, 'wo': jax.random.normal(ko, (NH * HD, D), dtype=jnp.float32) * s}
    _L0_attn_all = _L0_attn_setup()
    _L0_attn_in = {k: v for k, v in _L0_attn_all.items() if k in ('wq', 'wk', 'wv', 'wo')}
    del _L0_attn_all

    def _L0_ffn_setup():
        import jax, jax.numpy as jnp
        import numpy as np
        D = 512
        F = 1376
        B, S = (4, 256)
        key = jax.random.key(seed)
        k_x, k_g, k_u, k_d = jax.random.split(key, 4)
        scale = 0.02
        return {'x': jax.random.normal(k_x, (B, S, D), dtype=jnp.float32), 'W_gate': jax.random.normal(k_g, (F, D), dtype=jnp.float32) * scale, 'W_up': jax.random.normal(k_u, (F, D), dtype=jnp.float32) * scale, 'W_down': jax.random.normal(k_d, (D, F), dtype=jnp.float32) * scale}
    _L0_ffn_all = _L0_ffn_setup()
    _L0_ffn_in = {k: v for k, v in _L0_ffn_all.items() if k in ('W_gate', 'W_up', 'W_down')}
    del _L0_ffn_all

    def _L1_xattn_setup():
        import jax, jax.numpy as jnp
        import numpy as np
        HEADS = 32
        KV_HEADS = 8
        HEAD_DIM = 128
        EPS = 1e-06

        def rms_norm(x, w):
            var = jnp.mean(jnp.square(x.astype(jnp.float32)), axis=-1, keepdims=True)
            return (x.astype(jnp.float32) * jax.lax.rsqrt(var + EPS)).astype(x.dtype) * w
        key = jax.random.key(seed)
        ks = jax.random.split(key, 6)
        bsz, n_lat, seq, hidden = (8, 64, 512, 512)
        return {'latents': jax.random.normal(ks[0], (bsz, n_lat, hidden), jnp.float32), 'context': jax.random.normal(ks[1], (bsz, seq, hidden), jnp.float32), 'Wq': jax.random.normal(ks[2], (hidden, HEADS * HEAD_DIM), jnp.float32) * 0.02, 'Wk': jax.random.normal(ks[3], (hidden, KV_HEADS * HEAD_DIM), jnp.float32) * 0.02, 'Wv': jax.random.normal(ks[4], (hidden, KV_HEADS * HEAD_DIM), jnp.float32) * 0.02, 'Wo': jax.random.normal(ks[5], (HEADS * HEAD_DIM, hidden), jnp.float32) * 0.02, 'q_norm_w': jnp.ones((HEAD_DIM,), jnp.float32), 'k_norm_w': jnp.ones((HEAD_DIM,), jnp.float32)}
    _L1_xattn_all = _L1_xattn_setup()
    _L1_xattn_in = {k: v for k, v in _L1_xattn_all.items() if k in ('Wq', 'Wk', 'Wv', 'Wo', 'q_norm_w', 'k_norm_w')}
    del _L1_xattn_all

    def _L1_attn_setup():
        import jax, jax.numpy as jnp
        import numpy as np
        H = 512
        D = 1024
        N = 16
        K = 4
        R = 32
        BATCH = 1
        L = 256
        EPS = 1e-06

        def _rmsnorm(x, w):
            return x * jax.lax.rsqrt(jnp.mean(x * x, axis=-1, keepdims=True) + EPS) * w
        key = jax.random.key(seed)
        ks = jax.random.split(key, 10)
        s = 0.02
        return {'hidden_states': jax.random.normal(ks[0], (BATCH, L, H), jnp.float32), 'W_in': jax.random.normal(ks[1], (2 * D, H), jnp.float32) * s, 'conv_w': jax.random.normal(ks[2], (D, K), jnp.float32) * s, 'conv_b': jax.random.normal(ks[3], (D,), jnp.float32) * s, 'Wx': jax.random.normal(ks[4], (R + 2 * N, D), jnp.float32) * s, 'dt_ln_w': jnp.ones((R,), jnp.float32), 'b_ln_w': jnp.ones((N,), jnp.float32), 'c_ln_w': jnp.ones((N,), jnp.float32), 'Wdt': jax.random.normal(ks[5], (D, R), jnp.float32) * s, 'dt_bias': jax.random.normal(ks[6], (D,), jnp.float32) * s, 'A': -jnp.exp(jax.random.normal(ks[7], (D, N), jnp.float32) * 0.5), 'D_param': jnp.ones((D,), jnp.float32), 'W_out': jax.random.normal(ks[8], (H, D), jnp.float32) * s}
    _L1_attn_all = _L1_attn_setup()
    _L1_attn_in = {k: v for k, v in _L1_attn_all.items() if k in ('W_in', 'conv_w', 'conv_b', 'Wx', 'dt_ln_w', 'b_ln_w', 'c_ln_w', 'Wdt', 'dt_bias', 'A', 'D_param', 'W_out')}
    del _L1_attn_all

    def _L1_ffn_setup():
        import jax, jax.numpy as jnp
        import numpy as np
        _TRIPLES = [(1, 2, 3), (1, 4, 5), (1, 7, 6), (2, 4, 6), (2, 5, 7), (3, 4, 7), (3, 6, 5)]

        def _oct_struct():
            S = np.zeros((8, 8, 8), np.float32)
            S[0, 0, 0] = 1.0
            for i in range(1, 8):
                S[0, i, i] = 1.0
                S[i, 0, i] = 1.0
                S[i, i, 0] = -1.0
            for a, b, c in _TRIPLES:
                for x, y, z in ((a, b, c), (b, c, a), (c, a, b)):
                    S[x, y, z] = 1.0
                    S[y, x, z] = -1.0
            return jnp.asarray(S)
        S_OCT = _oct_struct()
        N_EMBD = 512
        HIDDEN = 1366

        def ternary_dequant(W):
            scale = jnp.mean(jnp.abs(W))
            Wq = scale * jnp.clip(jnp.round(W / scale), -1.0, 1.0)
            return W + jax.lax.stop_gradient(Wq - W)

        def oct_ternary_linear(xp, W):
            Wq = ternary_dequant(W)
            M = jnp.einsum('jik,jod->koid', S_OCT, Wq)
            return jnp.einsum('...id,koid->...ko', xp, M)
        key = jax.random.key(seed)
        k1, k2, k3, k4 = jax.random.split(key, 4)
        B, T = (2, 256)
        d8, h8 = (N_EMBD // 8, HIDDEN // 8)
        std_in = 1.0 / np.sqrt(N_EMBD)
        std_h = 1.0 / np.sqrt(HIDDEN)
        return {'x': jax.random.normal(k1, (B, T, N_EMBD), jnp.float32), 'w_gate': jax.random.normal(k2, (8, h8, d8), jnp.float32) * std_in, 'w_up': jax.random.normal(k3, (8, h8, d8), jnp.float32) * std_in, 'w_down': jax.random.normal(k4, (8, d8, h8), jnp.float32) * std_h}
    _L1_ffn_all = _L1_ffn_setup()
    _L1_ffn_in = {k: v for k, v in _L1_ffn_all.items() if k in ('w_gate', 'w_up', 'w_down')}
    del _L1_ffn_all
    return {'x': x, 'ctx_4096': ctx_4096, 'mask_1x1xSxS2_ff0': mask_1x1xSxS2_ff0, 'L0_xattn_Wq': _L0_xattn_in['Wq'], 'L0_xattn_Wk': _L0_xattn_in['Wk'], 'L0_xattn_Wv': _L0_xattn_in['Wv'], 'L0_xattn_Wo': _L0_xattn_in['Wo'], 'L0_xattn_q_norm_w': _L0_xattn_in['q_norm_w'], 'L0_xattn_k_norm_w': _L0_xattn_in['k_norm_w'], 'L0_attn_wq': _L0_attn_in['wq'], 'L0_attn_wk': _L0_attn_in['wk'], 'L0_attn_wv': _L0_attn_in['wv'], 'L0_attn_wo': _L0_attn_in['wo'], 'L0_ffn_W_gate': _L0_ffn_in['W_gate'], 'L0_ffn_W_up': _L0_ffn_in['W_up'], 'L0_ffn_W_down': _L0_ffn_in['W_down'], 'L1_xattn_Wq': _L1_xattn_in['Wq'], 'L1_xattn_Wk': _L1_xattn_in['Wk'], 'L1_xattn_Wv': _L1_xattn_in['Wv'], 'L1_xattn_Wo': _L1_xattn_in['Wo'], 'L1_xattn_q_norm_w': _L1_xattn_in['q_norm_w'], 'L1_xattn_k_norm_w': _L1_xattn_in['k_norm_w'], 'L1_attn_W_in': _L1_attn_in['W_in'], 'L1_attn_conv_w': _L1_attn_in['conv_w'], 'L1_attn_conv_b': _L1_attn_in['conv_b'], 'L1_attn_Wx': _L1_attn_in['Wx'], 'L1_attn_dt_ln_w': _L1_attn_in['dt_ln_w'], 'L1_attn_b_ln_w': _L1_attn_in['b_ln_w'], 'L1_attn_c_ln_w': _L1_attn_in['c_ln_w'], 'L1_attn_Wdt': _L1_attn_in['Wdt'], 'L1_attn_dt_bias': _L1_attn_in['dt_bias'], 'L1_attn_A': _L1_attn_in['A'], 'L1_attn_D_param': _L1_attn_in['D_param'], 'L1_attn_W_out': _L1_attn_in['W_out'], 'L1_ffn_w_gate': _L1_ffn_in['w_gate'], 'L1_ffn_w_up': _L1_ffn_in['w_up'], 'L1_ffn_w_down': _L1_ffn_in['w_down']}

def reference(x, ctx_4096, mask_1x1xSxS2_ff0, L0_xattn_Wq, L0_xattn_Wk, L0_xattn_Wv, L0_xattn_Wo, L0_xattn_q_norm_w, L0_xattn_k_norm_w, L0_attn_wq, L0_attn_wk, L0_attn_wv, L0_attn_wo, L0_ffn_W_gate, L0_ffn_W_up, L0_ffn_W_down, L1_xattn_Wq, L1_xattn_Wk, L1_xattn_Wv, L1_xattn_Wo, L1_xattn_q_norm_w, L1_xattn_k_norm_w, L1_attn_W_in, L1_attn_conv_w, L1_attn_conv_b, L1_attn_Wx, L1_attn_dt_ln_w, L1_attn_b_ln_w, L1_attn_c_ln_w, L1_attn_Wdt, L1_attn_dt_bias, L1_attn_A, L1_attn_D_param, L1_attn_W_out, L1_ffn_w_gate, L1_ffn_w_up, L1_ffn_w_down):
    import jax
    import jax.numpy as jnp

    def _L0_xattn_ref(hidden_states, cross_attention_states, attention_mask, Wq, Wk, Wv, Wo, q_norm_w, k_norm_w):
        import jax, jax.numpy as jnp
        import numpy as np
        B, Q, K, D = (1, 128, 6404, 512)
        H, KVH, HD = (32, 8, 128)
        GROUPS = H // KVH
        EPS = 1e-05

        def _rmsnorm(x, w):
            xf = x.astype(jnp.float32)
            var = jnp.mean(xf * xf, axis=-1, keepdims=True)
            return (xf * jax.lax.rsqrt(var + EPS)).astype(x.dtype) * w
        bsz, q_len, _ = hidden_states.shape
        kv_len = cross_attention_states.shape[1]
        q = (hidden_states @ Wq.T).reshape(bsz, q_len, H, HD).transpose(0, 2, 1, 3)
        k = (cross_attention_states @ Wk.T).reshape(bsz, kv_len, KVH, HD).transpose(0, 2, 1, 3)
        v = (cross_attention_states @ Wv.T).reshape(bsz, kv_len, KVH, HD).transpose(0, 2, 1, 3)
        q = _rmsnorm(q, q_norm_w)
        k = jnp.repeat(k, GROUPS, axis=1)
        v = jnp.repeat(v, GROUPS, axis=1)
        k = _rmsnorm(k, k_norm_w)
        scale = 1.0 / np.sqrt(HD)
        scores = jnp.einsum('bhqd,bhkd->bhqk', q, k) * scale
        scores = scores + attention_mask[:, :, :, :kv_len]
        probs = jax.nn.softmax(scores.astype(jnp.float32), axis=-1).astype(q.dtype)
        out = jnp.einsum('bhqk,bhkd->bhqd', probs, v)
        out = out.transpose(0, 2, 1, 3).reshape(bsz, q_len, H * HD)
        return out @ Wo.T

    def _L0_attn_ref(x, wq, wk, wv, wo):
        import jax, jax.numpy as jnp
        import numpy as np
        B, S, D = (2, 256, 512)
        NH, NKV = (32, 8)
        HD = D // NH
        NREP = NH // NKV
        SCALE = HD ** (-0.5)
        b, s, _ = x.shape
        q = (x @ wq).reshape(b, s, NH, HD)
        k = (x @ wk).reshape(b, s, NKV, HD)
        v = (x @ wv).reshape(b, s, NKV, HD)
        k = jnp.repeat(k, NREP, axis=2)
        v = jnp.repeat(v, NREP, axis=2)
        scores = jnp.einsum('bihd,bjhd->bhij', q, k) * SCALE
        causal = jnp.tril(jnp.ones((s, s), dtype=bool))
        scores = jnp.where(causal, scores, jnp.finfo(scores.dtype).min)
        attn = jax.nn.softmax(scores, axis=-1)
        out = jnp.einsum('bhij,bjhd->bihd', attn, v)
        out = out.reshape(b, s, NH * HD)
        return out @ wo

    def _L0_ffn_ref(x, W_gate, W_up, W_down):
        import jax, jax.numpy as jnp
        import numpy as np
        D = 512
        F = 1376
        B, S = (4, 256)
        out_shape = x.shape[:-1] + (W_down.shape[0],)
        xt = x.reshape(-1, x.shape[-1])
        up = xt @ W_up.T
        gate = jax.nn.silu(xt @ W_gate.T)
        y = gate * up @ W_down.T
        return y.reshape(out_shape)

    def _L1_xattn_ref(latents, context, Wq, Wk, Wv, Wo, q_norm_w, k_norm_w):
        import jax, jax.numpy as jnp
        import numpy as np
        HEADS = 32
        KV_HEADS = 8
        HEAD_DIM = 128
        EPS = 1e-06

        def rms_norm(x, w):
            var = jnp.mean(jnp.square(x.astype(jnp.float32)), axis=-1, keepdims=True)
            return (x.astype(jnp.float32) * jax.lax.rsqrt(var + EPS)).astype(x.dtype) * w
        bsz, q_len, hidden = latents.shape
        kv = jnp.concatenate([context, latents], axis=1)
        kv_len = kv.shape[1]
        groups = HEADS // KV_HEADS
        q = (latents @ Wq).reshape(bsz, q_len, HEADS, HEAD_DIM).transpose(0, 2, 1, 3)
        k = (kv @ Wk).reshape(bsz, kv_len, KV_HEADS, HEAD_DIM).transpose(0, 2, 1, 3)
        v = (kv @ Wv).reshape(bsz, kv_len, KV_HEADS, HEAD_DIM).transpose(0, 2, 1, 3)
        q = rms_norm(q, q_norm_w)
        k = rms_norm(k, k_norm_w)
        qg = q.reshape(bsz, KV_HEADS, groups, q_len, HEAD_DIM)
        scale = 1.0 / np.sqrt(HEAD_DIM)
        scores = jnp.einsum('bhgqd,bhkd->bhgqk', qg, k) * scale
        probs = jax.nn.softmax(scores.astype(jnp.float32), axis=-1).astype(q.dtype)
        out = jnp.einsum('bhgqk,bhkd->bhgqd', probs, v)
        out = out.reshape(bsz, HEADS, q_len, HEAD_DIM).transpose(0, 2, 1, 3)
        out = out.reshape(bsz, q_len, HEADS * HEAD_DIM)
        return out @ Wo

    def _L1_attn_ref(hidden_states, W_in, conv_w, conv_b, Wx, dt_ln_w, b_ln_w, c_ln_w, Wdt, dt_bias, A, D_param, W_out):
        import jax, jax.numpy as jnp
        import numpy as np
        H = 512
        D = 1024
        N = 16
        K = 4
        R = 32
        BATCH = 1
        L = 256
        EPS = 1e-06

        def _rmsnorm(x, w):
            return x * jax.lax.rsqrt(jnp.mean(x * x, axis=-1, keepdims=True) + EPS) * w
        proj = hidden_states @ W_in.T
        u, gate = jnp.split(proj, 2, axis=-1)
        x = jnp.transpose(u, (0, 2, 1))
        x = jax.lax.conv_general_dilated(x, conv_w[:, None, :], window_strides=(1,), padding=[(K - 1, 0)], dimension_numbers=('NCH', 'OIH', 'NCH'), feature_group_count=D)
        u = jax.nn.silu(jnp.transpose(x, (0, 2, 1)) + conv_b)
        ssm_p = u @ Wx.T
        dt, Bm, Cm = jnp.split(ssm_p, [R, R + N], axis=-1)
        dt = _rmsnorm(dt, dt_ln_w)
        Bm = _rmsnorm(Bm, b_ln_w)
        Cm = _rmsnorm(Cm, c_ln_w)
        delta = jax.nn.softplus(dt @ Wdt.T + dt_bias)

        def step(state, xs):
            d_t, B_t, C_t, u_t = xs
            dA = jnp.exp(d_t[..., None] * A)
            state = dA * state + (d_t * u_t)[..., None] * B_t[:, None, :]
            y_t = jnp.einsum('bdn,bn->bd', state, C_t)
            return (state, y_t)
        init = jnp.zeros((hidden_states.shape[0], D, N), hidden_states.dtype)
        xs = (jnp.swapaxes(delta, 0, 1), jnp.swapaxes(Bm, 0, 1), jnp.swapaxes(Cm, 0, 1), jnp.swapaxes(u, 0, 1))
        _, ys = jax.lax.scan(step, init, xs)
        y = jnp.swapaxes(ys, 0, 1) + u * D_param
        y = y * jax.nn.silu(gate)
        return y @ W_out.T

    def _L1_ffn_ref(x, w_gate, w_up, w_down):
        import jax, jax.numpy as jnp
        import numpy as np
        _TRIPLES = [(1, 2, 3), (1, 4, 5), (1, 7, 6), (2, 4, 6), (2, 5, 7), (3, 4, 7), (3, 6, 5)]

        def _oct_struct():
            S = np.zeros((8, 8, 8), np.float32)
            S[0, 0, 0] = 1.0
            for i in range(1, 8):
                S[0, i, i] = 1.0
                S[i, 0, i] = 1.0
                S[i, i, 0] = -1.0
            for a, b, c in _TRIPLES:
                for x, y, z in ((a, b, c), (b, c, a), (c, a, b)):
                    S[x, y, z] = 1.0
                    S[y, x, z] = -1.0
            return jnp.asarray(S)
        S_OCT = _oct_struct()
        N_EMBD = 512
        HIDDEN = 1366

        def ternary_dequant(W):
            scale = jnp.mean(jnp.abs(W))
            Wq = scale * jnp.clip(jnp.round(W / scale), -1.0, 1.0)
            return W + jax.lax.stop_gradient(Wq - W)

        def oct_ternary_linear(xp, W):
            Wq = ternary_dequant(W)
            M = jnp.einsum('jik,jod->koid', S_OCT, Wq)
            return jnp.einsum('...id,koid->...ko', xp, M)
        B, T, D = x.shape
        xp = x.reshape(B, T, 8, D // 8)
        gate = oct_ternary_linear(xp, w_gate).reshape(B, T, -1)
        up = oct_ternary_linear(xp, w_up).reshape(B, T, -1)
        h = jax.nn.silu(gate) * up
        hp = h.reshape(B, T, 8, h.shape[-1] // 8)
        out = oct_ternary_linear(hp, w_down).reshape(B, T, D)
        return out
    x = x + _L0_xattn_ref(_layernorm(x, axis=-1), ctx_4096, mask_1x1xSxS2_ff0, L0_xattn_Wq, L0_xattn_Wk, L0_xattn_Wv, L0_xattn_Wo, L0_xattn_q_norm_w, L0_xattn_k_norm_w)
    x = x + _L0_attn_ref(_layernorm(x, axis=-1), L0_attn_wq, L0_attn_wk, L0_attn_wv, L0_attn_wo)
    x = x + _L0_ffn_ref(_layernorm(x, axis=-1), L0_ffn_W_gate, L0_ffn_W_up, L0_ffn_W_down)
    x = x + _L1_xattn_ref(_layernorm(x, axis=-1), ctx_4096, L1_xattn_Wq, L1_xattn_Wk, L1_xattn_Wv, L1_xattn_Wo, L1_xattn_q_norm_w, L1_xattn_k_norm_w)
    x = x + _L1_attn_ref(_layernorm(x, axis=-1), L1_attn_W_in, L1_attn_conv_w, L1_attn_conv_b, L1_attn_Wx, L1_attn_dt_ln_w, L1_attn_b_ln_w, L1_attn_c_ln_w, L1_attn_Wdt, L1_attn_dt_bias, L1_attn_A, L1_attn_D_param, L1_attn_W_out)
    x = x + _L1_ffn_ref(_layernorm(x, axis=-1), L1_ffn_w_gate, L1_ffn_w_up, L1_ffn_w_down)
    return x

_drawn_inputs = setup_inputs


def setup_inputs(seed=0):
    import zlib

    import numpy as np

    out = dict(_drawn_inputs(seed))
    spreads = {'L0_xattn_q_norm_w': (1.0, 0.6),
     'L0_xattn_k_norm_w': (1.0, 0.6),
     'L1_xattn_q_norm_w': (1.0, 0.6),
     'L1_xattn_k_norm_w': (1.0, 0.6),
     'L1_attn_dt_ln_w': (1.0, 0.6),
     'L1_attn_b_ln_w': (1.0, 0.6),
     'L1_attn_c_ln_w': (1.0, 0.6),
     'L1_attn_D_param': (1.0, 0.6)}
    factors = {'L0_attn_wq': 5.617,
     'L0_attn_wk': 5.617,
     'L1_attn_W_in': 3.993,
     'L1_attn_conv_w': 4.911,
     'L1_attn_conv_b': 5.359,
     'L1_attn_Wx': 5.015,
     'L1_attn_Wdt': 8.0,
     'L1_attn_dt_bias': 8.0,
     'L1_attn_A': 8.0,
     'L1_attn_W_out': 4.085,
     'L1_ffn_w_gate': 2.951,
     'L1_ffn_w_up': 2.832,
     'L1_ffn_w_down': 2.828}
    for name, (base, spread) in spreads.items():
        noise = np.random.default_rng([zlib.crc32(name.encode()), seed]).standard_normal(out[name].shape)
        drawn = base * np.exp(spread * noise) if base else spread * noise
        out[name] = jnp.asarray(drawn.astype(out[name].dtype))
    for name, factor in factors.items():
        out[name] = (out[name] * factor).astype(out[name].dtype)
    return out
```

```python
from contextlib import ExitStack, contextmanager

import numpy as np
import concourse.bass as bass
from concourse import mybir

F32 = mybir.dt.float32
F32R = mybir.dt.float32r
ALU = mybir.AluOpType
ACT = mybir.ActivationFunctionType
AX = mybir.AxisListType

P = 128
B, Q, D = 8, 32, 512
KEYS = 512
TOK = B * Q
TT = TOK // P
BT = P // Q
DC = D // P
KVH, GRP, HD = 8, 4, 128
COLS = 512
KVCOLS = 2 * KVH * HD
FFN = 1376
CHUNKS = KEYS // P


class Ctx:
    pass


def tiles(stack, nc):
    def sb(name, shape, dt=F32):
        return stack.enter_context(nc.sbuf_tensor(name, shape, dt))

    def ps(name, shape):
        return stack.enter_context(nc.psum_tensor(name, shape, F32))

    def sem(name):
        return nc.alloc_semaphore(name)

    return sb, ps, sem


@contextmanager
def own_semaphores(nc):
    before = nc.snapshot_sems()
    yield
    nc.all_engine_barrier()
    nc.clear_and_free_semaphores(nc.allocated_since(before))
    nc.all_engine_barrier()


def split_matmul(pe, out, a_hi, a_lo, b_hi, b_lo, first, last):
    pe.matmul(out, a_hi, b_hi, start=first, stop=False)
    pe.matmul(out, a_hi, b_lo, start=False, stop=False)
    return pe.matmul(out, a_lo, b_hi, start=False, stop=last)


def stage_constants(c, x_dram):
    nc = c.nc
    with ExitStack() as st:
        sb, ps, sem = tiles(st, nc)
        x_in, ident0, ident1 = sem("x_in"), sem("ident0"), sem("ident1")
        block = st.enter_context(nc.Block())

        @block.sync
        def _(sp):
            sp.dma_start(c.x[:], x_dram.rearrange("(t p) d -> p t d", p=P)).then_inc(x_in, 16)
            sp.wait_ge(x_in, 16)

        @block.gpsimd
        def _(pool):
            pool.memset(c.ident[:], 0.0).then_inc(ident0, 1)
            pool.memset(c.minus_half[:], -0.5)
            pool.wait_ge(ident0, 1)
            pool.affine_select(out=c.ident[:], in_=c.ident[:], compare_op=ALU.not_equal, fill=1.0,
                               base=0, pattern=[[-1, P]], channel_multiplier=1).then_inc(ident1, 1)
            pool.wait_ge(ident1, 1)


def stage_layernorm(c, tag, xT_hi, xT_lo):
    nc = c.nc
    with ExitStack() as st:
        sb, ps, sem = tiles(st, nc)
        stats = sb(f"{tag}_stats", [P, TT, 6])
        mv = sb(f"{tag}_mv", [P, TT, 2])
        var = sb(f"{tag}_var", [P, TT])
        rstd = sb(f"{tag}_rstd", [P, TT])
        xn = sb(f"{tag}_xn", [P, TT, D])
        xT_ps = [ps(f"{tag}_xT_ps{t}", [P, DC * P]) for t in range(TT)]
        stats_done, mv_done = sem(f"{tag}_stats_done"), sem(f"{tag}_mv_done")
        var_done, rstd_done = sem(f"{tag}_var_done"), sem(f"{tag}_rstd_done")
        xn_done, xT_ready, hi_done, lo_done = (sem(f"{tag}_{n}") for n in ("xn_done", "xT_ready", "hi_done", "lo_done"))
        block = st.enter_context(nc.Block())

        @block.vector
        def _(dve):
            for t in range(TT):
                dve.bn_stats(stats[:, t, :], c.x[:, t, :]).then_inc(stats_done, 1)
            for t in range(TT):
                dve.wait_ge(stats_done, t + 1)
                dve.bn_aggr(mv[:, t, :], stats[:, t, :]).then_inc(mv_done, 1)
            for t in range(TT):
                dve.wait_ge(rstd_done, 1)
                dve.wait_ge(mv_done, TT)
                dve.tensor_scalar(xn[:, t, :], c.x[:, t, :], mv[:, t, 0:1], rstd[:, t:t + 1],
                                  ALU.subtract, ALU.mult).then_inc(xn_done, 1)
            for t in range(TT):
                dve.wait_ge(hi_done, t + 1)
                dve.tensor_tensor(xT_lo[:, :, t * P:(t + 1) * P],
                                  xT_ps[t][:].rearrange("p (c n) -> p c n", c=DC),
                                  xT_hi[:, :, t * P:(t + 1) * P].bitcast(F32), ALU.subtract).then_inc(lo_done, 1)

        @block.gpsimd
        def _(pool):
            pool.wait_ge(mv_done, TT)
            pool.tensor_scalar(var[:], mv[:, :, 1], 1e-5, None, ALU.add).then_inc(var_done, 1)
            pool.wait_ge(var_done, 1)
            pool.tensor_tensor(rstd[:], var[:], c.minus_half[:, 0:TT], ALU.pow).then_inc(rstd_done, 1)

        @block.tensor
        def _(pe):
            for t in range(TT):
                pe.wait_ge(xn_done, t + 1)
                for k in range(DC):
                    last = pe.transpose(xT_ps[t][:, k * P:(k + 1) * P], xn[:, t, k * P:(k + 1) * P], c.ident[:])
                last.then_inc(xT_ready, 1)

        @block.scalar
        def _(act):
            for t in range(TT):
                act.wait_ge(xT_ready, t + 1)
                act.activation(xT_hi[:, :, t * P:(t + 1) * P],
                               xT_ps[t][:].rearrange("p (c n) -> p c n", c=DC), ACT.Copy).then_inc(hi_done, 1)


def stage_queries(c, tag, wq_dram, wkv_dram, norm_w_dram, eps, xT_hi, xT_lo, w_hi, w_lo, q_dram,
                  klat_dram, vlat_dram):
    nc = c.nc
    with_latents = klat_dram is not None
    q_groups = KVH
    kv_groups = KVCOLS // COLS
    groups = q_groups + kv_groups
    items = [("q", g, t) for g in range(q_groups) for t in range(TT)]
    if with_latents:
        items += [("k", g, t) for g in range(kv_groups // 2) for t in range(TT)]
        items += [("v", g, t) for g in range(kv_groups // 2, kv_groups) for t in range(TT)]
    n_norm = sum(kind != "v" for kind, _, _ in items)

    with ExitStack() as st:
        sb, ps, sem = tiles(st, nc)
        raw = sb(f"{tag}_raw", [P, 2, DC, COLS])
        wq_hi = sb(f"{tag}_wq_hi", [P, 2, DC, COLS], F32R)
        wq_lo = sb(f"{tag}_wq_lo", [P, 2, DC, COLS], F32R)
        sq = sb(f"{tag}_sq", [P, COLS])
        ss = sb(f"{tag}_ss", [P, 2, GRP])
        ms = sb(f"{tag}_ms", [P, 2, GRP])
        rr = sb(f"{tag}_rr", [P, 2, GRP])
        nrm = sb(f"{tag}_nrm", [P, 2, COLS])
        stg = sb(f"{tag}_stg", [P, 2, COLS])
        nw = sb(f"{tag}_nw", [P, 2])
        qkw = sb(f"{tag}_qkw", [P, 1])
        proj = [ps(f"{tag}_proj{i}", [P, COLS]) for i in range(2)]
        turn = [ps(f"{tag}_turn{i}", [P, COLS]) for i in range(2)]
        raw_in = [sem(f"{tag}_raw_in{i}") for i in range(2)]
        nw_in, qkw_done = sem(f"{tag}_nw_in"), sem(f"{tag}_qkw_done")
        w_hi_done, w_lo_done = sem(f"{tag}_w_hi_done"), sem(f"{tag}_w_lo_done")
        proj_ready, sq_done, ss_done, ms_done, rr_done, nrm_done, turn_ready, stg_done = (
            sem(f"{tag}_{n}") for n in ("proj_ready", "sq_done", "ss_done", "ms_done", "rr_done", "nrm_done",
                                        "turn_ready", "stg_done"))
        stored = [sem(f"{tag}_stored{i}") for i in range(2)]
        block = st.enter_context(nc.Block())

        def weights(g):
            if g < q_groups:
                return wq_hi[:, g % 2], wq_lo[:, g % 2]
            cols = slice((g - q_groups) * COLS, (g - q_groups + 1) * COLS)
            return w_hi[:, :, cols], w_lo[:, :, cols]

        @block.sync
        def _(sp):
            for i, w in enumerate(norm_w_dram):
                sp.dma_start(nw[:, i:i + 1], w.rearrange("(p o) -> p o", o=1)).then_inc(nw_in, 16)
            def load(g):
                if g >= 2:
                    sp.wait_ge(w_lo_done, g - 1)
                src = wq_dram[g] if g < q_groups else wkv_dram[g - q_groups]
                sp.dma_start(raw[:, g % 2], src).then_inc(raw_in[g % 2], 16)

            load(0)
            load(1)
            for i, (kind, g, t) in enumerate(items):
                if i < TT * q_groups and i % TT == 0:
                    load(i // TT + 2)
                if i == TT * q_groups - 1:
                    for left in range(q_groups + 2, groups):
                        load(left)
                sp.wait_ge(stg_done, i + 1)
                src = stg[:, i % 2, :]
                if kind == "v":
                    cols = slice((g - kv_groups // 2) * COLS, (g - kv_groups // 2 + 1) * COLS)
                    dst = vlat_dram.rearrange("b q n -> (b q) n")[t * P:(t + 1) * P, cols]
                elif kind == "q":
                    dst = q_dram[t * BT:(t + 1) * BT, :, g, :].rearrange("b p n -> p b n")
                    src = src.rearrange("p (b n) -> p b n", b=BT)
                else:
                    dst = klat_dram[t * BT:(t + 1) * BT, :, g * GRP:(g + 1) * GRP, :].rearrange("b p g n -> p b (g n)")
                    src = src.rearrange("p (b n) -> p b n", b=BT)
                sp.dma_start(dst, src).then_inc(stored[i % 2], 16)
            n = len(items)
            sp.wait_ge(stored[0], 16 * ((n + 1) // 2))
            sp.wait_ge(stored[1], 16 * (n // 2))

        @block.scalar
        def _(act):
            def make_hi(g):
                act.wait_ge(raw_in[g % 2], 16 * (g // 2 + 1))
                if 2 <= g < q_groups:
                    act.wait_ge(proj_ready, TT * (g - 1))
                act.activation(weights(g)[0], raw[:, g % 2], ACT.Copy).then_inc(w_hi_done, 1)

            def square(i):
                act.wait_ge(proj_ready, i + 1)
                if i:
                    act.wait_ge(ss_done, i)
                act.activation(sq[:], proj[i % 2][:], ACT.Square).then_inc(sq_done, 1)

            def turned(i, m):
                kind, g, t = items[i]
                if i >= 2:
                    act.wait_ge(stored[i % 2], 16 * (i // 2))
                if kind == "v":
                    act.wait_ge(proj_ready, i + 1)
                    act.activation(stg[:, i % 2, :], proj[i % 2][:], ACT.Copy).then_inc(stg_done, 1)
                    return
                act.wait_ge(turn_ready, m + 1)
                out = stg[:, i % 2, :].rearrange("p (b g n) -> p g b n", b=BT, g=GRP)
                src = turn[m % 2][:].rearrange("p (g b n) -> p g b n", b=BT, g=GRP)
                if kind == "q":
                    if i == 0:
                        act.wait_ge(qkw_done, 1)
                    act.activation(out, src, ACT.Copy, scale=qkw[:, 0:1]).then_inc(stg_done, 1)
                else:
                    act.activation(out, src, ACT.Copy).then_inc(stg_done, 1)

            make_hi(0)
            made = 1
            for i in range(len(items) + 1):
                if i % TT == 0 and made < groups:
                    make_hi(made)
                    made += 1
                if i < n_norm:
                    square(i)
                if 1 <= i <= n_norm:
                    turned(i - 1, i - 1)
                if i == n_norm and with_latents:
                    for v in range(n_norm, len(items)):
                        turned(v, None)
                    break
                if i == 2 * q_groups - 1:
                    while made < groups:
                        make_hi(made)
                        made += 1

        @block.vector
        def _(dve):
            dve.wait_ge(nw_in, 32)
            dve.tensor_scalar(qkw[:], nw[:, 0:1], nw[:, 1:2], float(HD) ** -0.5, ALU.mult,
                              ALU.mult).then_inc(qkw_done, 1)

            def make_lo(g):
                dve.wait_ge(w_hi_done, g + 1)
                dve.tensor_tensor(weights(g)[1], raw[:, g % 2], weights(g)[0].bitcast(F32),
                                  ALU.subtract).then_inc(w_lo_done, 1)

            make_lo(0)
            made = 1
            for i in range(n_norm):
                if i % TT == 0 and made < groups:
                    make_lo(made)
                    made += 1
                if i == 2 * q_groups - 1:
                    while made < groups:
                        make_lo(made)
                        made += 1
                dve.wait_ge(sq_done, i + 1)
                dve.tensor_reduce(ss[:, i % 2, :], sq[:].rearrange("p (g n) -> p g n", g=GRP), AX.X,
                                  ALU.add).then_inc(ss_done, 1)
                dve.wait_ge(rr_done, i + 1)
                if i >= 2:
                    dve.wait_ge(turn_ready, i - 1)
                dve.tensor_tensor(nrm[:, i % 2, :].rearrange("p (g n) -> p g n", g=GRP),
                                  proj[i % 2][:].rearrange("p (g n) -> p g n", g=GRP),
                                  rr[:, i % 2, :].unsqueeze(2).to_broadcast([P, GRP, HD]),
                                  ALU.mult).then_inc(nrm_done, 1)

        @block.gpsimd
        def _(pool):
            for i in range(n_norm):
                pool.wait_ge(ss_done, i + 1)
                pool.tensor_scalar(ms[:, i % 2, :], ss[:, i % 2, :], 1.0 / HD, eps, ALU.mult,
                                   ALU.add).then_inc(ms_done, 1)
                pool.wait_ge(ms_done, i + 1)
                if i >= 2:
                    pool.wait_ge(nrm_done, i - 1)
                pool.tensor_tensor(rr[:, i % 2, :], ms[:, i % 2, :], c.minus_half[:, 0:GRP],
                                   ALU.pow).then_inc(rr_done, 1)

        @block.tensor
        def _(pe):
            def turn_rows(m):
                pe.wait_ge(nrm_done, m + 1)
                if m >= 2:
                    pe.wait_ge(stg_done, m - 1)
                for g in range(GRP):
                    last = pe.transpose(turn[m % 2][:, g * P:(g + 1) * P], nrm[:, m % 2, g * P:(g + 1) * P],
                                        c.ident[:])
                last.then_inc(turn_ready, 1)

            for i, (kind, g, t) in enumerate(items):
                at = g if kind == "q" else q_groups + g
                pe.wait_ge(w_lo_done, at + 1)
                if i >= 2:
                    if i - 2 < n_norm:
                        pe.wait_ge(nrm_done, i - 1)
                    else:
                        pe.wait_ge(stg_done, i - 1)
                hi, lo = weights(at)
                for k in range(DC):
                    toks = slice(t * P, (t + 1) * P)
                    last = split_matmul(pe, proj[i % 2][:], xT_hi[:, k, toks], xT_lo[:, k, toks], hi[:, k], lo[:, k],
                                        k == 0, k == DC - 1)
                last.then_inc(proj_ready, 1)
                if 1 <= i <= n_norm:
                    turn_rows(i - 1)
            if n_norm == len(items):
                turn_rows(n_norm - 1)


def stage_context(c, tag, ctxT_dram, mask_dram, eps, w_hi, w_lo, q_dram, klat_dram, vlat_dram, o_dram):
    nc = c.nc
    with_latents = klat_dram is not None
    with_mask = mask_dram is not None
    NK = KEYS + (Q if with_latents else 0)
    ROWS = GRP * Q
    assert ROWS == P
    HPC = KVH // CHUNKS

    with ExitStack() as st:
        sb, ps, sem = tiles(st, nc)
        ct_raw = sb(f"{tag}_ct_raw", [P, 2, DC, P])
        ct_hi = sb(f"{tag}_ct_hi", [P, 2, DC, P], F32R)
        ct_lo = sb(f"{tag}_ct_lo", [P, 2, DC, P], F32R)
        ksq = sb(f"{tag}_ksq", [P, COLS])
        kss = sb(f"{tag}_kss", [P, 2, GRP])
        kms = sb(f"{tag}_kms", [P, 2, GRP])
        krr = sb(f"{tag}_krr", [P, 2, GRP])
        khat = sb(f"{tag}_khat", [P, 2, COLS])
        kT = sb(f"{tag}_kT", [P, 2, KVH, KEYS])
        vv = sb(f"{tag}_vv", [P, 2, CHUNKS, KVH * HD])
        qcur = sb(f"{tag}_qcur", [P, 2, KVH, ROWS])
        ocur = sb(f"{tag}_ocur", [P, 2, KVH, ROWS])
        pr = sb(f"{tag}_pr", [P, 2, NK])
        pT = sb(f"{tag}_pT", [P, 2, KEYS])
        nmax = sb(f"{tag}_nmax", [P, 2])
        den = sb(f"{tag}_den", [P, 2])
        rden = sb(f"{tag}_rden", [P, 2])
        if with_mask:
            mask = sb(f"{tag}_mask", [P, KEYS])
            sm = sb(f"{tag}_sm", [P, KEYS])
        if with_latents:
            klat = sb(f"{tag}_klat", [P, 2, KVH, Q])
            vlat = sb(f"{tag}_vlat", [Q, 2, KVH * HD])
            pTlat = sb(f"{tag}_pTlat", [Q, 2, P])
        kp = [ps(f"{tag}_kp{i}", [P, COLS]) for i in range(2)]
        vp = ps(f"{tag}_vp", [P, COLS])
        ktp = ps(f"{tag}_ktp", [P, COLS])
        scp = ps(f"{tag}_scp", [P, 2 * COLS])
        ptp = ps(f"{tag}_ptp", [P, KEYS])
        op = ps(f"{tag}_op", [P, COLS])
        ct_in = [sem(f"{tag}_ct_in{i}") for i in range(2)]
        q_in = [sem(f"{tag}_q_in{i}") for i in range(2)]
        o_out = [sem(f"{tag}_o_out{i}") for i in range(2)]
        m_in = sem(f"{tag}_m_in")
        (ct_hi_done, ct_lo_done, k_ready, v_ready, ksq_done, kss_done, kms_done, krr_done, khat_done, ktp_ready,
         kT_done, v_done, s_ready, sm_done, nmax_done, exp_done, rden_done, pn_done, ptp_ready, pT_done, o_ready,
         o_done) = (sem(f"{tag}_{n}") for n in (
             "ct_hi_done", "ct_lo_done", "k_ready", "v_ready", "ksq_done", "kss_done", "kms_done", "krr_done",
             "khat_done", "ktp_ready", "kT_done", "v_done", "s_ready", "sm_done", "nmax_done", "exp_done", "rden_done",
             "pn_done", "ptp_ready", "pT_done", "o_ready", "o_done"))
        block = st.enter_context(nc.Block())
        Q_LOADS = 3 if with_latents else 1

        def over_batches(eng, run):
            run(0, 0)
            run(0, 1)
            with eng.Fori(1, B // 2) as pair:
                run(pair, 0)
                run(pair, 1)
            run(B // 2, 0)

        def wait(eng, semaphore, value):
            if not (isinstance(value, int) and value <= 0):
                eng.wait_ge(semaphore, value)

        def parts(pair, par):
            return not (isinstance(pair, int) and pair == B // 2), not (isinstance(pair, int) and pair == par == 0)

        def chunk_no(pair, par, t):
            return pair * (2 * CHUNKS) + (par * CHUNKS + t)

        def head_no(pair, par, t):
            return pair * (2 * KVH) + (par * KVH + t * HPC - KVH)

        @block.sync
        def _(sp):
            if with_mask:
                for g in range(GRP):
                    sp.dma_start(mask[g * Q:(g + 1) * Q, :], mask_dram).then_inc(m_in, 16)

            def load_chunk(pair, par, t):
                n = chunk_no(pair, par, t)
                wait(sp, ct_lo_done, n - 1)
                sp.dma_start(ct_raw[:, t % 2], ctxT_dram[n]).then_inc(ct_in[t % 2], 16)

            def load_queries(pair, par):
                b = pair * 2 + par
                wait(sp, s_ready, (b - 1) * KVH)
                sp.dma_start(qcur[:, par], q_dram[b]).then_inc(q_in[par], 16)
                if with_latents:
                    wait(sp, o_ready, (b - 1) * KVH)
                    sp.dma_start(klat[:, par], klat_dram[b]).then_inc(q_in[par], 16)
                    sp.dma_start(vlat[:, par], vlat_dram[b]).then_inc(q_in[par], 16)

            def store(pair, par):
                b = pair * 2 + par
                sp.wait_ge(o_done, (b - 1) * KVH)
                sp.dma_start(o_dram[b - 2], ocur[:, par]).then_inc(o_out[par], 16)

            def run(pair, par):
                project, _ = parts(pair, par)
                if project:
                    load_chunk(pair, par, 0)
                    load_chunk(pair, par, 1)
                if not (isinstance(pair, int) and pair == 0):
                    store(pair, par)
                if project:
                    load_queries(pair, par)
                    for t in range(2, CHUNKS):
                        load_chunk(pair, par, t)

            over_batches(sp, run)
            store(B // 2, 1)
            for i in range(2):
                sp.wait_ge(o_out[i], 16 * (B // 2))

        @block.scalar
        def _(act):
            def make_hi(pair, par, t):
                n = chunk_no(pair, par, t)
                act.wait_ge(ct_in[t % 2], pair * (16 * CHUNKS) + 16 * (par * CHUNKS // 2 + t // 2 + 1))
                wait(act, v_ready, (n - 1) * 2)
                act.activation(ct_hi[:, t % 2], ct_raw[:, t % 2], ACT.Copy).then_inc(ct_hi_done, 1)

            def square(n, j):
                act.wait_ge(k_ready, n * 2 + (j + 1))
                wait(act, kss_done, n * 2 + j)
                act.activation(ksq[:], kp[j][:], ACT.Square).then_inc(ksq_done, 1)

            def keys(n, j, par, t):
                act.wait_ge(ktp_ready, n * 2 + (j + 1))
                act.activation(kT[:, par, j * GRP:(j + 1) * GRP, t * P:(t + 1) * P],
                               ktp[:].rearrange("p (g n) -> p g n", g=GRP), ACT.Copy).then_inc(kT_done, 1)

            def values(n, j, par, t):
                act.wait_ge(v_ready, n * 2 + (j + 1))
                act.activation(vv[:, par, t, j * COLS:(j + 1) * COLS], vp[:], ACT.Copy).then_inc(v_done, 1)

            def exps(h, slot):
                act.wait_ge(nmax_done, h + 1)
                wait(act, ptp_ready, h - 1)
                act.activation(pr[:, slot, :], sm[:] if with_mask else scp[:, 0:NK], ACT.Exp,
                               bias=nmax[:, slot:slot + 1], accum_out=den[:, slot:slot + 1]).then_inc(exp_done, 1)

            def run(pair, par):
                project, attend = parts(pair, par)
                if project and par == 0:
                    make_hi(pair, 0, 0)
                for t in range(CHUNKS):
                    n, h = chunk_no(pair, par, t), head_no(pair, par, t)
                    if attend:
                        exps(h, 0)
                    if project:
                        if not (t == CHUNKS - 1 and par == 1):
                            make_hi(pair, par, t + 1)
                        square(n, 0)
                        square(n, 1)
                        keys(n, 0, par, t)
                    if attend:
                        exps(h + 1, 1)
                    if project:
                        values(n, 0, par, t)
                        values(n, 1, par, t)
                        keys(n, 1, par, t)

            over_batches(act, run)

        @block.vector
        def _(dve):
            def key_sums(n, j):
                dve.wait_ge(ksq_done, n * 2 + (j + 1))
                dve.tensor_reduce(kss[:, j, :], ksq[:].rearrange("p (g n) -> p g n", g=GRP), AX.X,
                                  ALU.add).then_inc(kss_done, 1)
                dve.wait_ge(kss_done, n * 2 + (j + 1))
                dve.tensor_scalar(kms[:, j, :], kss[:, j, :], 1.0 / HD, eps, ALU.mult, ALU.add).then_inc(kms_done, 1)

            def key_scale(n, j):
                dve.wait_ge(krr_done, n * 2 + (j + 1))
                wait(dve, ktp_ready, n * 2 + (j - 1))
                dve.tensor_tensor(khat[:, j, :].rearrange("p (g n) -> p g n", g=GRP),
                                  kp[j][:].rearrange("p (g n) -> p g n", g=GRP),
                                  krr[:, j, :].unsqueeze(2).to_broadcast([P, GRP, HD]), ALU.mult).then_inc(khat_done, 1)

            def row_max(h, slot):
                dve.wait_ge(s_ready, h + 1)
                if with_mask:
                    wait(dve, exp_done, h)
                    dve.tensor_tensor(sm[:], scp[:, 0:KEYS], mask[:], ALU.add).then_inc(sm_done, 1)
                    dve.wait_ge(sm_done, h + 1)
                    dve.tensor_reduce(nmax[:, slot:slot + 1], sm[:], AX.X, ALU.max,
                                      negate=True).then_inc(nmax_done, 1)
                else:
                    dve.tensor_reduce(nmax[:, slot:slot + 1], scp[:, 0:NK], AX.X, ALU.max,
                                      negate=True).then_inc(nmax_done, 1)

            def normalise(h, slot):
                dve.wait_ge(exp_done, h + 1)
                dve.reciprocal(rden[:, slot:slot + 1], den[:, slot:slot + 1]).then_inc(rden_done, 1)
                dve.wait_ge(rden_done, h + 1)
                dve.tensor_scalar(pr[:, slot, :], pr[:, slot, :], rden[:, slot:slot + 1], None,
                                  ALU.mult).then_inc(pn_done, 1)

            def probs(h, slot):
                dve.wait_ge(ptp_ready, h + 1)
                if with_latents:
                    dve.tensor_copy(pTlat[:, slot, :], op[0:Q, P:2 * P])
                dve.tensor_copy(pT[:, slot, :], ptp[:]).then_inc(pT_done, 1)

            def outputs(h, opar, j):
                dve.wait_ge(o_ready, h + 1)
                dve.tensor_copy(ocur[:, opar, j, :], op[:, 0:P]).then_inc(o_done, 1)

            def run(pair, par):
                project, attend = parts(pair, par)
                for t in range(CHUNKS):
                    n, h, j = chunk_no(pair, par, t), head_no(pair, par, t), t * HPC
                    if attend:
                        row_max(h, 0)
                        normalise(h, 0)
                        if t:
                            outputs(h - 1, 1 - par, j - 1)
                        elif not (isinstance(h, int) and h == 0):
                            outputs(h - 1, par, KVH - 1)
                    if project:
                        key_sums(n, 0)
                        key_scale(n, 0)
                    if attend:
                        probs(h, 0)
                    if project:
                        key_sums(n, 1)
                        key_scale(n, 1)
                    if attend:
                        row_max(h + 1, 1)
                        normalise(h + 1, 1)
                        outputs(h, 1 - par, j)
                        probs(h + 1, 1)
                wait(dve, o_out[par], pair * 16) if project else None

            if with_mask:
                dve.wait_ge(m_in, 16 * GRP)
            over_batches(dve, run)
            outputs(B * KVH - 1, 1, KVH - 1)

        @block.gpsimd
        def _(pool):
            def make_lo(n, slot):
                pool.wait_ge(ct_hi_done, n + 1)
                pool.tensor_tensor(ct_lo[:, slot], ct_raw[:, slot], ct_hi[:, slot].bitcast(F32),
                                   ALU.subtract).then_inc(ct_lo_done, 1)

            def key_factor(n, j):
                pool.wait_ge(kms_done, n * 2 + (j + 1))
                wait(pool, khat_done, n * 2 + (j - 1))
                pool.tensor_tensor(krr[:, j, :], kms[:, j, :], c.minus_half[:, 0:GRP], ALU.pow).then_inc(krr_done, 1)

            def run(pair, par):
                project, attend = parts(pair, par)
                if project and par == 0:
                    make_lo(chunk_no(pair, 0, 0), 0)
                for t in range(CHUNKS):
                    n = chunk_no(pair, par, t)
                    if project:
                        if not (t == CHUNKS - 1 and par == 1):
                            make_lo(n + 1, (t + 1) % 2)
                        key_factor(n, 0)
                        key_factor(n, 1)

            over_batches(pool, run)

        @block.tensor
        def _(pe):
            def project_group(out, slot, cols):
                for k in range(DC):
                    last = split_matmul(pe, out, ct_hi[:, slot, k, :], ct_lo[:, slot, k, :], w_hi[:, k, cols],
                                        w_lo[:, k, cols], k == 0, k == DC - 1)
                return last

            def project_k(n, j, slot):
                wait(pe, khat_done, n * 2 + (j - 1))
                project_group(kp[j][:], slot, slice(j * COLS, (j + 1) * COLS)).then_inc(k_ready, 1)

            def project_v(n, j, slot):
                wait(pe, v_done, n * 2 + j)
                cols = slice(KVH * HD + j * COLS, KVH * HD + (j + 1) * COLS)
                project_group(vp[:], slot, cols).then_inc(v_ready, 1)

            def turn_keys(n, j):
                pe.wait_ge(khat_done, n * 2 + (j + 1))
                wait(pe, kT_done, n * 2 + j)
                for g in range(GRP):
                    last = pe.transpose(ktp[:, g * P:(g + 1) * P], khat[:, j, g * P:(g + 1) * P], c.ident[:])
                last.then_inc(ktp_ready, 1)

            def scores(h, j, par):
                wait(pe, sm_done if with_mask else exp_done, h)
                last = pe.matmul(scp[:, 0:KEYS], qcur[:, par, j, :], kT[:, par, j, :], start=True, stop=True)
                if with_latents:
                    last = pe.matmul(scp[:, KEYS:NK], qcur[:, par, j, :], klat[:, par, j, :], start=True, stop=True)
                last.then_inc(s_ready, 1)

            def turn_probs(h, slot):
                pe.wait_ge(pn_done, h + 1)
                wait(pe, pT_done, h)
                if with_latents:
                    wait(pe, o_done, h)
                    pe.transpose(op[0:Q, P:2 * P], pr[:, slot, KEYS:NK], c.ident[:])
                for k in range(CHUNKS):
                    last = pe.transpose(ptp[:, k * P:(k + 1) * P], pr[:, slot, k * P:(k + 1) * P], c.ident[:])
                last.then_inc(ptp_ready, 1)

            def weigh(h, slot, j, par):
                pe.wait_ge(pT_done, h + 1)
                wait(pe, o_done, h)
                for k in range(CHUNKS):
                    last = pe.matmul(op[:, 0:P], vv[:, par, k, j * HD:(j + 1) * HD], pT[:, slot, k * P:(k + 1) * P],
                                     start=k == 0, stop=k == CHUNKS - 1 and not with_latents)
                if with_latents:
                    last = pe.matmul(op[:, 0:P], vlat[:, par, j * HD:(j + 1) * HD], pTlat[:, slot, :],
                                     start=False, stop=True)
                last.then_inc(o_ready, 1)

            def run(pair, par):
                project, attend = parts(pair, par)
                opar = 1 - par
                if attend:
                    pe.wait_ge(q_in[opar], (pair + par) * (16 * Q_LOADS))
                    pe.wait_ge(kT_done, chunk_no(pair, par, 0) * 2)
                    pe.wait_ge(v_done, chunk_no(pair, par, 0) * 2)
                for t in range(CHUNKS):
                    n, h, j, slot = chunk_no(pair, par, t), head_no(pair, par, t), t * HPC, t % 2
                    if attend:
                        scores(h, j, opar)
                    if project:
                        pe.wait_ge(ct_lo_done, n + 1)
                        project_k(n, 0, slot)
                    if attend and t:
                        weigh(h - 1, 1, j - 1, opar)
                    elif attend and not (isinstance(h, int) and h == 0):
                        weigh(h - 1, 1, KVH - 1, par)
                    if project:
                        project_k(n, 1, slot)
                    if attend:
                        turn_probs(h, 0)
                    if project:
                        turn_keys(n, 0)
                    if attend:
                        scores(h + 1, j + 1, opar)
                    if project:
                        project_v(n, 0, slot)
                    if attend:
                        weigh(h, 0, j, opar)
                    if project:
                        project_v(n, 1, slot)
                        turn_keys(n, 1)
                    if attend:
                        turn_probs(h + 1, 1)

            over_batches(pe, run)
            weigh(B * KVH - 1, 1, KVH - 1, 1)


def stage_accumulate(c, tag, w_dram, rows, a_hi=None, a_lo=None, o_dram=None):
    nc = c.nc
    groups = (len(rows) + DC - 1) // DC
    with ExitStack() as st:
        sb, ps, sem = tiles(st, nc)
        raw = sb(f"{tag}_raw", [P, 2, DC, D])
        wh = sb(f"{tag}_wh", [P, 2, DC, D], F32R)
        wl = sb(f"{tag}_wl", [P, 2, DC, D], F32R)
        w_in = [sem(f"{tag}_w_in{i}") for i in range(2)]
        hi_done, lo_done, used, summed = (sem(f"{tag}_{n}") for n in ("hi_done", "lo_done", "used", "summed"))
        out = [ps(f"{tag}_out{t}", [P, D]) for t in range(TT)]
        if o_dram is not None:
            oraw = sb(f"{tag}_oraw", [P, 2, B, GRP * Q])
            oh = sb(f"{tag}_oh", [P, 2, GRP, TOK], F32R)
            ol = sb(f"{tag}_ol", [P, 2, GRP, TOK], F32R)
            oh_done = sem(f"{tag}_oh_done")
            ol_done = sem(f"{tag}_ol_done")
            o_in = [sem(f"{tag}_o_in{i}") for i in range(2)]
        block = st.enter_context(nc.Block())

        def full(g):
            part = rows[g * DC:(g + 1) * DC]
            whole = [k for k in range(len(part)) if part[k] == part[0]]
            pieces = [(part[0], 0, len(whole))]
            if len(whole) < len(part):
                pieces.append((part[-1], len(whole), len(part)))
            return pieces

        @block.sync
        def _(sp):
            for g in range(groups):
                if g >= 2:
                    sp.wait_ge(lo_done, g - 1)
                for n, a, b in full(g):
                    sp.dma_start(raw[0:n, g % 2, a:b, :], w_dram[g][0:n, a:b, :]).then_inc(w_in[g % 2], 16)
                if o_dram is not None:
                    if g >= 2:
                        sp.wait_ge(ol_done, g - 1)
                    sp.dma_start(oraw[:, g % 2], o_dram[:, :, g, :].rearrange("b p n -> p b n")).then_inc(o_in[g % 2], 16)

        counts = [0, 0]
        need = []
        for g in range(groups):
            counts[g % 2] += 16 * len(full(g))
            need.append(counts[g % 2])

        @block.scalar
        def _(act):
            for g in range(groups):
                act.wait_ge(w_in[g % 2], need[g])
                if g >= 2:
                    act.wait_ge(used, g - 1)
                for n, a, b in full(g):
                    last = act.activation(wh[0:n, g % 2, a:b, :], raw[0:n, g % 2, a:b, :], ACT.Copy)
                last.then_inc(hi_done, 1)
                if o_dram is not None:
                    act.wait_ge(o_in[g % 2], 16 * (g // 2 + 1))
                    act.activation(oh[:, g % 2].rearrange("p g (b n) -> p b g n", b=B),
                                   oraw[:, g % 2].rearrange("p b (g n) -> p b g n", g=GRP), ACT.Copy).then_inc(oh_done, 1)

        @block.vector
        def _(dve):
            for g in range(groups):
                dve.wait_ge(hi_done, g + 1)
                for n, a, b in full(g):
                    last = dve.tensor_tensor(wl[0:n, g % 2, a:b, :], raw[0:n, g % 2, a:b, :],
                                             wh[0:n, g % 2, a:b, :].bitcast(F32), ALU.subtract)
                last.then_inc(lo_done, 1)
            for t in range(TT):
                dve.wait_ge(used, groups)
                dve.tensor_tensor(c.x[:, t, :], c.x[:, t, :], out[t][:], ALU.add).then_inc(summed, 1)
            dve.wait_ge(summed, TT)

        @block.gpsimd
        def _(pool):
            if o_dram is not None:
                for g in range(groups):
                    pool.wait_ge(oh_done, g + 1)
                    pool.tensor_tensor(ol[:, g % 2].rearrange("p g (b n) -> p b g n", b=B),
                                       oraw[:, g % 2].rearrange("p b (g n) -> p b g n", g=GRP),
                                       oh[:, g % 2].bitcast(F32).rearrange("p g (b n) -> p b g n", b=B),
                                       ALU.subtract).then_inc(ol_done, 1)

        @block.tensor
        def _(pe):
            for g in range(groups):
                pe.wait_ge(lo_done, g + 1)
                if o_dram is not None:
                    pe.wait_ge(ol_done, g + 1)
                part = rows[g * DC:(g + 1) * DC]
                for k, n in enumerate(part):
                    for t in range(TT):
                        toks = slice(t * P, (t + 1) * P)
                        if o_dram is not None:
                            hi, lo = oh[:, g % 2, k, toks], ol[:, g % 2, k, toks]
                        else:
                            hi, lo = a_hi[0:n, g * DC + k, toks], a_lo[0:n, g * DC + k, toks]
                        last = split_matmul(pe, out[t][:], hi, lo, wh[0:n, g % 2, k, :], wl[0:n, g % 2, k, :],
                                            g == k == 0, g == groups - 1 and k == len(part) - 1)
                last.then_inc(used, 1)


def stage_ffn(c, tag, wg_dram, wu_dram, width, xT_hi, xT_lo, hT_hi, hT_lo):
    nc = c.nc
    chunks = [min(P, width - P * f) for f in range((width + P - 1) // P)]
    n = len(chunks)
    per = COLS // P
    loads = 2 * ((n + per - 1) // per)
    with ExitStack() as st:
        sb, ps, sem = tiles(st, nc)
        raw = sb(f"{tag}_raw", [P, 2, DC, COLS])
        wh = sb(f"{tag}_wh", [P, 4, DC, COLS], F32R)
        wl = sb(f"{tag}_wl", [P, 4, DC, COLS], F32R)
        e = sb(f"{tag}_e", [P, 2, TOK])
        s = sb(f"{tag}_s", [P, 2, TOK])
        r = sb(f"{tag}_r", [P, 2, TOK])
        g = sb(f"{tag}_g", [P, 2, TOK])
        h = sb(f"{tag}_h", [P, 2, TOK])
        gu = [ps(f"{tag}_gu{i}", [P, 2 * TOK]) for i in range(2)]
        w_in = [sem(f"{tag}_w_in{i}") for i in range(2)]
        hi_done, lo_done, gu_ready, e_done, s_done, r_done, g_done, h_done, hT_hi_done, hT_lo_done = (
            sem(f"{tag}_{x}") for x in ("hi_done", "lo_done", "gu_ready", "e_done", "s_done", "r_done", "g_done",
                                        "h_done", "hT_hi_done", "hT_lo_done"))
        block = st.enter_context(nc.Block())

        @block.sync
        def _(sp):
            for q in range(loads):
                if q >= 2:
                    sp.wait_ge(lo_done, q - 1)
                sp.dma_start(raw[:, q % 2], (wu_dram if q % 2 else wg_dram)[q // 2]).then_inc(w_in[q % 2], 16)

        @block.scalar
        def _(act):
            def make_hi(q):
                act.wait_ge(w_in[q % 2], 16 * (q // 2 + 1))
                if q >= 4:
                    act.wait_ge(gu_ready, per * (q // 2 - 1))
                act.activation(wh[:, q % 4], raw[:, q % 2], ACT.Copy).then_inc(hi_done, 1)

            for q in range(4):
                make_hi(q)
            for f in range(n + 1):
                if f < n:
                    m = chunks[f]
                    act.wait_ge(gu_ready, f + 1)
                    if f >= 2:
                        act.wait_ge(s_done, f - 1)
                    act.activation(e[0:m, f % 2], gu[f % 2][0:m, 0:TOK], ACT.Exp, scale=-1.0).then_inc(e_done, 1)
                if f >= 1:
                    m = chunks[f - 1]
                    act.wait_ge(h_done, f)
                    act.activation(hT_hi[0:m, f - 1], h[0:m, (f - 1) % 2], ACT.Copy).then_inc(hT_hi_done, 1)
                if f == per - 1:
                    for q in range(4, loads):
                        make_hi(q)

        @block.vector
        def _(dve):
            def make_lo(q):
                dve.wait_ge(hi_done, q + 1)
                dve.tensor_tensor(wl[:, q % 4], raw[:, q % 2], wh[:, q % 4].bitcast(F32),
                                  ALU.subtract).then_inc(lo_done, 1)

            for q in range(4):
                make_lo(q)
            for f in range(n):
                m, b = chunks[f], f % 2
                dve.wait_ge(s_done, f + 1)
                dve.reciprocal(r[0:m, b], s[0:m, b]).then_inc(r_done, 1)
                dve.wait_ge(r_done, f + 1)
                dve.tensor_tensor(g[0:m, b], gu[b][0:m, 0:TOK], r[0:m, b], ALU.mult).then_inc(g_done, 1)
                dve.wait_ge(g_done, f + 1)
                if f >= 2:
                    dve.wait_ge(hT_lo_done, f - 1)
                dve.tensor_tensor(h[0:m, b], gu[b][0:m, TOK:], g[0:m, b], ALU.mult).then_inc(h_done, 1)
                if f == per - 1:
                    for q in range(4, loads):
                        make_lo(q)

        @block.gpsimd
        def _(pool):
            for f in range(n + 1):
                if f < n:
                    m = chunks[f]
                    pool.wait_ge(e_done, f + 1)
                    if f >= 2:
                        pool.wait_ge(r_done, f - 1)
                    pool.tensor_scalar(s[0:m, f % 2], e[0:m, f % 2], 1.0, None, ALU.add).then_inc(s_done, 1)
                if f >= 1:
                    m = chunks[f - 1]
                    pool.wait_ge(hT_hi_done, f)
                    pool.tensor_tensor(hT_lo[0:m, f - 1], h[0:m, (f - 1) % 2], hT_hi[0:m, f - 1].bitcast(F32),
                                       ALU.subtract).then_inc(hT_lo_done, 1)

        @block.tensor
        def _(pe):
            for f in range(n):
                m, b = chunks[f], f % 2
                pe.wait_ge(lo_done, 2 * (f // per) + 2)
                if f >= 2:
                    pe.wait_ge(h_done, f - 1)
                cols = slice(f % per * P, f % per * P + m)
                for u in range(2):
                    q = (2 * (f // per) + u) % 4
                    for k in range(DC):
                        last = split_matmul(pe, gu[b][0:m, u * TOK:(u + 1) * TOK], wh[:, q, k, cols],
                                            wl[:, q, k, cols], xT_hi[:, k, :], xT_lo[:, k, :], k == 0, k == DC - 1)
                last.then_inc(gu_ready, 1)


NH, NKV, SHD = 32, 8, 16
SREP = NH // NKV


def stage_self_attention(c, wq_dram, wkv_dram, xT_hi, xT_lo, aT_hi, aT_lo):
    nc = c.nc
    HQ = NKV // 2
    NHK = NH * Q
    with ExitStack() as st:
        sb, ps, sem = tiles(st, nc)
        raw = sb("sa_raw", [P, DC, COLS + 2 * NKV * SHD])
        wh = sb("sa_wh", [P, DC, COLS + 2 * NKV * SHD], F32R)
        wl = sb("sa_wl", [P, DC, COLS + 2 * NKV * SHD], F32R)
        qT = sb("sa_qT", [P, SREP, TOK])
        diag8 = sb("sa_diag8", [P, NKV])
        diag4 = sb("sa_diag4", [P, HQ])
        causal = sb("sa_causal", [P, Q])
        kdiag = sb("sa_kdiag", [P, B, NKV, Q])
        vrep = sb("sa_vrep", [P, B, HQ, Q])
        vdiag = sb("sa_vdiag", [P, B, 2, HQ * SHD])
        sm = sb("sa_sm", [P, TT, NHK])
        ex = sb("sa_ex", [P, TT, NHK])
        mx = sb("sa_mx", [P, TT, NH])
        den = sb("sa_den", [P, TT, NH])
        rden = sb("sa_rden", [P, TT, NH])
        pT = sb("sa_pT", [P, TT, NHK])
        o = sb("sa_o", [P, TT, D])
        two = ps("sa_two", [P, 2 * COLS])
        kv = ps("sa_kv", [P, COLS])
        sc = [ps(f"sa_sc{t}", [P, NHK]) for t in range(TT)]
        (w_in, hi_done, lo_done, masks, masks0, q_ready, kv_ready, qT_done, kdiag_done, vrep_done, vt_ready, vdiag_done,
         s_ready, sm_done, mx_done, sub_done, ex_done, den_done, rden_done, pn_done, pt_ready, pT_done, o_ready, o_done,
         at_ready, at_hi_done, at_lo_done) = (sem(f"sa_{n}") for n in (
             "w_in", "hi_done", "lo_done", "masks", "masks0", "q_ready", "kv_ready", "qT_done", "kdiag_done",
             "vrep_done", "vt_ready", "vdiag_done", "s_ready", "sm_done", "mx_done", "sub_done", "ex_done",
             "den_done", "rden_done", "pn_done", "pt_ready", "pT_done", "o_ready", "o_done", "at_ready",
             "at_hi_done", "at_lo_done"))
        block = st.enter_context(nc.Block())

        @block.sync
        def _(sp):
            sp.dma_start(raw[:, :, 0:COLS], wq_dram).then_inc(w_in, 16)
            sp.dma_start(raw[:, :, COLS:], wkv_dram).then_inc(w_in, 16)

        @block.scalar
        def _(act):
            act.wait_ge(w_in, 32)
            act.activation(wh[:], raw[:], ACT.Copy).then_inc(hi_done, 1)
            act.wait_ge(q_ready, 1)
            act.activation(qT[:].rearrange("p g n -> p (g n)"), two[:], ACT.Copy,
                           scale=float(SHD) ** -0.5).then_inc(qT_done, 1)
            act.wait_ge(kdiag_done, 1)
            act.activation(vrep[:], kv[:, TOK:].rearrange("p (b n) -> p b n", b=B).unsqueeze(2)
                           .to_broadcast([P, B, HQ, Q]), ACT.Copy).then_inc(vrep_done, 1)
            for t in range(TT):
                act.wait_ge(sub_done, t + 1)
                act.activation(ex[:, t, :], sm[:, t, :], ACT.Exp).then_inc(ex_done, 1)
            for t in range(TT):
                act.wait_ge(pt_ready, t + 1)
                act.activation(pT[:, t, :], sc[t][:], ACT.Copy).then_inc(pT_done, 1)
            for t in range(TT):
                act.wait_ge(at_ready, t + 1)
                act.activation(aT_hi[:, :, t * P:(t + 1) * P], sc[t][:, 0:D].rearrange("p (g n) -> p g n", g=SREP),
                               ACT.Copy).then_inc(at_hi_done, 1)

        @block.gpsimd
        def _(pool):
            pool.memset(diag8[:], 1.0)
            pool.memset(diag4[:], 1.0)
            pool.memset(causal[:], 0.0).then_inc(masks0, 1)
            pool.wait_ge(masks0, 1)
            lowest = float(np.finfo(np.float32).min)
            for b in range(BT):
                rows = slice(b * Q, (b + 1) * Q)
                pool.affine_select(out=causal[rows, :], in_=causal[rows, :], compare_op=ALU.is_ge, fill=lowest,
                                   base=0, pattern=[[-1, Q]], channel_multiplier=1).then_inc(masks, 1)
                pool.wait_ge(masks, b + 1)
            at = BT
            for mask, width, cols in ((diag8, SHD, NKV), (diag4, Q, HQ)):
                for low in (True, False):
                    pool.affine_select(out=mask[:], in_=mask[:], compare_op=ALU.is_ge, fill=0.0,
                                       base=0 if low else width - 1, pattern=[[-width if low else width, cols]],
                                       channel_multiplier=1 if low else -1).then_inc(masks, 1)
                    at += 1
                    pool.wait_ge(masks, at)
            for t in range(TT):
                pool.wait_ge(rden_done, t + 1)
                p3 = ex[:, t, :].rearrange("p (h n) -> p h n", h=NH)
                pool.tensor_tensor(p3, p3, rden[:, t, :].unsqueeze(2).to_broadcast([P, NH, Q]),
                                   ALU.mult).then_inc(pn_done, 1)

        @block.vector
        def _(dve):
            dve.wait_ge(hi_done, 1)
            dve.tensor_tensor(wl[:], raw[:], wh[:].bitcast(F32), ALU.subtract).then_inc(lo_done, 1)
            dve.wait_ge(kv_ready, 1)
            dve.wait_ge(masks, BT + 4)
            dve.tensor_tensor(kdiag[:], kv[:, 0:TOK].rearrange("p (b n) -> p b n", b=B).unsqueeze(2)
                              .to_broadcast([P, B, NKV, Q]),
                              diag8[:].unsqueeze(1).unsqueeze(3).to_broadcast([P, B, NKV, Q]),
                              ALU.mult).then_inc(kdiag_done, 1)
            dve.wait_ge(vt_ready, 1)
            dve.tensor_tensor(vdiag[:].rearrange("p b u (j d) -> p (b u) j d", d=SHD),
                              two[:].rearrange("p (a j d) -> p a j d", j=HQ, d=SHD),
                              diag4[:].unsqueeze(1).unsqueeze(3).to_broadcast([P, 2 * B, HQ, SHD]),
                              ALU.mult).then_inc(vdiag_done, 1)
            for t in range(TT):
                s3 = sm[:, t, :].rearrange("p (h n) -> p h n", h=NH)
                dve.wait_ge(s_ready, t + 1)
                dve.tensor_tensor(s3, sc[t][:].rearrange("p (h n) -> p h n", h=NH),
                                  causal[:].unsqueeze(1).to_broadcast([P, NH, Q]), ALU.add).then_inc(sm_done, 1)
                dve.wait_ge(sm_done, t + 1)
                dve.tensor_reduce(mx[:, t, :], s3, AX.X, ALU.max).then_inc(mx_done, 1)
                dve.wait_ge(mx_done, t + 1)
                dve.tensor_tensor(s3, s3, mx[:, t, :].unsqueeze(2).to_broadcast([P, NH, Q]),
                                  ALU.subtract).then_inc(sub_done, 1)
            for t in range(TT):
                dve.wait_ge(ex_done, t + 1)
                dve.tensor_reduce(den[:, t, :], ex[:, t, :].rearrange("p (h n) -> p h n", h=NH), AX.X,
                                  ALU.add).then_inc(den_done, 1)
                dve.wait_ge(den_done, t + 1)
                dve.reciprocal(rden[:, t, :], den[:, t, :]).then_inc(rden_done, 1)
            for t in range(TT):
                dve.wait_ge(o_ready, t + 1)
                dve.tensor_copy(o[:, t, :], two[:, t * D:(t + 1) * D]).then_inc(o_done, 1)
            for t in range(TT):
                dve.wait_ge(at_hi_done, t + 1)
                dve.tensor_tensor(aT_lo[:, :, t * P:(t + 1) * P], sc[t][:, 0:D].rearrange("p (g n) -> p g n", g=SREP),
                                  aT_hi[:, :, t * P:(t + 1) * P].bitcast(F32), ALU.subtract).then_inc(at_lo_done, 1)

        @block.tensor
        def _(pe):
            pe.wait_ge(lo_done, 1)

            def project(out, col):
                for k in range(DC):
                    cols = slice(col, col + P)
                    last = split_matmul(pe, out, wh[:, k, cols], wl[:, k, cols], xT_hi[:, k, :], xT_lo[:, k, :],
                                        k == 0, k == DC - 1)
                return last

            project(kv[:, 0:TOK], COLS)
            project(kv[:, TOK:], COLS + P).then_inc(kv_ready, 1)
            for g in range(SREP):
                last = project(two[:, g * TOK:(g + 1) * TOK], g * P)
            last.then_inc(q_ready, 1)
            pe.wait_ge(vrep_done, 1)
            pe.wait_ge(qT_done, 1)
            for b in range(B):
                last = pe.transpose(two[:, b * P:(b + 1) * P], vrep[:, b].rearrange("p r n -> p (r n)"), c.ident[:])
            last.then_inc(vt_ready, 1)
            pe.wait_ge(kdiag_done, 1)
            for t in range(TT):
                for b in range(BT):
                    for g in range(SREP):
                        last = pe.matmul(sc[t][b * Q:(b + 1) * Q, g * NKV * Q:(g + 1) * NKV * Q],
                                         qT[:, g, (t * BT + b) * Q:(t * BT + b + 1) * Q],
                                         kdiag[:, t * BT + b].rearrange("p j n -> p (j n)"), start=True, stop=True)
                last.then_inc(s_ready, 1)
            for t in range(TT):
                pe.wait_ge(pn_done, t + 1)
                for a in range(NHK // P):
                    last = pe.transpose(sc[t][:, a * P:(a + 1) * P], ex[:, t, a * P:(a + 1) * P], c.ident[:])
                last.then_inc(pt_ready, 1)
            pe.wait_ge(vdiag_done, 1)
            for t in range(TT):
                pe.wait_ge(pT_done, t + 1)
                for b in range(BT):
                    for a in range(NHK // P):
                        width = HQ * SHD
                        last = pe.matmul(two[b * Q:(b + 1) * Q, t * D + a * width:t * D + (a + 1) * width],
                                         pT[:, t, a * P + b * Q:a * P + (b + 1) * Q], vdiag[:, t * BT + b, a % 2, :],
                                         start=True, stop=True)
                last.then_inc(o_ready, 1)
            for t in range(TT):
                pe.wait_ge(o_done, t + 1)
                for g in range(SREP):
                    last = pe.transpose(sc[t][:, g * P:(g + 1) * P], o[:, t, g * P:(g + 1) * P], c.ident[:])
                last.then_inc(at_ready, 1)


MD, MN, MK, MR = 1024, 16, 4, 32
MC = MD // P
MSP = MR + 2 * MN


def stage_scan_inputs(c, win_dram, conv_w, conv_b, xT_hi, xT_lo, u, sg):
    nc = c.nc
    groups = 2 * MD // COLS
    pairs = MC
    per = COLS // (2 * P)
    W = 2 * TOK
    with ExitStack() as st:
        sb, ps, sem = tiles(st, nc)
        raw = sb("mi_raw", [P, 2, DC, COLS])
        wh = sb("mi_wh", [P, 2, DC, COLS], F32R)
        wl = sb("mi_wl", [P, 2, DC, COLS], F32R)
        ux = sb("mi_ux", [P, 2, W])
        acc = sb("mi_acc", [P, 2, W])
        e = sb("mi_e", [P, 2, W])
        s = sb("mi_s", [P, 2, W])
        r = sb("mi_r", [P, 2, W])
        pj = [ps(f"mi_pj{i}", [P, W]) for i in range(4)]
        w_in = [sem(f"mi_w_in{i}") for i in range(2)]
        hi_done, lo_done, pj_ready, ux_done, conv_done, acc_done, e_done, s_done, r_done, out_done = (
            sem(f"mi_{x}") for x in ("hi_done", "lo_done", "pj_ready", "ux_done", "conv_done", "acc_done", "e_done",
                                     "s_done", "r_done", "out_done"))
        block = st.enter_context(nc.Block())

        @block.sync
        def _(sp):
            for g in range(groups):
                if g >= 2:
                    sp.wait_ge(lo_done, g - 1)
                sp.dma_start(raw[:, g % 2], win_dram[g]).then_inc(w_in[g % 2], 16)

        @block.scalar
        def _(act):
            def make_hi(g):
                act.wait_ge(w_in[g % 2], 16 * (g // 2 + 1))
                if g >= 2:
                    act.wait_ge(pj_ready, per * (g - 1))
                act.activation(wh[:, g % 2], raw[:, g % 2], ACT.Copy).then_inc(hi_done, 1)

            make_hi(0)
            make_hi(1)
            for m in range(pairs):
                if m % per == 0 and m and m // per + 1 < groups:
                    make_hi(m // per + 1)
                gate = m >= pairs // 2
                act.wait_ge(pj_ready, m + 1)
                if m >= 2:
                    act.wait_ge(s_done, m - 1)
                if gate:
                    act.activation(e[:, m % 2], pj[m % 4][:], ACT.Exp, scale=-1.0).then_inc(e_done, 1)
                else:
                    if m >= 2:
                        act.wait_ge(acc_done, m - 1)
                    act.activation(ux[:, m % 2], pj[m % 4][:], ACT.Copy).then_inc(ux_done, 1)
                    act.wait_ge(acc_done, m + 1)
                    act.activation(e[:, m % 2], acc[:, m % 2], ACT.Exp, scale=-1.0).then_inc(e_done, 1)

        @block.gpsimd
        def _(pool):
            for m in range(pairs):
                pool.wait_ge(e_done, m + 1)
                if m >= 2:
                    pool.wait_ge(r_done, m - 1)
                pool.tensor_scalar(s[:, m % 2], e[:, m % 2], 1.0, None, ALU.add).then_inc(s_done, 1)

        @block.vector
        def _(dve):
            def make_lo(g):
                dve.wait_ge(hi_done, g + 1)
                dve.tensor_tensor(wl[:, g % 2], raw[:, g % 2], wh[:, g % 2].bitcast(F32),
                                  ALU.subtract).then_inc(lo_done, 1)

            taps = 0
            make_lo(0)
            make_lo(1)
            for m in range(pairs):
                b = m % 2
                gate = m >= pairs // 2
                if m % per == 0 and m and m // per + 1 < groups:
                    make_lo(m // per + 1)
                if not gate:
                    dve.wait_ge(ux_done, m + 1)
                    if m >= 2:
                        dve.wait_ge(out_done, m - 1)
                    for tap in range(MK):
                        if tap:
                            dve.wait_ge(conv_done, taps)
                        for k in range(2):
                            ch = 2 * m + k
                            x3 = ux[:, b, k * TOK:(k + 1) * TOK].rearrange("p (b t) -> p b t", b=B)
                            a3 = acc[:, b, k * TOK:(k + 1) * TOK].rearrange("p (b t) -> p b t", b=B)
                            w = conv_w[:, ch, MK - 1 - tap:MK - tap]
                            if tap == 0:
                                dve.tensor_scalar(a3, x3, w, conv_b[:, ch:ch + 1], ALU.mult,
                                                  ALU.add).then_inc(conv_done, 1)
                            else:
                                last = dve.scalar_tensor_tensor(out=a3[:, :, tap:], in0=x3[:, :, :Q - tap], scalar=w,
                                                                in1=a3[:, :, tap:], op0=ALU.mult, op1=ALU.add)
                                last.then_inc(conv_done if tap < MK - 1 or k == 0 else acc_done, 1)
                            taps += not (tap == MK - 1 and k == 1)
                dve.wait_ge(s_done, m + 1)
                dve.reciprocal(r[:, b], s[:, b]).then_inc(r_done, 1)
                dve.wait_ge(r_done, m + 1)
                if gate:
                    out, src = sg[:, 2 * m - MC:2 * m - MC + 2, :], pj[m % 4][:]
                else:
                    dve.wait_ge(conv_done, taps)
                    out, src = u[:, 2 * m:2 * m + 2, :], acc[:, b]
                dve.tensor_tensor(out.rearrange("p c n -> p (c n)"), src, r[:, b], ALU.mult).then_inc(out_done, 1)

        @block.tensor
        def _(pe):
            for m in range(pairs):
                g = m // per
                pe.wait_ge(lo_done, g + 1)
                if m >= 4:
                    pe.wait_ge(out_done, m - 3)
                for half in range(2):
                    col = (m % per * 2 + half) * P
                    for k in range(DC):
                        last = split_matmul(pe, pj[m % 4][:, half * TOK:(half + 1) * TOK], wh[:, g % 2, k, col:col + P],
                                            wl[:, g % 2, k, col:col + P], xT_hi[:, k, :], xT_lo[:, k, :],
                                            k == 0, k == DC - 1)
                last.then_inc(pj_ready, 1)


def stage_scan_params(c, wx_dram, wdt_dram, dt_bias, lnw_dram, bc_dram, u, delta, du, bc):
    nc = c.nc
    PARTS = MSP // MN
    W = 2 * TOK
    with ExitStack() as st:
        sb, ps, sem = tiles(st, nc)
        wx = sb("mp_wx", [P, MC, MSP])
        wdt = sb("mp_wdt", [MR, MD])
        lnw = sb("mp_lnw", [P, MSP])
        sq = sb("mp_sq", [P, TT, MSP])
        ss = sb("mp_ss", [P, TT, PARTS])
        s2 = sb("mp_s2", [P, TT])
        ms = sb("mp_ms", [P, TT, PARTS])
        rr = sb("mp_rr", [P, TT, PARTS])
        n1 = sb("mp_n1", [P, TT, MSP])
        n2 = sb("mp_n2", [P, TT, MSP])
        dtT = sb("mp_dtT", [MR, TOK])
        bcT = sb("mp_bcT", [2 * MN, TOK])
        xb = sb("mp_xb", [P, MC, TOK])
        ax = sb("mp_ax", [P, MC, TOK])
        e = sb("mp_e", [P, MC, TOK])
        par = ps("mp_par", [P, TT * MSP])
        turn = ps("mp_turn", [MR, 2 * TOK])
        dl = [ps(f"mp_dl{m}", [P, W]) for m in range(MC // 2)]
        (w_in, par_ready, sq_done, ss_done, s2_done, s3_done, ms_done, rr_done, n1_done, n2_done, turn_ready, dtT_done,
         bcT_done, bc_out, bc_in, dl_ready, xb_done, ax_done, e_done, l_done, relu_done, d_done, du_done) = (
             sem(f"mp_{x}") for x in (
                 "w_in", "par_ready", "sq_done", "ss_done", "s2_done", "s3_done", "ms_done", "rr_done", "n1_done",
                 "n2_done", "turn_ready", "dtT_done", "bcT_done", "bc_out", "bc_in", "dl_ready", "xb_done", "ax_done",
                 "e_done", "l_done", "relu_done", "d_done", "du_done"))
        block = st.enter_context(nc.Block())

        @block.sync
        def _(sp):
            sp.dma_start(wx[:], wx_dram).then_inc(w_in, 16)
            sp.dma_start(wdt[:], wdt_dram).then_inc(w_in, 16)
            sp.dma_start(lnw[:], lnw_dram.unsqueeze(0).to_broadcast([P, MSP])).then_inc(w_in, 16)
            sp.wait_ge(bcT_done, 1)
            sp.dma_start(bc_dram, bcT[:]).then_inc(bc_out, 16)
            sp.wait_ge(bc_out, 16)
            sp.dma_start(bc[:], bc_dram.unsqueeze(0).to_broadcast([P, 2 * MN, TOK])).then_inc(bc_in, 16)
            sp.wait_ge(bc_in, 16)

        @block.tensor
        def _(pe):
            pe.wait_ge(w_in, 48)
            for t in range(TT):
                for k in range(MC):
                    last = pe.matmul(par[:, t * MSP:(t + 1) * MSP], u[:, k, t * P:(t + 1) * P], wx[:, k, :],
                                     start=k == 0, stop=k == MC - 1)
            last.then_inc(par_ready, 1)
            pe.wait_ge(n2_done, 1)
            for t in range(TT):
                pe.transpose(turn[:, t * P:(t + 1) * P], n2[:, t, 0:MR], c.ident[:])
                last = pe.transpose(turn[:, TOK + t * P:TOK + (t + 1) * P], n2[:, t, MR:], c.ident[:])
            last.then_inc(turn_ready, 1)
            pe.wait_ge(dtT_done, 1)
            for ch in range(MC):
                last = pe.matmul(dl[ch // 2][:, ch % 2 * TOK:(ch % 2 + 1) * TOK], wdt[:, ch * P:(ch + 1) * P], dtT[:],
                                 start=True, stop=True)
                if ch % 2:
                    last.then_inc(dl_ready, 1)

        @block.scalar
        def _(act):
            act.wait_ge(par_ready, 1)
            act.activation(sq[:].rearrange("p t n -> p (t n)"), par[:], ACT.Square).then_inc(sq_done, 1)
            act.wait_ge(turn_ready, 1)
            act.activation(dtT[:], turn[:, 0:TOK], ACT.Copy).then_inc(dtT_done, 1)
            act.activation(bcT[:], turn[:, TOK:], ACT.Copy).then_inc(bcT_done, 1)
            for ch in range(MC):
                act.wait_ge(xb_done, ch + 1)
                act.activation(ax[:, ch, :], xb[:, ch, :], ACT.Abs).then_inc(ax_done, 1)
            act.wait_ge(ax_done, MC)
            act.activation(e[:], ax[:], ACT.Exp, scale=-1.0).then_inc(e_done, 1)
            act.wait_ge(e_done, 1)
            act.activation(ax[:], e[:], ACT.Ln, bias=1.0).then_inc(l_done, 1)

        @block.gpsimd
        def _(pool):
            pool.wait_ge(s3_done, 1)
            pool.tensor_scalar(ms[:], ss[:], 1.0 / MN, 1e-6, ALU.mult, ALU.add).then_inc(ms_done, 1)
            pool.wait_ge(ms_done, 1)
            pool.tensor_tensor(rr[:].rearrange("p t n -> p (t n)"), ms[:].rearrange("p t n -> p (t n)"),
                               c.minus_half[:, 0:TT * PARTS], ALU.pow).then_inc(rr_done, 1)

        @block.vector
        def _(dve):
            dve.wait_ge(sq_done, 1)
            dve.tensor_reduce(ss[:].rearrange("p t n -> p (t n)"), sq[:].rearrange("p t (n k) -> p (t n) k", k=MN), AX.X,
                              ALU.add).then_inc(ss_done, 1)
            dve.wait_ge(ss_done, 1)
            dve.tensor_tensor(s2[:], ss[:, :, 0], ss[:, :, 1], ALU.add).then_inc(s2_done, 1)
            dve.wait_ge(s2_done, 1)
            dve.tensor_scalar(ss[:, :, 0:2], s2[:].unsqueeze(2).to_broadcast([P, TT, 2]), float(MN) / MR, None,
                              ALU.mult).then_inc(s3_done, 1)
            dve.wait_ge(rr_done, 1)
            dve.tensor_tensor(n1[:].rearrange("p t (n k) -> p (t n) k", k=MN),
                              par[:].rearrange("p (n k) -> p n k", k=MN),
                              rr[:].rearrange("p t n -> p (t n)").unsqueeze(2).to_broadcast([P, TT * PARTS, MN]),
                              ALU.mult).then_inc(n1_done, 1)
            dve.wait_ge(n1_done, 1)
            dve.wait_ge(w_in, 48)
            dve.tensor_tensor(n2[:], n1[:], lnw[:].unsqueeze(1).to_broadcast([P, TT, MSP]), ALU.mult).then_inc(n2_done, 1)
            for ch in range(MC):
                dve.wait_ge(dl_ready, ch // 2 + 1)
                dve.tensor_scalar(xb[:, ch, :], dl[ch // 2][:, ch % 2 * TOK:(ch % 2 + 1) * TOK], dt_bias[:, ch:ch + 1],
                                  None, ALU.add).then_inc(xb_done, 1)
            dve.wait_ge(xb_done, MC)
            dve.wait_ge(l_done, 1)
            dve.scalar_tensor_tensor(out=delta[:], in0=xb[:], scalar=0.0, in1=ax[:], op0=ALU.max,
                                     op1=ALU.add).then_inc(d_done, 1)
            dve.wait_ge(d_done, 1)
            dve.tensor_tensor(du[:], delta[:], u[:], ALU.mult).then_inc(du_done, 1)


def stage_scan(c, A, Dp, u, sg, delta, du, bc, yT_hi, yT_lo):
    nc = c.nc
    W = MN * TOK
    with ExitStack() as st:
        sb, ps, sem = tiles(st, nc)
        dA = sb("sc_dA", [P, 2, MN, TOK])
        x = sb("sc_x", [P, 2, MN, TOK])
        h = sb("sc_h", [P, 2, MN, TOK])
        y1 = sb("sc_y1", [P, 2, TOK])
        y2 = sb("sc_y2", [P, 2, TOK])
        yp = [ps(f"sc_yp{i}", [P, TOK]) for i in range(2)]
        dA_done, reset, x_done, h_done, hc_done, y_ready, y1_done, y2_done, hi_done, lo_done = (
            sem(f"sc_{n}") for n in ("dA_done", "reset", "x_done", "h_done", "hc_done", "y_ready", "y1_done",
                                     "y2_done", "hi_done", "lo_done"))
        block = st.enter_context(nc.Block())

        @block.scalar
        def _(act):
            def make_hi(k):
                act.wait_ge(y2_done, k + 1)
                act.activation(yT_hi[:, k, :], y2[:, k % 2], ACT.Copy).then_inc(hi_done, 1)

            for k in range(MC):
                if k >= 2:
                    act.wait_ge(h_done, k - 1)
                for n in range(MN):
                    last = act.activation(dA[:, k % 2, n, :], delta[:, k, :], ACT.Exp, scale=A[:, k, n:n + 1])
                last.then_inc(dA_done, 1)
                if k >= 2:
                    make_hi(k - 2)
            make_hi(MC - 2)
            make_hi(MC - 1)

        @block.gpsimd
        def _(pool):
            def make_lo(k):
                pool.wait_ge(hi_done, k + 1)
                pool.tensor_tensor(yT_lo[:, k, :], y2[:, k % 2], yT_hi[:, k, :].bitcast(F32),
                                   ALU.subtract).then_inc(lo_done, 1)

            for k in range(MC):
                if k >= 2:
                    pool.wait_ge(h_done, k - 1)
                pool.tensor_tensor(x[:, k % 2], du[:, k, :].unsqueeze(1).to_broadcast([P, MN, TOK]), bc[:, 0:MN, :],
                                   ALU.mult).then_inc(x_done, 1)
                if k >= 3:
                    make_lo(k - 3)
            for k in range(MC - 3, MC):
                make_lo(k)

        @block.vector
        def _(dve):
            def finish(k):
                dve.wait_ge(y_ready, k + 1)
                dve.scalar_tensor_tensor(out=y1[:, k % 2], in0=u[:, k, :], scalar=Dp[:, k:k + 1], in1=yp[k % 2][:],
                                         op0=ALU.mult, op1=ALU.add).then_inc(y1_done, 1)
                dve.wait_ge(y1_done, k + 1)
                if k >= 2:
                    dve.wait_ge(lo_done, k - 1)
                dve.tensor_tensor(y2[:, k % 2], y1[:, k % 2], sg[:, k, :], ALU.mult).then_inc(y2_done, 1)

            for k in range(MC):
                b = k % 2
                dve.wait_ge(dA_done, k + 1)
                dve.memset(dA[:, b].rearrange("p n (b t) -> p (n b) t", t=Q)[:, :, 0:1], 0.0).then_inc(reset, 1)
                dve.wait_ge(reset, k + 1)
                dve.wait_ge(x_done, k + 1)
                if k >= 2:
                    dve.wait_ge(y_ready, k - 1)
                dve.tensor_tensor_scan(h[:, b].rearrange("p n t -> p (n t)"), dA[:, b].rearrange("p n t -> p (n t)"),
                                       x[:, b].rearrange("p n t -> p (n t)"), 0.0, ALU.mult,
                                       ALU.add).then_inc(h_done, 1)
                dve.wait_ge(h_done, k + 1)
                dve.tensor_tensor(h[:, b], h[:, b], bc[:, MN:, :], ALU.mult).then_inc(hc_done, 1)
                if k:
                    finish(k - 1)
            finish(MC - 1)

        @block.tensor
        def _(pe):
            for k in range(MC):
                pe.wait_ge(hc_done, k + 1)
                if k >= 2:
                    pe.wait_ge(y1_done, k - 1)
                for n in range(MN):
                    last = pe.matmul(yp[k % 2][:], c.ident[:], h[:, k % 2, n, :], start=n == 0, stop=n == MN - 1)
                last.then_inc(y_ready, 1)


OC = 8
OIN, OHID = D // OC, 1366 // OC
OHALF = OHID // 2


def octonion_signs():
    table = np.zeros((OC, OC, OC), np.int64)
    table[0, 0, 0] = 1
    for i in range(1, OC):
        table[0, i, i] = table[i, 0, i] = 1
        table[i, i, 0] = -1
    for a, b, d in [(1, 2, 3), (1, 4, 5), (1, 7, 6), (2, 4, 6), (2, 5, 7), (3, 4, 7), (3, 6, 5)]:
        for x, y, z in ((a, b, d), (b, d, a), (d, a, b)):
            table[x, y, z], table[y, x, z] = 1, -1
    return [[int(table[i ^ k, i, k]) for k in range(OC)] for i in range(OC)]


def stage_ternary(c, w_drams, m_gate, m_up, m_down, scales):
    nc = c.nc
    sign = octonion_signs()
    names = ("gate", "up", "down")
    shapes = ([P, OC, OHID], [P, OC, OHID], [OHALF, OC, 2, OIN])
    COUNT = OC * OHID * OIN
    with ExitStack() as st:
        sb, ps, sem = tiles(st, nc)
        w = [sb(f"te_w_{n}", s) for n, s in zip(names, shapes)]
        low = [sb(f"te_low_{n}", s) for n, s in zip(names, shapes)]
        tern = [sb(f"te_tern_{n}", [s[0], 2, *s[1:]], F32R) for n, s in zip(names, shapes)]
        ones = sb("te_ones", [P, P])
        sums = sb("te_sums", [P, 3])
        half = sb("te_half", [P, 3])
        mhalf = sb("te_mhalf", [P, 3])
        total = ps("te_total", [P, 3])
        (w_in, ones_done, sum_done, total_ready, half_done, mhalf_done, low_done, pos_done, neg_done,
         spread) = (sem(f"te_{n}") for n in ("w_in", "ones_done", "sum_done", "total_ready", "half_done",
                                             "mhalf_done", "low_done", "pos_done", "neg_done", "spread"))
        block = st.enter_context(nc.Block())

        @block.sync
        def _(sp):
            for i in range(2):
                for half_rows in range(2):
                    sp.dma_start(w[i][half_rows * OIN:(half_rows + 1) * OIN], w_drams[i]).then_inc(w_in, 16)
            sp.dma_start(w[2][:], w_drams[2]).then_inc(w_in, 16)

        @block.tensor
        def _(pe):
            pe.wait_ge(ones_done, 1)
            pe.wait_ge(sum_done, 3)
            for i in range(3):
                n = (OIN, OIN, OHALF)[i]
                last = pe.matmul(total[:, i:i + 1], ones[0:n, :], sums[0:n, i:i + 1], start=True, stop=True)
            last.then_inc(total_ready, 1)

        def place(i, k):
            return i % 2 * OIN, i // 2

        def spread_in(copy, which, m, i):
            p, chunk = place(i, 0)
            for k in range(OC):
                neg = int(sign[i][k] < 0)
                last = copy(m[p:p + OIN, chunk, k, :], tern[which][p:p + OIN, neg, i ^ k, :])
            last.then_inc(spread, 1)

        def spread_down(copy, i):
            for k in range(OC):
                neg = int(sign[i][k] < 0)
                last = copy(m_down[:, :, i, k * OIN:(k + 1) * OIN], tern[2][:, neg, i ^ k, :, :])
            last.then_inc(spread, 1)

        @block.gpsimd
        def _(pool):
            pool.memset(ones[:], 1.0).then_inc(ones_done, 1)
            pool.wait_ge(neg_done, 2)
            for i in range(0, OC, 2):
                spread_in(pool.tensor_copy, 1, m_up, i)

        @block.vector
        def _(dve):
            dve.wait_ge(w_in, 16 * 5)
            for i in range(3):
                n = shapes[i][0]
                dve.tensor_reduce(sums[0:n, i:i + 1], w[i][:], AX.XYZ if i == 2 else AX.XY, ALU.add,
                                  apply_absolute_value=True).then_inc(sum_done, 1)
            dve.wait_ge(total_ready, 1)
            dve.tensor_scalar(scales[:], total[:], 1.0 / COUNT, None, ALU.mult)
            dve.tensor_scalar(half[:], total[:], 0.5 / COUNT, None, ALU.mult).then_inc(half_done, 1)
            dve.tensor_scalar(mhalf[:], total[:], -0.5 / COUNT, None, ALU.mult).then_inc(mhalf_done, 1)
            dve.wait_ge(half_done, 1)
            dve.wait_ge(mhalf_done, 1)
            for i in range(3):
                n = shapes[i][0]
                flat = "p a b -> p (a b)" if i < 2 else "p a b c -> p (a b c)"
                wf, lf = w[i][:].rearrange(flat), low[i][:].rearrange(flat)
                dve.tensor_scalar(lf, wf, mhalf[0:n, i:i + 1], None, ALU.is_lt).then_inc(low_done, 1)
                dve.wait_ge(low_done, i + 1)
                dve.scalar_tensor_tensor(out=tern[i][:, 0].rearrange(flat), in0=wf, scalar=half[0:n, i:i + 1], in1=lf,
                                         op0=ALU.is_gt, op1=ALU.subtract).then_inc(pos_done, 1)
            dve.wait_ge(neg_done, 1)
            for i in range(0, OC, 2):
                spread_in(dve.tensor_copy, 0, m_gate, i)
            dve.wait_ge(neg_done, 3)
            for i in range(0, OC, 2):
                spread_down(dve.tensor_copy, i)

        @block.scalar
        def _(act):
            def copy(out, in_):
                return act.activation(out, in_.bitcast(F32), ACT.Copy)

            for i in range(3):
                act.wait_ge(pos_done, i + 1)
                act.activation(tern[i][:, 1], tern[i][:, 0].bitcast(F32), ACT.Copy, scale=-1.0).then_inc(neg_done, 1)
            act.wait_ge(neg_done, 3)
            for i in range(1, OC, 2):
                spread_in(copy, 0, m_gate, i)
            for i in range(1, OC, 2):
                spread_in(copy, 1, m_up, i)
            for i in range(1, OC, 2):
                spread_down(copy, i)


def stage_octonion(c, m_gate, m_up, m_down, scales, xT_hi, xT_lo):
    nc = c.nc
    n = 2 * OC
    with ExitStack() as st:
        sb, ps, sem = tiles(st, nc)
        msg = sb("oc_msg", [P, 1])
        e = sb("oc_e", [OHALF, 2, TOK])
        s = sb("oc_s", [OHALF, 2, TOK])
        r = sb("oc_r", [OHALF, 2, TOK])
        g = sb("oc_g", [OHALF, 2, TOK])
        h = sb("oc_h", [OHALF, 2, TOK])
        hT_hi = sb("oc_hT_hi", [OHALF, n, TOK], F32R)
        hT_lo = sb("oc_hT_lo", [OHALF, n, TOK], F32R)
        gu = [ps(f"oc_gu{i}", [OHALF, 2 * TOK]) for i in range(2)]
        out = [ps(f"oc_out{t}", [P, D]) for t in range(TT)]
        msg_done, gu_ready, e_done, s_done, r_done, g_done, h_done, hi_done, lo_done, out_ready, sum_done = (
            sem(f"oc_{x}") for x in ("msg_done", "gu_ready", "e_done", "s_done", "r_done", "g_done", "h_done",
                                     "hi_done", "lo_done", "out_ready", "sum_done"))
        block = st.enter_context(nc.Block())

        @block.tensor
        def _(pe):
            for f in range(n):
                comp, hh = f // 2, f % 2
                if f >= 2:
                    pe.wait_ge(h_done, f - 1)
                for u, m in enumerate((m_gate, m_up)):
                    for k in range(DC):
                        w = m[:, k, comp, hh * OHALF:(hh + 1) * OHALF]
                        dst = gu[f % 2][:, u * TOK:(u + 1) * TOK]
                        pe.matmul(dst, w, xT_hi[:, k, :], start=k == 0, stop=False)
                        last = pe.matmul(dst, w, xT_lo[:, k, :], start=False, stop=k == DC - 1)
                last.then_inc(gu_ready, 1)
            for f in range(n):
                comp, hh = f // 2, f % 2
                pe.wait_ge(lo_done, f + 1)
                for t in range(TT):
                    toks = slice(t * P, (t + 1) * P)
                    w = m_down[:, hh, comp, :]
                    pe.matmul(out[t][:], hT_hi[:, f, toks], w, start=f == 0, stop=False)
                    last = pe.matmul(out[t][:], hT_lo[:, f, toks], w, start=False, stop=f == n - 1)
            last.then_inc(out_ready, 1)

        @block.scalar
        def _(act):
            act.wait_ge(msg_done, 1)
            for f in range(n + 1):
                if f < n:
                    act.wait_ge(gu_ready, f + 1)
                    if f >= 2:
                        act.wait_ge(s_done, f - 1)
                    act.activation(e[:, f % 2], gu[f % 2][:, 0:TOK], ACT.Exp, scale=msg[0:OHALF, :]).then_inc(e_done, 1)
                if f:
                    act.wait_ge(h_done, f)
                    act.activation(hT_hi[:, f - 1], h[:, (f - 1) % 2], ACT.Copy).then_inc(hi_done, 1)

        @block.gpsimd
        def _(pool):
            pool.tensor_scalar(msg[:], scales[:, 0:1], -1.0, None, ALU.mult).then_inc(msg_done, 1)
            for f in range(n + 1):
                if f < n:
                    pool.wait_ge(e_done, f + 1)
                    if f >= 2:
                        pool.wait_ge(r_done, f - 1)
                    pool.tensor_scalar(s[:, f % 2], e[:, f % 2], 1.0, None, ALU.add).then_inc(s_done, 1)
                if f:
                    pool.wait_ge(hi_done, f)
                    pool.tensor_tensor(hT_lo[:, f - 1], h[:, (f - 1) % 2], hT_hi[:, f - 1].bitcast(F32),
                                       ALU.subtract).then_inc(lo_done, 1)

        @block.vector
        def _(dve):
            for f in range(n):
                b = f % 2
                dve.wait_ge(s_done, f + 1)
                dve.reciprocal(r[:, b], s[:, b]).then_inc(r_done, 1)
                dve.wait_ge(r_done, f + 1)
                dve.scalar_tensor_tensor(out=g[:, b], in0=gu[b][:, 0:TOK], scalar=scales[0:OHALF, 0:1], in1=r[:, b],
                                         op0=ALU.mult, op1=ALU.mult).then_inc(g_done, 1)
                dve.wait_ge(g_done, f + 1)
                if f >= 2:
                    dve.wait_ge(lo_done, f - 1)
                dve.scalar_tensor_tensor(out=h[:, b], in0=gu[b][:, TOK:], scalar=scales[0:OHALF, 1:2], in1=g[:, b],
                                         op0=ALU.mult, op1=ALU.mult).then_inc(h_done, 1)
            dve.wait_ge(out_ready, 1)
            for t in range(TT):
                dve.scalar_tensor_tensor(out=c.x[:, t, :], in0=out[t][:], scalar=scales[:, 2:3], in1=c.x[:, t, :],
                                         op0=ALU.mult, op1=ALU.add).then_inc(sum_done, 1)
            dve.wait_ge(sum_done, TT)


def build(nc, t, out, stop=99):
    c = Ctx()
    c.nc = nc
    with ExitStack() as st:
        sb, ps, sem = tiles(st, nc)
        c.x = sb("x_res", [P, TT, D])
        c.ident = sb("ident", [P, P])
        c.minus_half = sb("minus_half", [P, 8])
        q_dram = nc.dram_tensor("q_scratch", (B, P, KVH, GRP * Q), F32).ap()
        o_dram = nc.dram_tensor("o_scratch", (B, P, KVH, GRP * Q), F32).ap()
        klat_dram = nc.dram_tensor("klat_scratch", (B, P, KVH, Q), F32).ap()
        vlat_dram = nc.dram_tensor("vlat_scratch", (B, Q, KVH * HD), F32).ap()
        stage_constants(c, t["x"])

        def cross(layer, eps, mask):
            tag = f"x{layer}"
            lat = layer == 1
            with ExitStack() as s2:
                sb, _, _ = tiles(s2, nc)
                w_hi = sb(f"{tag}_w_hi", [P, DC, KVCOLS], F32R)
                w_lo = sb(f"{tag}_w_lo", [P, DC, KVCOLS], F32R)
                with ExitStack() as s3:
                    sb, _, _ = tiles(s3, nc)
                    xT_hi = sb(f"{tag}_xT_hi", [P, DC, TOK], F32R)
                    xT_lo = sb(f"{tag}_xT_lo", [P, DC, TOK], F32R)
                    stage_layernorm(c, f"{tag}_ln", xT_hi, xT_lo)
                    stage_queries(c, f"{tag}_q", t[f"wq{layer}"], t[f"wkv{layer}"], (t[f"qn{layer}"], t[f"kn{layer}"]),
                                  eps, xT_hi, xT_lo, w_hi, w_lo, q_dram, klat_dram if lat else None,
                                  vlat_dram if lat else None)
                stage_context(c, f"{tag}_c", t["ctxT"], mask, eps, w_hi, w_lo, q_dram, klat_dram if lat else None,
                              vlat_dram if lat else None, o_dram)
            stage_accumulate(c, f"{tag}_o", t[f"wo{layer}"], [P] * (KVH * GRP), o_dram=o_dram)

        if stop in (1, 99):
            with own_semaphores(nc):
                cross(0, 1e-5, t["mask"])

        if stop in (2, 99):
            with own_semaphores(nc), ExitStack() as s2:
                sb, _, _ = tiles(s2, nc)
                aT_hi, aT_lo = sb("aT_hi", [P, SREP, TOK], F32R), sb("aT_lo", [P, SREP, TOK], F32R)
                with ExitStack() as s3:
                    sb, _, _ = tiles(s3, nc)
                    xT_hi, xT_lo = sb("sa_xT_hi", [P, DC, TOK], F32R), sb("sa_xT_lo", [P, DC, TOK], F32R)
                    stage_layernorm(c, "sa_ln", xT_hi, xT_lo)
                    stage_self_attention(c, t["sa_wq"], t["sa_wkv"], xT_hi, xT_lo, aT_hi, aT_lo)
                stage_accumulate(c, "sa_out", t["sa_wo"], [P] * SREP, aT_hi, aT_lo)

        if stop in (3, 99):
            with own_semaphores(nc), ExitStack() as s2:
                sb, _, _ = tiles(s2, nc)
                F = FFN
                nf = (F + P - 1) // P
                hT_hi, hT_lo = sb("ffn_hT_hi", [P, nf, TOK], F32R), sb("ffn_hT_lo", [P, nf, TOK], F32R)
                with ExitStack() as s3:
                    sb, _, _ = tiles(s3, nc)
                    xT_hi, xT_lo = sb("ffn_xT_hi", [P, DC, TOK], F32R), sb("ffn_xT_lo", [P, DC, TOK], F32R)
                    stage_layernorm(c, "ffn_ln", xT_hi, xT_lo)
                    stage_ffn(c, "ffn", t["ffn_wg"], t["ffn_wu"], F, xT_hi, xT_lo, hT_hi, hT_lo)
                stage_accumulate(c, "ffn_out", t["ffn_wd"], [min(P, F - P * f) for f in range(nf)], hT_hi, hT_lo)

        if stop in (4, 99):
            with own_semaphores(nc):
                cross(1, 1e-6, None)

        if stop in (5, 99):
            with own_semaphores(nc), ExitStack() as s2:
                sb, _, sem = tiles(s2, nc)
                u, sg = sb("m_u", [P, MC, TOK]), sb("m_sg", [P, MC, TOK])
                conv_w, conv_b, dt_bias = sb("m_conv_w", [P, MC, MK]), sb("m_conv_b", [P, MC]), sb("m_dt_bias", [P, MC])
                A, Dp = sb("m_A", [P, MC, MN]), sb("m_Dp", [P, MC])
                with ExitStack() as s3:
                    sb3, _, sem3 = tiles(s3, nc)
                    xT_hi, xT_lo = sb3("mi_xT_hi", [P, DC, TOK], F32R), sb3("mi_xT_lo", [P, DC, TOK], F32R)
                    per_channel = sem3("m_per_channel")
                    with nc.Block() as block:
                        @block.sync
                        def _(sp):
                            for dst, src in ((conv_w, "conv_w"), (conv_b, "conv_b"), (dt_bias, "dt_bias"), (A, "A"),
                                             (Dp, "Dp")):
                                sp.dma_start(dst[:], t[src]).then_inc(per_channel, 16)
                            sp.wait_ge(per_channel, 16 * 5)
                    stage_layernorm(c, "mi_ln", xT_hi, xT_lo)
                    stage_scan_inputs(c, t["win"], conv_w, conv_b, xT_hi, xT_lo, u, sg)
                yT_hi, yT_lo = sb("m_yT_hi", [P, MC, TOK], F32R), sb("m_yT_lo", [P, MC, TOK], F32R)
                with ExitStack() as s3:
                    sb3, _, _ = tiles(s3, nc)
                    delta, du = sb3("m_delta", [P, MC, TOK]), sb3("m_du", [P, MC, TOK])
                    bc = sb3("m_bc", [P, 2 * MN, TOK])
                    bc_dram = nc.dram_tensor("bc_scratch", (2 * MN, TOK), F32).ap()
                    stage_scan_params(c, t["wx"], t["wdt"], dt_bias, t["scan_lnw"], bc_dram, u, delta, du, bc)
                    stage_scan(c, A, Dp, u, sg, delta, du, bc, yT_hi, yT_lo)
                stage_accumulate(c, "m_out", t["wout"], [P] * MC, yT_hi, yT_lo)

        if stop in (6, 99):
            with own_semaphores(nc), ExitStack() as s2:
                sb, _, _ = tiles(s2, nc)
                m_gate, m_up = (sb(f"o_m_{n}", [P, OC // 2, OC, OHID], F32R) for n in ("gate", "up"))
                m_down = sb("o_m_down", [OHALF, 2, OC, D], F32R)
                scales = sb("o_scales", [P, 3])
                stage_ternary(c, (t["og"], t["ou"], t["od"]), m_gate, m_up, m_down, scales)
                xT_hi, xT_lo = sb("o_xT_hi", [P, DC, TOK], F32R), sb("o_xT_lo", [P, DC, TOK], F32R)
                stage_layernorm(c, "o_ln", xT_hi, xT_lo)
                stage_octonion(c, m_gate, m_up, m_down, scales, xT_hi, xT_lo)
        with ExitStack() as s2:
            _, _, sem = tiles(s2, nc)
            out_done = sem("out_done")
            block = s2.enter_context(nc.Block())

            @block.sync
            def _(sp):
                sp.dma_start(out.rearrange("(t p) d -> p t d", p=P), c.x[:]).then_inc(out_done, 16)
                sp.wait_ge(out_done, 16)


def lay_out(i):
    f = lambda a: np.ascontiguousarray(np.asarray(a))

    def groups(w, cols=COLS):
        k, n = w.shape
        return f(w.reshape(k // P, P, n // cols, cols).transpose(2, 1, 0, 3))

    def rows(w):
        n, d = w.shape
        g = -(-n // (DC * P))
        full = np.zeros((g * DC * P, d), w.dtype)
        full[:n] = w
        return f(full.reshape(g, DC, P, d).transpose(0, 2, 1, 3))

    a = {}
    a["x"] = f(i["x"]).reshape(TOK, D)
    ctx = np.asarray(i["ctx_4096"])
    a["ctxT"] = f(ctx.reshape(B * CHUNKS, P, DC, P).transpose(0, 3, 2, 1))
    a["mask"] = f(i["mask_1x1xSxS2_ff0"]).reshape(Q, KEYS)
    n = lambda k: np.asarray(i[k])
    a["wq0"], a["wq1"] = groups(n("L0_xattn_Wq").T), groups(n("L1_xattn_Wq"))
    a["wkv0"] = np.concatenate([groups(n("L0_xattn_Wk").T), groups(n("L0_xattn_Wv").T)])
    a["wkv1"] = np.concatenate([groups(n("L1_xattn_Wk")), groups(n("L1_xattn_Wv"))])
    a["wo0"], a["wo1"] = rows(n("L0_xattn_Wo").T), rows(n("L1_xattn_Wo"))
    for layer in (0, 1):
        a[f"qn{layer}"], a[f"kn{layer}"] = f(n(f"L{layer}_xattn_q_norm_w")), f(n(f"L{layer}_xattn_k_norm_w"))

    def by_group(w, axis):
        w = np.moveaxis(w, axis, 0)
        w = w.reshape(NKV, SREP, SHD, -1).transpose(1, 0, 2, 3).reshape(D, -1)
        return np.moveaxis(w, 0, axis)

    a["sa_wq"] = groups(by_group(n("L0_attn_wq"), 1))[0]
    a["sa_wkv"] = groups(np.concatenate([n("L0_attn_wk"), n("L0_attn_wv")], 1), 2 * NKV * SHD)[0]
    a["sa_wo"] = rows(by_group(n("L0_attn_wo"), 0))

    def padded(w):
        full = np.zeros((D, -(-w.shape[1] // COLS) * COLS), w.dtype)
        full[:, :w.shape[1]] = w
        return groups(full)

    a["ffn_wg"], a["ffn_wu"] = padded(n("L0_ffn_W_gate").T), padded(n("L0_ffn_W_up").T)
    a["ffn_wd"] = rows(n("L0_ffn_W_down").T)

    def channels(w):
        return f(np.moveaxis(w.reshape(MC, P, *w.shape[1:]), 0, 1))

    a["win"] = groups(n("L1_attn_W_in").T)
    a["conv_w"], a["conv_b"] = channels(n("L1_attn_conv_w")), channels(n("L1_attn_conv_b"))
    a["dt_bias"], a["A"], a["Dp"] = (channels(n(f"L1_attn_{k}")) for k in ("dt_bias", "A", "D_param"))
    a["wx"], a["wdt"] = channels(n("L1_attn_Wx").T), f(n("L1_attn_Wdt").T)
    a["scan_lnw"] = np.concatenate([n("L1_attn_dt_ln_w"), n("L1_attn_b_ln_w"), n("L1_attn_c_ln_w")])
    a["wout"] = rows(n("L1_attn_W_out").T)
    a["og"], a["ou"] = (f(n(f"L1_ffn_w_{k}").transpose(2, 0, 1)) for k in ("gate", "up"))
    a["od"] = f(n("L1_ffn_w_down").reshape(OC, OIN, 2, OHALF).transpose(3, 0, 2, 1))
    return a


def kernel(**inputs):
    import concourse.bacc as bacc
    from concourse.bass_utils import run_bass_kernel_spmd

    nc = bacc.Bacc("TRN2", target_bir_lowering=False, num_devices=1)
    arrays = lay_out(inputs)
    tensors = {k: nc.dram_tensor(k, a.shape, mybir.dt.from_np(a.dtype), kind="ExternalInput").ap()
               for k, a in arrays.items()}
    out = nc.dram_tensor("out", (TOK, D), F32, kind="ExternalOutput").ap()
    build(nc, tensors, out)
    got = run_bass_kernel_spmd(nc, [arrays], core_ids=[0]).results[0]["out"]
    return got.reshape(B, Q, D)
```

```python
from contextlib import ExitStack, contextmanager

import numpy as np
import concourse.bass as bass
from concourse import mybir

F32 = mybir.dt.float32
F32R = mybir.dt.float32r
ALU = mybir.AluOpType
ACT = mybir.ActivationFunctionType
AX = mybir.AxisListType

P = 128
B, Q, D = 8, 32, 512
KEYS = 512
TOK = B * Q
TT = TOK // P
BT = P // Q
DC = D // P
KVH, GRP, HD = 8, 4, 128
COLS = 512
KVCOLS = 2 * KVH * HD
FFN = 1376
CHUNKS = KEYS // P


class Ctx:
    pass


def tiles(stack, nc):
    def sb(name, shape, dt=F32):
        return stack.enter_context(nc.sbuf_tensor(name, shape, dt))

    def ps(name, shape):
        return stack.enter_context(nc.psum_tensor(name, shape, F32))

    def sem(name):
        return nc.alloc_semaphore(name)

    return sb, ps, sem


@contextmanager
def own_semaphores(nc):
    before = nc.snapshot_sems()
    yield
    nc.all_engine_barrier()
    nc.clear_and_free_semaphores(nc.allocated_since(before))
    nc.all_engine_barrier()


def split_matmul(pe, out, a_hi, a_lo, b_hi, b_lo, first, last):
    pe.matmul(out, a_hi, b_hi, start=first, stop=False)
    pe.matmul(out, a_hi, b_lo, start=False, stop=False)
    return pe.matmul(out, a_lo, b_hi, start=False, stop=last)


def stage_constants(c, x_dram):
    nc = c.nc
    with ExitStack() as st:
        sb, ps, sem = tiles(st, nc)
        x_in, ident0, ident1 = sem("x_in"), sem("ident0"), sem("ident1")
        block = st.enter_context(nc.Block())

        @block.sync
        def _(sp):
            sp.dma_start(c.x[:], x_dram.rearrange("(t p) d -> p t d", p=P)).then_inc(x_in, 16)
            sp.wait_ge(x_in, 16)

        @block.gpsimd
        def _(pool):
            pool.memset(c.ident[:], 0.0).then_inc(ident0, 1)
            pool.memset(c.minus_half[:], -0.5)
            pool.wait_ge(ident0, 1)
            pool.affine_select(out=c.ident[:], in_=c.ident[:], compare_op=ALU.not_equal, fill=1.0,
                               base=0, pattern=[[-1, P]], channel_multiplier=1).then_inc(ident1, 1)
            pool.wait_ge(ident1, 1)


class LayerNorm:

    def __init__(self, c, st, tag, xT_hi, xT_lo, banks=None):
        sb, ps, sem = tiles(st, c.nc)
        self.c, self.xT_hi, self.xT_lo = c, xT_hi, xT_lo
        self.stats = sb(f"{tag}_ln_stats", [P, TT, 6])
        self.mv = sb(f"{tag}_ln_mv", [P, TT, 2])
        self.var = sb(f"{tag}_ln_var", [P, TT])
        self.rstd = sb(f"{tag}_ln_rstd", [P, TT])
        self.xn = sb(f"{tag}_ln_xn", [P, TT, D])
        self.xT_ps = banks or [ps(f"{tag}_ln_xT_ps{t}", [P, DC * P]) for t in range(TT)]
        (self.stats_done, self.mv_done, self.var_done, self.rstd_done, self.xn_done, self.xT_ready, self.hi_done,
         self.done) = (sem(f"{tag}_ln_{n}") for n in ("stats_done", "mv_done", "var_done", "rstd_done", "xn_done",
                                                      "xT_ready", "hi_done", "done"))

    def vector(self, dve):
        c = self.c
        for t in range(TT):
            dve.bn_stats(self.stats[:, t, :], c.x[:, t, :]).then_inc(self.stats_done, 1)
        for t in range(TT):
            dve.wait_ge(self.stats_done, t + 1)
            dve.bn_aggr(self.mv[:, t, :], self.stats[:, t, :]).then_inc(self.mv_done, 1)
        dve.wait_ge(self.mv_done, TT)
        dve.tensor_scalar(self.var[:], self.mv[:, :, 1], 1e-5, None, ALU.add).then_inc(self.var_done, 1)
        for t in range(TT):
            dve.wait_ge(self.rstd_done, 1)
            dve.tensor_scalar(self.xn[:, t, :], c.x[:, t, :], self.mv[:, t, 0:1], self.rstd[:, t:t + 1],
                              ALU.subtract, ALU.mult).then_inc(self.xn_done, 1)
        for t in range(TT):
            dve.wait_ge(self.hi_done, t + 1)
            toks = slice(t * P, (t + 1) * P)
            dve.tensor_tensor(self.xT_lo[:, :, toks], self.xT_ps[t][:, 0:DC * P].rearrange("p (c n) -> p c n", c=DC),
                              self.xT_hi[:, :, toks].bitcast(F32), ALU.subtract).then_inc(self.done, 1)

    def gpsimd(self, pool):
        pool.wait_ge(self.var_done, 1)
        pool.tensor_tensor(self.rstd[:], self.var[:], self.c.minus_half[:, 0:TT], ALU.pow).then_inc(self.rstd_done, 1)

    def tensor(self, pe):
        for t in range(TT):
            pe.wait_ge(self.xn_done, t + 1)
            for k in range(DC):
                cols = slice(k * P, (k + 1) * P)
                last = pe.transpose(self.xT_ps[t][:, cols], self.xn[:, t, cols], self.c.ident[:])
            last.then_inc(self.xT_ready, 1)

    def scalar(self, act):
        for t in range(TT):
            act.wait_ge(self.xT_ready, t + 1)
            act.activation(self.xT_hi[:, :, t * P:(t + 1) * P], self.xT_ps[t][:, 0:DC * P].rearrange("p (c n) -> p c n", c=DC),
                           ACT.Copy).then_inc(self.hi_done, 1)


def stage_queries(c, tag, chunks, ctxT_dram, wq_dram, wkv_dram, norm_w_dram, eps, xT_hi, xT_lo, w_hi, w_lo,
                  q_dram, klat_dram, vlat_dram):
    nc = c.nc
    with_latents = klat_dram is not None
    q_groups = KVH
    kv_groups = KVCOLS // COLS
    order = [("q", 0)]
    for g in range(1, q_groups):
        order.append(("q", g))
        if g % 2 == 0 or g == q_groups - 1:
            order.append(("kv", g // 2 - 1 if g % 2 == 0 else kv_groups - 1))
    groups = len(order)
    assert groups == q_groups + kv_groups and order[-1][0] == "kv"
    place = {name: at for at, name in enumerate(order)}
    LAG = 2
    RAW, WQ, NP = 4, 3, 4
    ct_raw, ct_hi, ct_lo, ct_in, ct_hi_done, ct_lo_done = chunks
    items = [("q", g, t) for g in range(q_groups) for t in range(TT)]
    if with_latents:
        items += [("k", g, t) for g in range(kv_groups // 2) for t in range(TT)]
        items += [("v", g, t) for g in range(kv_groups // 2, kv_groups) for t in range(TT)]
    n_norm = sum(kind != "v" for kind, _, _ in items)

    with ExitStack() as st:
        sb, ps, sem = tiles(st, nc)
        raw = sb(f"{tag}_raw", [P, RAW, DC, COLS])
        wq_hi = sb(f"{tag}_wq_hi", [P, WQ, DC, COLS], F32R)
        wq_lo = sb(f"{tag}_wq_lo", [P, WQ, DC, COLS], F32R)
        sq = sb(f"{tag}_sq", [P, COLS])
        ss = sb(f"{tag}_ss", [P, 2, GRP])
        ms = sb(f"{tag}_ms", [P, 2, GRP])
        rr = sb(f"{tag}_rr", [P, 2, GRP])
        nrm = sb(f"{tag}_nrm", [P, 2, COLS])
        stg = sb(f"{tag}_stg", [P, 2, COLS])
        nw = sb(f"{tag}_nw", [P, 2])
        qkw = sb(f"{tag}_qkw", [P, 1])
        proj = [ps(f"{tag}_proj{i}", [P, COLS]) for i in range(NP)]
        turn = [ps(f"{tag}_turn{i}", [P, COLS]) for i in range(2)]
        raw_in = [sem(f"{tag}_raw_in{i}") for i in range(RAW)]
        nw_in, qkw_done = sem(f"{tag}_nw_in"), sem(f"{tag}_qkw_done")
        w_hi_done, w_lo_done = sem(f"{tag}_w_hi_done"), sem(f"{tag}_w_lo_done")
        proj_ready, sq_done, ss_done, ms_done, rr_done, nrm_done, turn_ready, stg_done = (
            sem(f"{tag}_{n}") for n in ("proj_ready", "sq_done", "ss_done", "ms_done", "rr_done", "nrm_done",
                                        "turn_ready", "stg_done"))
        stored = [sem(f"{tag}_stored{i}") for i in range(2)]
        norm = LayerNorm(c, st, tag, xT_hi, xT_lo)
        block = st.enter_context(nc.Block())

        def weights(kind, g):
            if kind == "q":
                return wq_hi[:, g % WQ], wq_lo[:, g % WQ]
            return w_hi[:, :, g * COLS:(g + 1) * COLS], w_lo[:, :, g * COLS:(g + 1) * COLS]

        def split_by(i):
            return min(groups, i + 1)

        assert all(split_by(TT * g - 1) > place["q", g] for g in range(1, q_groups))
        assert split_by(TT * q_groups - 1) == groups

        @block.sync
        def _(sp):
            for i, w in enumerate(norm_w_dram):
                sp.dma_start(nw[:, i:i + 1], w.rearrange("(p o) -> p o", o=1)).then_inc(nw_in, 16)
            def load(at):
                kind, g = order[at]
                if at >= RAW:
                    sp.wait_ge(w_lo_done, at - RAW + 1)
                src = wq_dram[g] if kind == "q" else wkv_dram[g]
                sp.dma_start(raw[:, at % RAW], src).then_inc(raw_in[at % RAW], 16)

            for at in range(RAW):
                load(at)
            loaded = RAW
            for n in range(2):
                sp.dma_start(ct_raw[:, n], ctxT_dram[n]).then_inc(ct_in[n], 16)
            for i, (kind, g, t) in enumerate(items):
                while loaded < min(groups, split_by(i) + RAW):
                    load(loaded)
                    loaded += 1
                sp.wait_ge(stg_done, i + 1)
                src = stg[:, i % 2, :]
                if kind == "v":
                    cols = slice((g - kv_groups // 2) * COLS, (g - kv_groups // 2 + 1) * COLS)
                    dst = vlat_dram.rearrange("b q n -> (b q) n")[t * P:(t + 1) * P, cols]
                elif kind == "q":
                    dst = q_dram[t * BT:(t + 1) * BT, :, g, :].rearrange("b p n -> p b n")
                    src = src.rearrange("p (b n) -> p b n", b=BT)
                else:
                    dst = klat_dram[t * BT:(t + 1) * BT, :, g * GRP:(g + 1) * GRP, :].rearrange("b p g n -> p b (g n)")
                    src = src.rearrange("p (b n) -> p b n", b=BT)
                sp.dma_start(dst, src).then_inc(stored[i % 2], 16)
            n = len(items)
            sp.wait_ge(stored[0], 16 * ((n + 1) // 2))
            sp.wait_ge(stored[1], 16 * (n // 2))

        @block.scalar
        def _(act):
            norm.scalar(act)

            def make_hi(at):
                kind, g = order[at]
                act.wait_ge(raw_in[at % RAW], 16 * (at // RAW + 1))
                if kind == "q" and g >= WQ:
                    act.wait_ge(proj_ready, TT * (g - WQ + 1))
                act.activation(weights(kind, g)[0], raw[:, at % RAW], ACT.Copy).then_inc(w_hi_done, 1)

            def square(i):
                act.wait_ge(proj_ready, i + 1)
                if i:
                    act.wait_ge(ss_done, i)
                act.activation(sq[:], proj[i % NP][:], ACT.Square).then_inc(sq_done, 1)

            def turned(i):
                kind, g, t = items[i]
                if i >= 2:
                    act.wait_ge(stored[i % 2], 16 * (i // 2))
                if kind == "v":
                    act.wait_ge(proj_ready, i + 1)
                    act.activation(stg[:, i % 2, :], proj[i % NP][:], ACT.Copy).then_inc(stg_done, 1)
                    return
                act.wait_ge(turn_ready, i + 1)
                out = stg[:, i % 2, :].rearrange("p (b g n) -> p g b n", b=BT, g=GRP)
                src = turn[i % 2][:].rearrange("p (g b n) -> p g b n", b=BT, g=GRP)
                if kind == "q":
                    if i == 0:
                        act.wait_ge(qkw_done, 1)
                    act.activation(out, src, ACT.Copy, scale=qkw[:, 0:1]).then_inc(stg_done, 1)
                else:
                    act.activation(out, src, ACT.Copy).then_inc(stg_done, 1)

            made = 0
            for i in range(n_norm):
                while made < split_by(i):
                    make_hi(made)
                    made += 1
                if i == 4:
                    act.wait_ge(ct_in[0], 16)
                    act.activation(ct_hi[:, 0], ct_raw[:, 0], ACT.Copy).then_inc(ct_hi_done, 1)
                square(i)
                if i >= LAG:
                    turned(i - LAG)
            for i in range(n_norm - LAG, len(items)):
                turned(i)

        @block.vector
        def _(dve):
            norm.vector(dve)
            dve.wait_ge(nw_in, 32)
            dve.tensor_scalar(qkw[:], nw[:, 0:1], nw[:, 1:2], float(HD) ** -0.5, ALU.mult,
                              ALU.mult).then_inc(qkw_done, 1)

            def make_lo(at):
                kind, g = order[at]
                hi, lo = weights(kind, g)
                dve.wait_ge(w_hi_done, at + 1)
                dve.tensor_tensor(lo, raw[:, at % RAW], hi.bitcast(F32), ALU.subtract).then_inc(w_lo_done, 1)

            make_lo(0)
            made = 1
            for i in range(n_norm):
                dve.wait_ge(sq_done, i + 1)
                dve.tensor_reduce(ss[:, i % 2, :], sq[:].rearrange("p (g n) -> p g n", g=GRP), AX.X,
                                  ALU.add).then_inc(ss_done, 1)
                while made < split_by(i):
                    make_lo(made)
                    made += 1
                dve.wait_ge(rr_done, i + 1)
                if i >= 2:
                    dve.wait_ge(turn_ready, i - 1)
                dve.tensor_tensor(nrm[:, i % 2, :].rearrange("p (g n) -> p g n", g=GRP),
                                  proj[i % NP][:].rearrange("p (g n) -> p g n", g=GRP),
                                  rr[:, i % 2, :].unsqueeze(2).to_broadcast([P, GRP, HD]),
                                  ALU.mult).then_inc(nrm_done, 1)

        @block.gpsimd
        def _(pool):
            norm.gpsimd(pool)
            for i in range(n_norm):
                pool.wait_ge(ss_done, i + 1)
                pool.tensor_scalar(ms[:, i % 2, :], ss[:, i % 2, :], 1.0 / HD, eps, ALU.mult,
                                   ALU.add).then_inc(ms_done, 1)
                pool.wait_ge(ms_done, i + 1)
                if i >= 2:
                    pool.wait_ge(nrm_done, i - 1)
                pool.tensor_tensor(rr[:, i % 2, :], ms[:, i % 2, :], c.minus_half[:, 0:GRP],
                                   ALU.pow).then_inc(rr_done, 1)
                if i == 5:
                    pool.wait_ge(ct_hi_done, 1)
                    pool.tensor_tensor(ct_lo[:, 0], ct_raw[:, 0], ct_hi[:, 0].bitcast(F32),
                                       ALU.subtract).then_inc(ct_lo_done, 1)

        @block.tensor
        def _(pe):
            norm.tensor(pe)
            pe.wait_ge(norm.done, TT)
            def turn_rows(m):
                pe.wait_ge(nrm_done, m + 1)
                if m >= 2:
                    pe.wait_ge(stg_done, m - 1)
                for g in range(GRP):
                    last = pe.transpose(turn[m % 2][:, g * P:(g + 1) * P], nrm[:, m % 2, g * P:(g + 1) * P],
                                        c.ident[:])
                last.then_inc(turn_ready, 1)

            for i, (kind, g, t) in enumerate(items):
                name = ("q" if kind == "q" else "kv", g)
                pe.wait_ge(w_lo_done, place[name] + 1)
                if i >= NP:
                    if i - NP < n_norm:
                        pe.wait_ge(nrm_done, i - NP + 1)
                    else:
                        pe.wait_ge(stg_done, i - NP + 1)
                hi, lo = weights(*name)
                for k in range(DC):
                    toks = slice(t * P, (t + 1) * P)
                    last = split_matmul(pe, proj[i % NP][:], xT_hi[:, k, toks], xT_lo[:, k, toks], hi[:, k], lo[:, k],
                                        k == 0, k == DC - 1)
                last.then_inc(proj_ready, 1)
                if LAG <= i < n_norm + LAG:
                    turn_rows(i - LAG)
            for m in range(len(items) - LAG, n_norm):
                turn_rows(m)


def context_chunks(nc, st, tag):
    sb, _, sem = tiles(st, nc)
    return (sb(f"{tag}_ct_raw", [P, 2, DC, P]), sb(f"{tag}_ct_hi", [P, 2, DC, P], F32R),
            sb(f"{tag}_ct_lo", [P, 2, DC, P], F32R), [sem(f"{tag}_ct_in{i}") for i in range(2)],
            sem(f"{tag}_ct_hi_done"), sem(f"{tag}_ct_lo_done"))


def stage_context(c, tag, chunks, ctxT_dram, mask_dram, eps, w_hi, w_lo, q_dram, klat_dram, vlat_dram, o_dram):
    nc = c.nc
    with_latents = klat_dram is not None
    with_mask = mask_dram is not None
    NK = KEYS + (Q if with_latents else 0)
    ROWS = GRP * Q
    assert ROWS == P
    HPC = KVH // CHUNKS

    with ExitStack() as st:
        sb, ps, sem = tiles(st, nc)
        ct_raw, ct_hi, ct_lo, ct_in, ct_hi_done, ct_lo_done = chunks
        ksq = sb(f"{tag}_ksq", [P, COLS])
        kss = sb(f"{tag}_kss", [P, 2, GRP])
        kms = sb(f"{tag}_kms", [P, 2, GRP])
        krr = sb(f"{tag}_krr", [P, 2, GRP])
        khat = sb(f"{tag}_khat", [P, 2, COLS])
        kT = sb(f"{tag}_kT", [P, 2, KVH, KEYS])
        vv = sb(f"{tag}_vv", [P, 2, CHUNKS, KVH * HD])
        qcur = sb(f"{tag}_qcur", [P, 2, KVH, ROWS])
        ocur = sb(f"{tag}_ocur", [P, 2, KVH, ROWS])
        pr = sb(f"{tag}_pr", [P, 2, NK])
        pT = sb(f"{tag}_pT", [P, 2, KEYS])
        nmax = sb(f"{tag}_nmax", [P, 2])
        den = sb(f"{tag}_den", [P, 2])
        rden = sb(f"{tag}_rden", [P, 2])
        if with_mask:
            mask = sb(f"{tag}_mask", [P, KEYS])
            sm = sb(f"{tag}_sm", [P, KEYS])
        if with_latents:
            klat = sb(f"{tag}_klat", [P, 2, KVH, Q])
            vlat = sb(f"{tag}_vlat", [Q, 2, KVH * HD])
            pTlat = sb(f"{tag}_pTlat", [Q, 2, P])
        kp = [ps(f"{tag}_kp{i}", [P, COLS]) for i in range(2)]
        vp = ps(f"{tag}_vp", [P, COLS])
        ktp = ps(f"{tag}_ktp", [P, COLS])
        scp = ps(f"{tag}_scp", [P, 2 * COLS])
        ptp = ps(f"{tag}_ptp", [P, KEYS])
        op = ps(f"{tag}_op", [P, COLS])
        q_in = [sem(f"{tag}_q_in{i}") for i in range(2)]
        o_out = [sem(f"{tag}_o_out{i}") for i in range(2)]
        m_in = sem(f"{tag}_m_in")
        (k_ready, v_ready, ksq_done, kss_done, kms_done, krr_done, khat_done, ktp_ready,
         kT_done, v_done, s_ready, sm_done, nmax_done, exp_done, rden_done, pn_done, ptp_ready, pT_done, o_ready,
         o_done) = (sem(f"{tag}_{n}") for n in (
             "k_ready", "v_ready", "ksq_done", "kss_done", "kms_done", "krr_done",
             "khat_done", "ktp_ready", "kT_done", "v_done", "s_ready", "sm_done", "nmax_done", "exp_done", "rden_done",
             "pn_done", "ptp_ready", "pT_done", "o_ready", "o_done"))
        block = st.enter_context(nc.Block())
        Q_LOADS = 3 if with_latents else 1

        def over_batches(eng, run):
            run(0, 0)
            run(0, 1)
            with eng.Fori(1, B // 2) as pair:
                run(pair, 0)
                run(pair, 1)

        def wait(eng, semaphore, value):
            if not (isinstance(value, int) and value <= 0):
                eng.wait_ge(semaphore, value)

        def attends(pair, par):
            return not (isinstance(pair, int) and pair == par == 0)

        def chunk_no(pair, par, t):
            return pair * (2 * CHUNKS) + (par * CHUNKS + t)

        def head_no(pair, par, t):
            return pair * (2 * KVH) + (par * KVH + t * HPC - KVH)

        @block.sync
        def _(sp):
            if with_mask:
                for g in range(GRP):
                    sp.dma_start(mask[g * Q:(g + 1) * Q, :], mask_dram).then_inc(m_in, 16)

            def load_chunk(pair, par, t):
                n = chunk_no(pair, par, t)
                wait(sp, ct_lo_done, n - 1)
                sp.dma_start(ct_raw[:, t % 2], ctxT_dram[n]).then_inc(ct_in[t % 2], 16)

            def load_queries(pair, par):
                b = pair * 2 + par
                wait(sp, s_ready, (b - 1) * KVH)
                sp.dma_start(qcur[:, par], q_dram[b]).then_inc(q_in[par], 16)
                if with_latents:
                    wait(sp, o_ready, (b - 1) * KVH)
                    sp.dma_start(klat[:, par], klat_dram[b]).then_inc(q_in[par], 16)
                    sp.dma_start(vlat[:, par], vlat_dram[b]).then_inc(q_in[par], 16)

            def store(pair, par):
                b = pair * 2 + par
                sp.wait_ge(o_done, (b - 1) * KVH)
                sp.dma_start(o_dram[b - 2], ocur[:, par]).then_inc(o_out[par], 16)

            def run(pair, par):
                if attends(pair, par):
                    load_chunk(pair, par, 0)
                    load_chunk(pair, par, 1)
                if not (isinstance(pair, int) and pair == 0):
                    store(pair, par)
                load_queries(pair, par)
                for t in range(2, CHUNKS):
                    load_chunk(pair, par, t)

            over_batches(sp, run)
            store(B // 2, 0)
            store(B // 2, 1)
            for i in range(2):
                sp.wait_ge(o_out[i], 16 * (B // 2))

        @block.scalar
        def _(act):
            def make_hi(pair, par, t):
                n = chunk_no(pair, par, t)
                act.wait_ge(ct_in[t % 2], pair * (16 * CHUNKS) + 16 * (par * CHUNKS // 2 + t // 2 + 1))
                wait(act, v_ready, (n - 1) * 2)
                act.activation(ct_hi[:, t % 2], ct_raw[:, t % 2], ACT.Copy).then_inc(ct_hi_done, 1)

            def square(n, j):
                act.wait_ge(k_ready, n * 2 + (j + 1))
                wait(act, kss_done, n * 2 + j)
                act.activation(ksq[:], kp[j][:], ACT.Square).then_inc(ksq_done, 1)

            def keys(n, j, par, t):
                act.wait_ge(ktp_ready, n * 2 + (j + 1))
                act.activation(kT[:, par, j * GRP:(j + 1) * GRP, t * P:(t + 1) * P],
                               ktp[:].rearrange("p (g n) -> p g n", g=GRP), ACT.Copy).then_inc(kT_done, 1)

            def values(n, j, par, t):
                act.wait_ge(v_ready, n * 2 + (j + 1))
                act.activation(vv[:, par, t, j * COLS:(j + 1) * COLS], vp[:], ACT.Copy).then_inc(v_done, 1)

            def exps(h, slot):
                act.wait_ge(nmax_done, h + 1)
                wait(act, ptp_ready, h - 1)
                act.activation(pr[:, slot, :], sm[:] if with_mask else scp[:, 0:NK], ACT.Exp,
                               bias=nmax[:, slot:slot + 1], accum_out=den[:, slot:slot + 1]).then_inc(exp_done, 1)

            def run(pair, par):
                attend = attends(pair, par)
                if par == 0 and not isinstance(pair, int):
                    make_hi(pair, 0, 0)
                for t in range(CHUNKS):
                    n, h = chunk_no(pair, par, t), head_no(pair, par, t)
                    if attend:
                        exps(h, 0)
                    if not (t == CHUNKS - 1 and par == 1):
                        make_hi(pair, par, t + 1)
                    square(n, 0)
                    square(n, 1)
                    keys(n, 0, par, t)
                    if attend:
                        exps(h + 1, 1)
                    values(n, 0, par, t)
                    keys(n, 1, par, t)
                    values(n, 1, par, t)

            over_batches(act, run)
            for j in range(KVH):
                exps((B - 1) * KVH + j, j % 2)

        @block.vector
        def _(dve):
            def key_sums(n, j):
                dve.wait_ge(ksq_done, n * 2 + (j + 1))
                dve.tensor_reduce(kss[:, j, :], ksq[:].rearrange("p (g n) -> p g n", g=GRP), AX.X,
                                  ALU.add).then_inc(kss_done, 1)
                dve.wait_ge(kss_done, n * 2 + (j + 1))
                dve.tensor_scalar(kms[:, j, :], kss[:, j, :], 1.0 / HD, eps, ALU.mult, ALU.add).then_inc(kms_done, 1)

            def key_scale(n, j):
                dve.wait_ge(krr_done, n * 2 + (j + 1))
                wait(dve, ktp_ready, n * 2 + (j - 1))
                dve.tensor_tensor(khat[:, j, :].rearrange("p (g n) -> p g n", g=GRP),
                                  kp[j][:].rearrange("p (g n) -> p g n", g=GRP),
                                  krr[:, j, :].unsqueeze(2).to_broadcast([P, GRP, HD]), ALU.mult).then_inc(khat_done, 1)

            def row_max(h, slot):
                dve.wait_ge(s_ready, h + 1)
                if with_mask:
                    wait(dve, exp_done, h)
                    dve.tensor_tensor(sm[:], scp[:, 0:KEYS], mask[:], ALU.add).then_inc(sm_done, 1)
                    dve.wait_ge(sm_done, h + 1)
                    dve.tensor_reduce(nmax[:, slot:slot + 1], sm[:], AX.X, ALU.max,
                                      negate=True).then_inc(nmax_done, 1)
                else:
                    dve.tensor_reduce(nmax[:, slot:slot + 1], scp[:, 0:NK], AX.X, ALU.max,
                                      negate=True).then_inc(nmax_done, 1)

            def normalise(h, slot):
                dve.wait_ge(exp_done, h + 1)
                dve.reciprocal(rden[:, slot:slot + 1], den[:, slot:slot + 1]).then_inc(rden_done, 1)
                dve.wait_ge(rden_done, h + 1)
                dve.tensor_scalar(pr[:, slot, :], pr[:, slot, :], rden[:, slot:slot + 1], None,
                                  ALU.mult).then_inc(pn_done, 1)

            def probs(h, slot):
                dve.wait_ge(ptp_ready, h + 1)
                if with_latents:
                    dve.tensor_copy(pTlat[:, slot, :], op[0:Q, P:2 * P])
                dve.tensor_copy(pT[:, slot, :], ptp[:]).then_inc(pT_done, 1)

            def outputs(h, opar, j):
                dve.wait_ge(o_ready, h + 1)
                dve.tensor_copy(ocur[:, opar, j, :], op[:, 0:P]).then_inc(o_done, 1)

            def run(pair, par):
                attend = attends(pair, par)
                for t in range(CHUNKS):
                    n, h, j = chunk_no(pair, par, t), head_no(pair, par, t), t * HPC
                    if attend:
                        row_max(h, 0)
                        normalise(h, 0)
                        if t:
                            outputs(h - 1, 1 - par, j - 1)
                        elif not (isinstance(h, int) and h == 0):
                            outputs(h - 1, par, KVH - 1)
                    key_sums(n, 0)
                    key_scale(n, 0)
                    if attend:
                        probs(h, 0)
                    key_sums(n, 1)
                    if attend:
                        row_max(h + 1, 1)
                    key_scale(n, 1)
                    if attend:
                        normalise(h + 1, 1)
                        outputs(h, 1 - par, j)
                        probs(h + 1, 1)
                wait(dve, o_out[par], pair * 16)

            if with_mask:
                dve.wait_ge(m_in, 16 * GRP)
            over_batches(dve, run)
            last = (B - 1) * KVH
            for j in range(KVH):
                row_max(last + j, j % 2)
                if j == 0:
                    outputs(last - 1, 0, KVH - 1)
                else:
                    probs(last + j - 1, (j - 1) % 2)
                normalise(last + j, j % 2)
                if j:
                    outputs(last + j - 1, 1, j - 1)
            probs(last + KVH - 1, (KVH - 1) % 2)
            outputs(last + KVH - 1, 1, KVH - 1)

        @block.gpsimd
        def _(pool):
            def make_lo(n, slot):
                pool.wait_ge(ct_hi_done, n + 1)
                pool.tensor_tensor(ct_lo[:, slot], ct_raw[:, slot], ct_hi[:, slot].bitcast(F32),
                                   ALU.subtract).then_inc(ct_lo_done, 1)

            def key_factor(n, j):
                pool.wait_ge(kms_done, n * 2 + (j + 1))
                wait(pool, khat_done, n * 2 + (j - 1))
                pool.tensor_tensor(krr[:, j, :], kms[:, j, :], c.minus_half[:, 0:GRP], ALU.pow).then_inc(krr_done, 1)

            def run(pair, par):
                attend = attends(pair, par)
                if par == 0 and not isinstance(pair, int):
                    make_lo(chunk_no(pair, 0, 0), 0)
                for t in range(CHUNKS):
                    n = chunk_no(pair, par, t)
                    if not (t == CHUNKS - 1 and par == 1):
                        make_lo(n + 1, (t + 1) % 2)
                    key_factor(n, 0)
                    key_factor(n, 1)

            over_batches(pool, run)

        @block.tensor
        def _(pe):
            def project_group(out, slot, cols):
                for k in range(DC):
                    last = split_matmul(pe, out, ct_hi[:, slot, k, :], ct_lo[:, slot, k, :], w_hi[:, k, cols],
                                        w_lo[:, k, cols], k == 0, k == DC - 1)
                return last

            def project_k(n, j, slot):
                wait(pe, khat_done, n * 2 + (j - 1))
                project_group(kp[j][:], slot, slice(j * COLS, (j + 1) * COLS)).then_inc(k_ready, 1)

            def project_v(n, j, slot):
                wait(pe, v_done, n * 2 + j)
                cols = slice(KVH * HD + j * COLS, KVH * HD + (j + 1) * COLS)
                project_group(vp[:], slot, cols).then_inc(v_ready, 1)

            def turn_keys(n, j):
                pe.wait_ge(khat_done, n * 2 + (j + 1))
                wait(pe, kT_done, n * 2 + j)
                for g in range(GRP):
                    last = pe.transpose(ktp[:, g * P:(g + 1) * P], khat[:, j, g * P:(g + 1) * P], c.ident[:])
                last.then_inc(ktp_ready, 1)

            def scores(h, j, par):
                wait(pe, sm_done if with_mask else exp_done, h)
                last = pe.matmul(scp[:, 0:KEYS], qcur[:, par, j, :], kT[:, par, j, :], start=True, stop=True)
                if with_latents:
                    last = pe.matmul(scp[:, KEYS:NK], qcur[:, par, j, :], klat[:, par, j, :], start=True, stop=True)
                last.then_inc(s_ready, 1)

            def turn_probs(h, slot):
                pe.wait_ge(pn_done, h + 1)
                wait(pe, pT_done, h)
                if with_latents:
                    wait(pe, o_done, h)
                    pe.transpose(op[0:Q, P:2 * P], pr[:, slot, KEYS:NK], c.ident[:])
                for k in range(CHUNKS):
                    last = pe.transpose(ptp[:, k * P:(k + 1) * P], pr[:, slot, k * P:(k + 1) * P], c.ident[:])
                last.then_inc(ptp_ready, 1)

            def weigh(h, slot, j, par):
                pe.wait_ge(pT_done, h + 1)
                wait(pe, o_done, h)
                for k in range(CHUNKS):
                    last = pe.matmul(op[:, 0:P], vv[:, par, k, j * HD:(j + 1) * HD], pT[:, slot, k * P:(k + 1) * P],
                                     start=k == 0, stop=k == CHUNKS - 1 and not with_latents)
                if with_latents:
                    last = pe.matmul(op[:, 0:P], vlat[:, par, j * HD:(j + 1) * HD], pTlat[:, slot, :],
                                     start=False, stop=True)
                last.then_inc(o_ready, 1)

            def run(pair, par):
                attend = attends(pair, par)
                opar = 1 - par
                if attend:
                    pe.wait_ge(q_in[opar], (pair + par) * (16 * Q_LOADS))
                    pe.wait_ge(kT_done, chunk_no(pair, par, 0) * 2)
                for t in range(CHUNKS):
                    n, h, j, slot = chunk_no(pair, par, t), head_no(pair, par, t), t * HPC, t % 2
                    if attend:
                        scores(h, j, opar)
                    pe.wait_ge(ct_lo_done, n + 1)
                    project_k(n, 0, slot)
                    if attend and t:
                        weigh(h - 1, 1, j - 1, opar)
                    elif attend and not (isinstance(h, int) and h == 0):
                        weigh(h - 1, 1, KVH - 1, par)
                    project_k(n, 1, slot)
                    if attend:
                        turn_probs(h, 0)
                    turn_keys(n, 0)
                    if attend:
                        scores(h + 1, j + 1, opar)
                    project_v(n, 0, slot)
                    if attend:
                        if t == 0:
                            pe.wait_ge(v_done, n * 2)
                        weigh(h, 0, j, opar)
                    turn_keys(n, 1)
                    project_v(n, 1, slot)
                    if attend:
                        turn_probs(h + 1, 1)

            over_batches(pe, run)
            last = (B - 1) * KVH
            pe.wait_ge(q_in[1], B // 2 * 16 * Q_LOADS)
            pe.wait_ge(kT_done, B * CHUNKS * 2)
            scores(last, 0, 1)
            weigh(last - 1, 1, KVH - 1, 0)
            pe.wait_ge(v_done, B * CHUNKS * 2)
            for j in range(KVH):
                if j + 1 < KVH:
                    scores(last + j + 1, j + 1, 1)
                turn_probs(last + j, j % 2)
                weigh(last + j, j % 2, j, 1)


def stage_accumulate(c, tag, w_dram, rows, a_hi=None, a_lo=None, o_dram=None):
    nc = c.nc
    groups = (len(rows) + DC - 1) // DC
    with ExitStack() as st:
        sb, ps, sem = tiles(st, nc)
        raw = sb(f"{tag}_raw", [P, 2, DC, D])
        wh = sb(f"{tag}_wh", [P, 2, DC, D], F32R)
        wl = sb(f"{tag}_wl", [P, 2, DC, D], F32R)
        w_in = [sem(f"{tag}_w_in{i}") for i in range(2)]
        hi_done, lo_done, used, summed = (sem(f"{tag}_{n}") for n in ("hi_done", "lo_done", "used", "summed"))
        out = [ps(f"{tag}_out{t}", [P, D]) for t in range(TT)]
        if o_dram is not None:
            oraw = sb(f"{tag}_oraw", [P, 2, B, GRP * Q])
            oh = sb(f"{tag}_oh", [P, 2, GRP, TOK], F32R)
            ol = sb(f"{tag}_ol", [P, 2, GRP, TOK], F32R)
            oh_done = sem(f"{tag}_oh_done")
            ol_done = sem(f"{tag}_ol_done")
            o_in = [sem(f"{tag}_o_in{i}") for i in range(2)]
        block = st.enter_context(nc.Block())

        def full(g):
            part = rows[g * DC:(g + 1) * DC]
            whole = [k for k in range(len(part)) if part[k] == part[0]]
            pieces = [(part[0], 0, len(whole))]
            if len(whole) < len(part):
                pieces.append((part[-1], len(whole), len(part)))
            return pieces

        @block.sync
        def _(sp):
            for g in range(groups):
                if g >= 2:
                    sp.wait_ge(lo_done, g - 1)
                for n, a, b in full(g):
                    sp.dma_start(raw[0:n, g % 2, a:b, :], w_dram[g][0:n, a:b, :]).then_inc(w_in[g % 2], 16)
                if o_dram is not None:
                    if g >= 2:
                        sp.wait_ge(ol_done, g - 1)
                    sp.dma_start(oraw[:, g % 2], o_dram[:, :, g, :].rearrange("b p n -> p b n")).then_inc(o_in[g % 2], 16)

        counts = [0, 0]
        need = []
        for g in range(groups):
            counts[g % 2] += 16 * len(full(g))
            need.append(counts[g % 2])

        @block.scalar
        def _(act):
            for g in range(groups):
                act.wait_ge(w_in[g % 2], need[g])
                if g >= 2:
                    act.wait_ge(used, g - 1)
                for n, a, b in full(g):
                    last = act.activation(wh[0:n, g % 2, a:b, :], raw[0:n, g % 2, a:b, :], ACT.Copy)
                last.then_inc(hi_done, 1)
                if o_dram is not None:
                    act.wait_ge(o_in[g % 2], 16 * (g // 2 + 1))
                    act.activation(oh[:, g % 2].rearrange("p g (b n) -> p b g n", b=B),
                                   oraw[:, g % 2].rearrange("p b (g n) -> p b g n", g=GRP), ACT.Copy).then_inc(oh_done, 1)

        @block.vector
        def _(dve):
            for g in range(groups):
                dve.wait_ge(hi_done, g + 1)
                for n, a, b in full(g):
                    last = dve.tensor_tensor(wl[0:n, g % 2, a:b, :], raw[0:n, g % 2, a:b, :],
                                             wh[0:n, g % 2, a:b, :].bitcast(F32), ALU.subtract)
                last.then_inc(lo_done, 1)
            for t in range(TT):
                dve.wait_ge(used, groups)
                dve.tensor_tensor(c.x[:, t, :], c.x[:, t, :], out[t][:], ALU.add).then_inc(summed, 1)
            dve.wait_ge(summed, TT)

        @block.gpsimd
        def _(pool):
            if o_dram is not None:
                for g in range(groups):
                    pool.wait_ge(oh_done, g + 1)
                    pool.tensor_tensor(ol[:, g % 2].rearrange("p g (b n) -> p b g n", b=B),
                                       oraw[:, g % 2].rearrange("p b (g n) -> p b g n", g=GRP),
                                       oh[:, g % 2].bitcast(F32).rearrange("p g (b n) -> p b g n", b=B),
                                       ALU.subtract).then_inc(ol_done, 1)

        @block.tensor
        def _(pe):
            for g in range(groups):
                pe.wait_ge(lo_done, g + 1)
                if o_dram is not None:
                    pe.wait_ge(ol_done, g + 1)
                part = rows[g * DC:(g + 1) * DC]
                for k, n in enumerate(part):
                    for t in range(TT):
                        toks = slice(t * P, (t + 1) * P)
                        if o_dram is not None:
                            hi, lo = oh[:, g % 2, k, toks], ol[:, g % 2, k, toks]
                        else:
                            hi, lo = a_hi[0:n, g * DC + k, toks], a_lo[0:n, g * DC + k, toks]
                        last = split_matmul(pe, out[t][:], hi, lo, wh[0:n, g % 2, k, :], wl[0:n, g % 2, k, :],
                                            g == k == 0, g == groups - 1 and k == len(part) - 1)
                last.then_inc(used, 1)


def stage_ffn(c, tag, wg_dram, wu_dram, width, xT_hi, xT_lo, hT_hi, hT_lo):
    nc = c.nc
    chunks = [min(P, width - P * f) for f in range((width + P - 1) // P)]
    n = len(chunks)
    per = COLS // P
    loads = 2 * ((n + per - 1) // per)
    with ExitStack() as st:
        sb, ps, sem = tiles(st, nc)
        raw = sb(f"{tag}_raw", [P, 2, DC, COLS])
        wh = sb(f"{tag}_wh", [P, 4, DC, COLS], F32R)
        wl = sb(f"{tag}_wl", [P, 4, DC, COLS], F32R)
        g = sb(f"{tag}_g", [P, 2, TOK])
        h = sb(f"{tag}_h", [P, 2, TOK])
        gu = [ps(f"{tag}_gu{i}", [P, 2 * TOK]) for i in range(2)]
        w_in = [sem(f"{tag}_w_in{i}") for i in range(2)]
        hi_done, lo_done, gu_ready, g_done, h_done, hT_hi_done, hT_lo_done = (
            sem(f"{tag}_{x}") for x in ("hi_done", "lo_done", "gu_ready", "g_done", "h_done", "hT_hi_done",
                                        "hT_lo_done"))
        norm = LayerNorm(c, st, tag, xT_hi, xT_lo)
        block = st.enter_context(nc.Block())

        @block.sync
        def _(sp):
            for q in range(loads):
                if q >= 2:
                    sp.wait_ge(lo_done, q - 1)
                sp.dma_start(raw[:, q % 2], (wu_dram if q % 2 else wg_dram)[q // 2]).then_inc(w_in[q % 2], 16)

        @block.scalar
        def _(act):
            norm.scalar(act)

            def make_hi(q):
                act.wait_ge(w_in[q % 2], 16 * (q // 2 + 1))
                if q >= 4:
                    act.wait_ge(gu_ready, per * (q // 2 - 1))
                act.activation(wh[:, q % 4], raw[:, q % 2], ACT.Copy).then_inc(hi_done, 1)

            for q in range(4):
                make_hi(q)
            for f in range(n + 1):
                if f < n:
                    m = chunks[f]
                    act.wait_ge(gu_ready, f + 1)
                    if f >= 2:
                        act.wait_ge(h_done, f - 1)
                    act.activation(g[0:m, f % 2], gu[f % 2][0:m, 0:TOK], ACT.Silu).then_inc(g_done, 1)
                if f >= 1:
                    m = chunks[f - 1]
                    act.wait_ge(h_done, f)
                    act.activation(hT_hi[0:m, f - 1], h[0:m, (f - 1) % 2], ACT.Copy).then_inc(hT_hi_done, 1)
                if f == per - 1:
                    for q in range(4, loads):
                        make_hi(q)

        @block.vector
        def _(dve):
            norm.vector(dve)

            def make_lo(q):
                dve.wait_ge(hi_done, q + 1)
                dve.tensor_tensor(wl[:, q % 4], raw[:, q % 2], wh[:, q % 4].bitcast(F32),
                                  ALU.subtract).then_inc(lo_done, 1)

            for q in range(4):
                make_lo(q)
            for f in range(n):
                m, b = chunks[f], f % 2
                dve.wait_ge(g_done, f + 1)
                if f >= 2:
                    dve.wait_ge(hT_lo_done, f - 1)
                dve.tensor_tensor(h[0:m, b], gu[b][0:m, TOK:], g[0:m, b], ALU.mult).then_inc(h_done, 1)
                if f == per - 1:
                    for q in range(4, loads):
                        make_lo(q)

        @block.gpsimd
        def _(pool):
            norm.gpsimd(pool)
            for f in range(n):
                m = chunks[f]
                pool.wait_ge(hT_hi_done, f + 1)
                pool.tensor_tensor(hT_lo[0:m, f], h[0:m, f % 2], hT_hi[0:m, f].bitcast(F32),
                                   ALU.subtract).then_inc(hT_lo_done, 1)

        @block.tensor
        def _(pe):
            norm.tensor(pe)
            pe.wait_ge(norm.done, TT)
            for f in range(n):
                m, b = chunks[f], f % 2
                pe.wait_ge(lo_done, 2 * (f // per) + 2)
                if f >= 2:
                    pe.wait_ge(h_done, f - 1)
                cols = slice(f % per * P, f % per * P + m)
                for u in range(2):
                    q = (2 * (f // per) + u) % 4
                    for k in range(DC):
                        last = split_matmul(pe, gu[b][0:m, u * TOK:(u + 1) * TOK], wh[:, q, k, cols],
                                            wl[:, q, k, cols], xT_hi[:, k, :], xT_lo[:, k, :], k == 0, k == DC - 1)
                last.then_inc(gu_ready, 1)


NH, NKV, SHD = 32, 8, 16
SREP = NH // NKV


def stage_self_attention(c, wq_dram, wkv_dram, xT_hi, xT_lo, aT_hi, aT_lo):
    nc = c.nc
    HQ = NKV // 2
    NHK = NH * Q
    with ExitStack() as st:
        sb, ps, sem = tiles(st, nc)
        raw = sb("sa_raw", [P, DC, COLS + 2 * NKV * SHD])
        wh = sb("sa_wh", [P, DC, COLS + 2 * NKV * SHD], F32R)
        wl = sb("sa_wl", [P, DC, COLS + 2 * NKV * SHD], F32R)
        qT = sb("sa_qT", [P, SREP, TOK])
        diag8 = sb("sa_diag8", [P, NKV])
        diag4 = sb("sa_diag4", [P, HQ])
        causal = sb("sa_causal", [P, Q])
        kdiag = sb("sa_kdiag", [P, B, NKV, Q])
        vrep = sb("sa_vrep", [P, B, HQ, Q])
        vdiag = sb("sa_vdiag", [P, B, 2, HQ * SHD])
        sm = sb("sa_sm", [P, TT, NHK])
        ex = sb("sa_ex", [P, TT, NHK])
        mx = sb("sa_mx", [P, TT, NH])
        den = sb("sa_den", [P, TT, NH])
        rden = sb("sa_rden", [P, TT, NH])
        pT = sb("sa_pT", [P, TT, NHK])
        o = sb("sa_o", [P, TT, D])
        two = ps("sa_two", [P, 2 * COLS])
        kv = ps("sa_kv", [P, COLS])
        sc = [ps(f"sa_sc{t}", [P, NHK]) for t in range(TT)]
        (w_in, hi_done, lo_done, masks, masks0, q_ready, kv_ready, qT_done, kdiag_done, vrep_done, vt_ready, vdiag_done,
         s_ready, sm_done, mx_done, sub_done, ex_done, den_done, rden_done, pn_done, pt_ready, pT_done, o_ready, o_done,
         at_ready, at_hi_done, at_lo_done) = (sem(f"sa_{n}") for n in (
             "w_in", "hi_done", "lo_done", "masks", "masks0", "q_ready", "kv_ready", "qT_done", "kdiag_done",
             "vrep_done", "vt_ready", "vdiag_done", "s_ready", "sm_done", "mx_done", "sub_done", "ex_done",
             "den_done", "rden_done", "pn_done", "pt_ready", "pT_done", "o_ready", "o_done", "at_ready",
             "at_hi_done", "at_lo_done"))
        norm = LayerNorm(c, st, "sa", xT_hi, xT_lo, sc)
        block = st.enter_context(nc.Block())

        @block.sync
        def _(sp):
            sp.dma_start(raw[:, :, 0:COLS], wq_dram).then_inc(w_in, 16)
            sp.dma_start(raw[:, :, COLS:], wkv_dram).then_inc(w_in, 16)

        @block.scalar
        def _(act):
            norm.scalar(act)
            act.wait_ge(w_in, 32)
            act.activation(wh[:], raw[:], ACT.Copy).then_inc(hi_done, 1)
            act.wait_ge(q_ready, 1)
            act.activation(qT[:].rearrange("p g n -> p (g n)"), two[:], ACT.Copy,
                           scale=float(SHD) ** -0.5).then_inc(qT_done, 1)
            act.wait_ge(kdiag_done, 1)
            act.activation(vrep[:], kv[:, TOK:].rearrange("p (b n) -> p b n", b=B).unsqueeze(2)
                           .to_broadcast([P, B, HQ, Q]), ACT.Copy).then_inc(vrep_done, 1)
            for t in range(TT):
                act.wait_ge(sub_done, t + 1)
                act.activation(ex[:, t, :], sm[:, t, :], ACT.Exp).then_inc(ex_done, 1)
            for t in range(TT):
                act.wait_ge(pt_ready, t + 1)
                act.activation(pT[:, t, :], sc[t][:], ACT.Copy).then_inc(pT_done, 1)
            for t in range(TT):
                act.wait_ge(at_ready, t + 1)
                act.activation(aT_hi[:, :, t * P:(t + 1) * P], sc[t][:, 0:D].rearrange("p (g n) -> p g n", g=SREP),
                               ACT.Copy).then_inc(at_hi_done, 1)

        @block.gpsimd
        def _(pool):
            norm.gpsimd(pool)
            pool.memset(diag8[:], 1.0)
            pool.memset(diag4[:], 1.0)
            pool.memset(causal[:], 0.0).then_inc(masks0, 1)
            pool.wait_ge(masks0, 1)
            lowest = float(np.finfo(np.float32).min)
            for b in range(BT):
                rows = slice(b * Q, (b + 1) * Q)
                pool.affine_select(out=causal[rows, :], in_=causal[rows, :], compare_op=ALU.is_ge, fill=lowest,
                                   base=0, pattern=[[-1, Q]], channel_multiplier=1).then_inc(masks, 1)
                pool.wait_ge(masks, b + 1)
            at = BT
            for mask, width, cols in ((diag8, SHD, NKV), (diag4, Q, HQ)):
                for low in (True, False):
                    pool.affine_select(out=mask[:], in_=mask[:], compare_op=ALU.is_ge, fill=0.0,
                                       base=0 if low else width - 1, pattern=[[-width if low else width, cols]],
                                       channel_multiplier=1 if low else -1).then_inc(masks, 1)
                    at += 1
                    pool.wait_ge(masks, at)
            for t in range(TT):
                pool.wait_ge(rden_done, t + 1)
                p3 = ex[:, t, :].rearrange("p (h n) -> p h n", h=NH)
                pool.tensor_tensor(p3, p3, rden[:, t, :].unsqueeze(2).to_broadcast([P, NH, Q]),
                                   ALU.mult).then_inc(pn_done, 1)

        @block.vector
        def _(dve):
            norm.vector(dve)
            dve.wait_ge(hi_done, 1)
            dve.tensor_tensor(wl[:], raw[:], wh[:].bitcast(F32), ALU.subtract).then_inc(lo_done, 1)
            dve.wait_ge(kv_ready, 1)
            dve.wait_ge(masks, BT + 4)
            dve.tensor_tensor(kdiag[:], kv[:, 0:TOK].rearrange("p (b n) -> p b n", b=B).unsqueeze(2)
                              .to_broadcast([P, B, NKV, Q]),
                              diag8[:].unsqueeze(1).unsqueeze(3).to_broadcast([P, B, NKV, Q]),
                              ALU.mult).then_inc(kdiag_done, 1)
            dve.wait_ge(vt_ready, 1)
            dve.tensor_tensor(vdiag[:].rearrange("p b u (j d) -> p (b u) j d", d=SHD),
                              two[:].rearrange("p (a j d) -> p a j d", j=HQ, d=SHD),
                              diag4[:].unsqueeze(1).unsqueeze(3).to_broadcast([P, 2 * B, HQ, SHD]),
                              ALU.mult).then_inc(vdiag_done, 1)
            for t in range(TT):
                s3 = sm[:, t, :].rearrange("p (h n) -> p h n", h=NH)
                dve.wait_ge(s_ready, t + 1)
                dve.tensor_tensor(s3, sc[t][:].rearrange("p (h n) -> p h n", h=NH),
                                  causal[:].unsqueeze(1).to_broadcast([P, NH, Q]), ALU.add).then_inc(sm_done, 1)
                dve.wait_ge(sm_done, t + 1)
                dve.tensor_reduce(mx[:, t, :], s3, AX.X, ALU.max).then_inc(mx_done, 1)
                dve.wait_ge(mx_done, t + 1)
                dve.tensor_tensor(s3, s3, mx[:, t, :].unsqueeze(2).to_broadcast([P, NH, Q]),
                                  ALU.subtract).then_inc(sub_done, 1)
            for t in range(TT):
                dve.wait_ge(ex_done, t + 1)
                dve.tensor_reduce(den[:, t, :], ex[:, t, :].rearrange("p (h n) -> p h n", h=NH), AX.X,
                                  ALU.add).then_inc(den_done, 1)
                dve.wait_ge(den_done, t + 1)
                dve.reciprocal(rden[:, t, :], den[:, t, :]).then_inc(rden_done, 1)
            for t in range(TT):
                dve.wait_ge(o_ready, t + 1)
                dve.tensor_copy(o[:, t, :], two[:, t * D:(t + 1) * D]).then_inc(o_done, 1)
            for t in range(TT):
                dve.wait_ge(at_hi_done, t + 1)
                dve.tensor_tensor(aT_lo[:, :, t * P:(t + 1) * P], sc[t][:, 0:D].rearrange("p (g n) -> p g n", g=SREP),
                                  aT_hi[:, :, t * P:(t + 1) * P].bitcast(F32), ALU.subtract).then_inc(at_lo_done, 1)

        @block.tensor
        def _(pe):
            norm.tensor(pe)
            pe.wait_ge(norm.done, TT)
            pe.wait_ge(lo_done, 1)

            def project(out, col):
                for k in range(DC):
                    cols = slice(col, col + P)
                    last = split_matmul(pe, out, wh[:, k, cols], wl[:, k, cols], xT_hi[:, k, :], xT_lo[:, k, :],
                                        k == 0, k == DC - 1)
                return last

            project(kv[:, 0:TOK], COLS)
            project(kv[:, TOK:], COLS + P).then_inc(kv_ready, 1)
            for g in range(SREP):
                last = project(two[:, g * TOK:(g + 1) * TOK], g * P)
            last.then_inc(q_ready, 1)
            pe.wait_ge(vrep_done, 1)
            pe.wait_ge(qT_done, 1)
            for b in range(B):
                last = pe.transpose(two[:, b * P:(b + 1) * P], vrep[:, b].rearrange("p r n -> p (r n)"), c.ident[:])
            last.then_inc(vt_ready, 1)
            pe.wait_ge(kdiag_done, 1)
            for t in range(TT):
                for b in range(BT):
                    for g in range(SREP):
                        last = pe.matmul(sc[t][b * Q:(b + 1) * Q, g * NKV * Q:(g + 1) * NKV * Q],
                                         qT[:, g, (t * BT + b) * Q:(t * BT + b + 1) * Q],
                                         kdiag[:, t * BT + b].rearrange("p j n -> p (j n)"), start=True, stop=True)
                last.then_inc(s_ready, 1)
            for t in range(TT):
                pe.wait_ge(pn_done, t + 1)
                for a in range(NHK // P):
                    last = pe.transpose(sc[t][:, a * P:(a + 1) * P], ex[:, t, a * P:(a + 1) * P], c.ident[:])
                last.then_inc(pt_ready, 1)
            pe.wait_ge(vdiag_done, 1)
            for t in range(TT):
                pe.wait_ge(pT_done, t + 1)
                for b in range(BT):
                    for a in range(NHK // P):
                        width = HQ * SHD
                        last = pe.matmul(two[b * Q:(b + 1) * Q, t * D + a * width:t * D + (a + 1) * width],
                                         pT[:, t, a * P + b * Q:a * P + (b + 1) * Q], vdiag[:, t * BT + b, a % 2, :],
                                         start=True, stop=True)
                last.then_inc(o_ready, 1)
            for t in range(TT):
                pe.wait_ge(o_done, t + 1)
                for g in range(SREP):
                    last = pe.transpose(sc[t][:, g * P:(g + 1) * P], o[:, t, g * P:(g + 1) * P], c.ident[:])
                last.then_inc(at_ready, 1)


MD, MN, MK, MR = 1024, 16, 4, 32
MC = MD // P
MSP = MR + 2 * MN


def stage_scan_inputs(c, win_dram, conv_w, conv_b, xT_hi, xT_lo, u, sg):
    nc = c.nc
    groups = 2 * MD // COLS
    pairs = MC
    per = COLS // (2 * P)
    W = 2 * TOK
    with ExitStack() as st:
        sb, ps, sem = tiles(st, nc)
        raw = sb("mi_raw", [P, 2, DC, COLS])
        wh = sb("mi_wh", [P, 2, DC, COLS], F32R)
        wl = sb("mi_wl", [P, 2, DC, COLS], F32R)
        ux = sb("mi_ux", [P, 2, W])
        acc = sb("mi_acc", [P, 2, W])
        pj = [ps(f"mi_pj{i}", [P, W]) for i in range(4)]
        w_in = [sem(f"mi_w_in{i}") for i in range(2)]
        hi_done, lo_done, pj_ready, ux_done, conv_done, acc_done, out_done = (
            sem(f"mi_{x}") for x in ("hi_done", "lo_done", "pj_ready", "ux_done", "conv_done", "acc_done",
                                     "out_done"))
        norm = LayerNorm(c, st, "mi", xT_hi, xT_lo)
        block = st.enter_context(nc.Block())

        @block.sync
        def _(sp):
            for g in range(groups):
                if g >= 2:
                    sp.wait_ge(lo_done, g - 1)
                sp.dma_start(raw[:, g % 2], win_dram[g]).then_inc(w_in[g % 2], 16)

        @block.scalar
        def _(act):
            norm.scalar(act)

            def make_hi(g):
                act.wait_ge(w_in[g % 2], 16 * (g // 2 + 1))
                if g >= 2:
                    act.wait_ge(pj_ready, per * (g - 1))
                act.activation(wh[:, g % 2], raw[:, g % 2], ACT.Copy).then_inc(hi_done, 1)

            def activate(m):
                act.wait_ge(conv_done, (2 * MK - 1) * (m + 1))
                act.wait_ge(acc_done, m + 1)
                act.activation(u[:, 2 * m:2 * m + 2, :].rearrange("p c n -> p (c n)"), acc[:, m % 2],
                               ACT.Silu).then_inc(out_done, 1)

            make_hi(0)
            make_hi(1)
            for m in range(pairs):
                if m % per == 0 and m and m // per + 1 < groups:
                    make_hi(m // per + 1)
                act.wait_ge(pj_ready, m + 1)
                if m >= pairs // 2:
                    act.activation(sg[:, 2 * m - MC:2 * m - MC + 2, :].rearrange("p c n -> p (c n)"), pj[m % 4][:],
                                   ACT.Silu).then_inc(out_done, 1)
                    continue
                if m >= 2:
                    act.wait_ge(acc_done, m - 1)
                act.activation(ux[:, m % 2], pj[m % 4][:], ACT.Copy).then_inc(ux_done, 1)
                if m:
                    activate(m - 1)
                if m == pairs // 2 - 1:
                    activate(m)

        @block.gpsimd
        def _(pool):
            norm.gpsimd(pool)

        @block.vector
        def _(dve):
            norm.vector(dve)

            def make_lo(g):
                dve.wait_ge(hi_done, g + 1)
                dve.tensor_tensor(wl[:, g % 2], raw[:, g % 2], wh[:, g % 2].bitcast(F32),
                                  ALU.subtract).then_inc(lo_done, 1)

            taps = 0
            make_lo(0)
            make_lo(1)
            for m in range(pairs):
                b = m % 2
                gate = m >= pairs // 2
                if m % per == 0 and m and m // per + 1 < groups:
                    make_lo(m // per + 1)
                if not gate:
                    dve.wait_ge(ux_done, m + 1)
                    if m >= 2:
                        dve.wait_ge(out_done, m - 1)
                    for tap in range(MK):
                        if tap:
                            dve.wait_ge(conv_done, taps)
                        for k in range(2):
                            ch = 2 * m + k
                            x3 = ux[:, b, k * TOK:(k + 1) * TOK].rearrange("p (b t) -> p b t", b=B)
                            a3 = acc[:, b, k * TOK:(k + 1) * TOK].rearrange("p (b t) -> p b t", b=B)
                            w = conv_w[:, ch, MK - 1 - tap:MK - tap]
                            if tap == 0:
                                dve.tensor_scalar(a3, x3, w, conv_b[:, ch:ch + 1], ALU.mult,
                                                  ALU.add).then_inc(conv_done, 1)
                            else:
                                last = dve.scalar_tensor_tensor(out=a3[:, :, tap:], in0=x3[:, :, :Q - tap], scalar=w,
                                                                in1=a3[:, :, tap:], op0=ALU.mult, op1=ALU.add)
                                last.then_inc(conv_done if tap < MK - 1 or k == 0 else acc_done, 1)
                            taps += not (tap == MK - 1 and k == 1)

        @block.tensor
        def _(pe):
            norm.tensor(pe)
            pe.wait_ge(norm.done, TT)
            for m in range(pairs):
                g = m // per
                pe.wait_ge(lo_done, g + 1)
                if m >= 4:
                    pe.wait_ge(ux_done, m - 3)
                for half in range(2):
                    col = (m % per * 2 + half) * P
                    for k in range(DC):
                        last = split_matmul(pe, pj[m % 4][:, half * TOK:(half + 1) * TOK], wh[:, g % 2, k, col:col + P],
                                            wl[:, g % 2, k, col:col + P], xT_hi[:, k, :], xT_lo[:, k, :],
                                            k == 0, k == DC - 1)
                last.then_inc(pj_ready, 1)


def stage_scan_params(c, wx_dram, wdt_dram, dt_bias, lnw_dram, bc_dram, u, delta, du, bc):
    nc = c.nc
    PARTS = MSP // MN
    W = 2 * TOK
    with ExitStack() as st:
        sb, ps, sem = tiles(st, nc)
        wx = sb("mp_wx", [P, MC, MSP])
        wdt = sb("mp_wdt", [MR, MD])
        lnw = sb("mp_lnw", [P, MSP])
        sq = sb("mp_sq", [P, TT, MSP])
        ss = sb("mp_ss", [P, TT, PARTS])
        s2 = sb("mp_s2", [P, TT])
        ms = sb("mp_ms", [P, TT, PARTS])
        rr = sb("mp_rr", [P, TT, PARTS])
        n1 = sb("mp_n1", [P, TT, MSP])
        n2 = sb("mp_n2", [P, TT, MSP])
        dtT = sb("mp_dtT", [MR, TOK])
        bcT = sb("mp_bcT", [2 * MN, TOK])
        xb = sb("mp_xb", [P, MC, TOK])
        ax = sb("mp_ax", [P, MC, TOK])
        e = sb("mp_e", [P, MC, TOK])
        par = ps("mp_par", [P, TT * MSP])
        turn = ps("mp_turn", [MR, 2 * TOK])
        dl = [ps(f"mp_dl{m}", [P, W]) for m in range(MC // 2)]
        (w_in, par_ready, sq_done, ss_done, s2_done, s3_done, ms_done, rr_done, n1_done, n2_done, turn_ready, dtT_done,
         bcT_done, bc_out, bc_in, dl_ready, xb_done, ax_done, e_done, l_done, relu_done, d_done, du_done) = (
             sem(f"mp_{x}") for x in (
                 "w_in", "par_ready", "sq_done", "ss_done", "s2_done", "s3_done", "ms_done", "rr_done", "n1_done",
                 "n2_done", "turn_ready", "dtT_done", "bcT_done", "bc_out", "bc_in", "dl_ready", "xb_done", "ax_done",
                 "e_done", "l_done", "relu_done", "d_done", "du_done"))
        block = st.enter_context(nc.Block())

        @block.sync
        def _(sp):
            sp.dma_start(wx[:], wx_dram).then_inc(w_in, 16)
            sp.dma_start(wdt[:], wdt_dram).then_inc(w_in, 16)
            sp.dma_start(lnw[:], lnw_dram.unsqueeze(0).to_broadcast([P, MSP])).then_inc(w_in, 16)
            sp.wait_ge(bcT_done, 1)
            sp.dma_start(bc_dram, bcT[:]).then_inc(bc_out, 16)
            sp.wait_ge(bc_out, 16)
            sp.dma_start(bc[:], bc_dram.unsqueeze(0).to_broadcast([P, 2 * MN, TOK])).then_inc(bc_in, 16)
            sp.wait_ge(bc_in, 16)

        @block.tensor
        def _(pe):
            pe.wait_ge(w_in, 48)
            for t in range(TT):
                for k in range(MC):
                    last = pe.matmul(par[:, t * MSP:(t + 1) * MSP], u[:, k, t * P:(t + 1) * P], wx[:, k, :],
                                     start=k == 0, stop=k == MC - 1)
            last.then_inc(par_ready, 1)
            pe.wait_ge(n2_done, 1)
            for t in range(TT):
                pe.transpose(turn[:, t * P:(t + 1) * P], n2[:, t, 0:MR], c.ident[:])
                last = pe.transpose(turn[:, TOK + t * P:TOK + (t + 1) * P], n2[:, t, MR:], c.ident[:])
            last.then_inc(turn_ready, 1)
            pe.wait_ge(dtT_done, 1)
            for ch in range(MC):
                last = pe.matmul(dl[ch // 2][:, ch % 2 * TOK:(ch % 2 + 1) * TOK], wdt[:, ch * P:(ch + 1) * P], dtT[:],
                                 start=True, stop=True)
                if ch % 2:
                    last.then_inc(dl_ready, 1)

        @block.scalar
        def _(act):
            act.wait_ge(par_ready, 1)
            act.activation(sq[:].rearrange("p t n -> p (t n)"), par[:], ACT.Square).then_inc(sq_done, 1)
            act.wait_ge(turn_ready, 1)
            act.activation(dtT[:], turn[:, 0:TOK], ACT.Copy).then_inc(dtT_done, 1)
            act.activation(bcT[:], turn[:, TOK:], ACT.Copy).then_inc(bcT_done, 1)
            for ch in range(MC):
                act.wait_ge(xb_done, ch + 1)
                act.activation(ax[:, ch, :], xb[:, ch, :], ACT.Abs).then_inc(ax_done, 1)
            act.wait_ge(ax_done, MC)
            act.activation(e[:], ax[:], ACT.Exp, scale=-1.0).then_inc(e_done, 1)
            act.wait_ge(e_done, 1)
            act.activation(ax[:], e[:], ACT.Ln, bias=1.0).then_inc(l_done, 1)

        @block.gpsimd
        def _(pool):
            pool.wait_ge(s3_done, 1)
            pool.tensor_scalar(ms[:], ss[:], 1.0 / MN, 1e-6, ALU.mult, ALU.add).then_inc(ms_done, 1)
            pool.wait_ge(ms_done, 1)
            pool.tensor_tensor(rr[:].rearrange("p t n -> p (t n)"), ms[:].rearrange("p t n -> p (t n)"),
                               c.minus_half[:, 0:TT * PARTS], ALU.pow).then_inc(rr_done, 1)

        @block.vector
        def _(dve):
            dve.wait_ge(sq_done, 1)
            dve.tensor_reduce(ss[:].rearrange("p t n -> p (t n)"), sq[:].rearrange("p t (n k) -> p (t n) k", k=MN), AX.X,
                              ALU.add).then_inc(ss_done, 1)
            dve.wait_ge(ss_done, 1)
            dve.tensor_tensor(s2[:], ss[:, :, 0], ss[:, :, 1], ALU.add).then_inc(s2_done, 1)
            dve.wait_ge(s2_done, 1)
            dve.tensor_scalar(ss[:, :, 0:2], s2[:].unsqueeze(2).to_broadcast([P, TT, 2]), float(MN) / MR, None,
                              ALU.mult).then_inc(s3_done, 1)
            dve.wait_ge(rr_done, 1)
            dve.tensor_tensor(n1[:].rearrange("p t (n k) -> p (t n) k", k=MN),
                              par[:].rearrange("p (n k) -> p n k", k=MN),
                              rr[:].rearrange("p t n -> p (t n)").unsqueeze(2).to_broadcast([P, TT * PARTS, MN]),
                              ALU.mult).then_inc(n1_done, 1)
            dve.wait_ge(n1_done, 1)
            dve.wait_ge(w_in, 48)
            dve.tensor_tensor(n2[:], n1[:], lnw[:].unsqueeze(1).to_broadcast([P, TT, MSP]), ALU.mult).then_inc(n2_done, 1)
            for ch in range(MC):
                dve.wait_ge(dl_ready, ch // 2 + 1)
                dve.tensor_scalar(xb[:, ch, :], dl[ch // 2][:, ch % 2 * TOK:(ch % 2 + 1) * TOK], dt_bias[:, ch:ch + 1],
                                  None, ALU.add).then_inc(xb_done, 1)
            dve.wait_ge(xb_done, MC)
            dve.wait_ge(l_done, 1)
            dve.scalar_tensor_tensor(out=delta[:], in0=xb[:], scalar=0.0, in1=ax[:], op0=ALU.max,
                                     op1=ALU.add).then_inc(d_done, 1)
            dve.wait_ge(d_done, 1)
            dve.tensor_tensor(du[:], delta[:], u[:], ALU.mult).then_inc(du_done, 1)


def stage_scan(c, A, Dp, u, sg, delta, du, bc, yT_hi, yT_lo):
    nc = c.nc
    W = MN * TOK
    with ExitStack() as st:
        sb, ps, sem = tiles(st, nc)
        dA = sb("sc_dA", [P, 2, MN, TOK])
        x = sb("sc_x", [P, 2, MN, TOK])
        h = sb("sc_h", [P, 2, MN, TOK])
        y1 = sb("sc_y1", [P, 2, TOK])
        y2 = sb("sc_y2", [P, 2, TOK])
        yp = [ps(f"sc_yp{i}", [P, TOK]) for i in range(2)]
        dA_done, reset, x_done, h_done, hc_done, y_ready, y1_done, y2_done, hi_done, lo_done = (
            sem(f"sc_{n}") for n in ("dA_done", "reset", "x_done", "h_done", "hc_done", "y_ready", "y1_done",
                                     "y2_done", "hi_done", "lo_done"))
        block = st.enter_context(nc.Block())

        @block.scalar
        def _(act):
            def make_hi(k):
                act.wait_ge(y2_done, k + 1)
                act.activation(yT_hi[:, k, :], y2[:, k % 2], ACT.Copy).then_inc(hi_done, 1)

            for k in range(MC):
                if k >= 2:
                    act.wait_ge(h_done, k - 1)
                for n in range(MN):
                    last = act.activation(dA[:, k % 2, n, :], delta[:, k, :], ACT.Exp, scale=A[:, k, n:n + 1])
                last.then_inc(dA_done, 1)
                if k >= 2:
                    make_hi(k - 2)
            make_hi(MC - 2)
            make_hi(MC - 1)

        @block.gpsimd
        def _(pool):
            def make_lo(k):
                pool.wait_ge(hi_done, k + 1)
                pool.tensor_tensor(yT_lo[:, k, :], y2[:, k % 2], yT_hi[:, k, :].bitcast(F32),
                                   ALU.subtract).then_inc(lo_done, 1)

            for k in range(MC):
                if k >= 2:
                    pool.wait_ge(h_done, k - 1)
                pool.tensor_tensor(x[:, k % 2], du[:, k, :].unsqueeze(1).to_broadcast([P, MN, TOK]), bc[:, 0:MN, :],
                                   ALU.mult).then_inc(x_done, 1)
                if k >= 3:
                    make_lo(k - 3)
            for k in range(MC - 3, MC):
                make_lo(k)

        @block.vector
        def _(dve):
            def finish(k):
                dve.wait_ge(y_ready, k + 1)
                dve.scalar_tensor_tensor(out=y1[:, k % 2], in0=u[:, k, :], scalar=Dp[:, k:k + 1], in1=yp[k % 2][:],
                                         op0=ALU.mult, op1=ALU.add).then_inc(y1_done, 1)
                dve.wait_ge(y1_done, k + 1)
                if k >= 2:
                    dve.wait_ge(lo_done, k - 1)
                dve.tensor_tensor(y2[:, k % 2], y1[:, k % 2], sg[:, k, :], ALU.mult).then_inc(y2_done, 1)

            for k in range(MC):
                b = k % 2
                dve.wait_ge(dA_done, k + 1)
                dve.memset(dA[:, b].rearrange("p n (b t) -> p (n b) t", t=Q)[:, :, 0:1], 0.0).then_inc(reset, 1)
                dve.wait_ge(reset, k + 1)
                dve.wait_ge(x_done, k + 1)
                if k >= 2:
                    dve.wait_ge(y_ready, k - 1)
                dve.tensor_tensor_scan(h[:, b].rearrange("p n t -> p (n t)"), dA[:, b].rearrange("p n t -> p (n t)"),
                                       x[:, b].rearrange("p n t -> p (n t)"), 0.0, ALU.mult,
                                       ALU.add).then_inc(h_done, 1)
                dve.wait_ge(h_done, k + 1)
                dve.tensor_tensor(h[:, b], h[:, b], bc[:, MN:, :], ALU.mult).then_inc(hc_done, 1)
                if k:
                    finish(k - 1)
            finish(MC - 1)

        @block.tensor
        def _(pe):
            for k in range(MC):
                pe.wait_ge(hc_done, k + 1)
                if k >= 2:
                    pe.wait_ge(y1_done, k - 1)
                for n in range(MN):
                    last = pe.matmul(yp[k % 2][:], c.ident[:], h[:, k % 2, n, :], start=n == 0, stop=n == MN - 1)
                last.then_inc(y_ready, 1)


OC = 8
OIN, OHID = D // OC, 1366 // OC
OHALF = OHID // 2


def octonion_signs():
    table = np.zeros((OC, OC, OC), np.int64)
    table[0, 0, 0] = 1
    for i in range(1, OC):
        table[0, i, i] = table[i, 0, i] = 1
        table[i, i, 0] = -1
    for a, b, d in [(1, 2, 3), (1, 4, 5), (1, 7, 6), (2, 4, 6), (2, 5, 7), (3, 4, 7), (3, 6, 5)]:
        for x, y, z in ((a, b, d), (b, d, a), (d, a, b)):
            table[x, y, z], table[y, x, z] = 1, -1
    return [[int(table[i ^ k, i, k]) for k in range(OC)] for i in range(OC)]


def stage_ternary(c, w_drams, m_gate, m_up, m_down, scales):
    nc = c.nc
    sign = octonion_signs()
    names = ("gate", "up", "down")
    shapes = ([P, OC, OHID], [P, OC, OHID], [OHALF, OC, 2, OIN])
    COUNT = OC * OHID * OIN
    with ExitStack() as st:
        sb, ps, sem = tiles(st, nc)
        w = [sb(f"te_w_{n}", s) for n, s in zip(names, shapes)]
        low = [sb(f"te_low_{n}", s) for n, s in zip(names, shapes)]
        tern = [sb(f"te_tern_{n}", [s[0], 2, *s[1:]], F32R) for n, s in zip(names, shapes)]
        ones = sb("te_ones", [P, P])
        sums = sb("te_sums", [P, 3])
        half = sb("te_half", [P, 3])
        mhalf = sb("te_mhalf", [P, 3])
        total = ps("te_total", [P, 3])
        (w_in, ones_done, sum_done, total_ready, half_done, mhalf_done, low_done, pos_done, neg_done,
         spread) = (sem(f"te_{n}") for n in ("w_in", "ones_done", "sum_done", "total_ready", "half_done",
                                             "mhalf_done", "low_done", "pos_done", "neg_done", "spread"))
        block = st.enter_context(nc.Block())

        @block.sync
        def _(sp):
            for i in range(2):
                for half_rows in range(2):
                    sp.dma_start(w[i][half_rows * OIN:(half_rows + 1) * OIN], w_drams[i]).then_inc(w_in, 16)
            sp.dma_start(w[2][:], w_drams[2]).then_inc(w_in, 16)

        @block.tensor
        def _(pe):
            pe.wait_ge(ones_done, 1)
            pe.wait_ge(sum_done, 3)
            for i in range(3):
                n = (OIN, OIN, OHALF)[i]
                last = pe.matmul(total[:, i:i + 1], ones[0:n, :], sums[0:n, i:i + 1], start=True, stop=True)
            last.then_inc(total_ready, 1)

        def place(i, k):
            return i % 2 * OIN, i // 2

        def spread_in(copy, which, m, i):
            p, chunk = place(i, 0)
            for k in range(OC):
                neg = int(sign[i][k] < 0)
                last = copy(m[p:p + OIN, chunk, k, :], tern[which][p:p + OIN, neg, i ^ k, :])
            last.then_inc(spread, 1)

        def spread_down(copy, i):
            for k in range(OC):
                neg = int(sign[i][k] < 0)
                last = copy(m_down[:, :, i, k * OIN:(k + 1) * OIN], tern[2][:, neg, i ^ k, :, :])
            last.then_inc(spread, 1)

        @block.gpsimd
        def _(pool):
            pool.memset(ones[:], 1.0).then_inc(ones_done, 1)
            pool.wait_ge(neg_done, 2)
            for i in range(0, OC, 2):
                spread_in(pool.tensor_copy, 1, m_up, i)

        @block.vector
        def _(dve):
            dve.wait_ge(w_in, 16 * 5)
            for i in range(3):
                n = shapes[i][0]
                dve.tensor_reduce(sums[0:n, i:i + 1], w[i][:], AX.XYZ if i == 2 else AX.XY, ALU.add,
                                  apply_absolute_value=True).then_inc(sum_done, 1)
            dve.wait_ge(total_ready, 1)
            dve.tensor_scalar(scales[:], total[:], 1.0 / COUNT, None, ALU.mult)
            dve.tensor_scalar(half[:], total[:], 0.5 / COUNT, None, ALU.mult).then_inc(half_done, 1)
            dve.tensor_scalar(mhalf[:], total[:], -0.5 / COUNT, None, ALU.mult).then_inc(mhalf_done, 1)
            dve.wait_ge(half_done, 1)
            dve.wait_ge(mhalf_done, 1)
            for i in range(3):
                n = shapes[i][0]
                flat = "p a b -> p (a b)" if i < 2 else "p a b c -> p (a b c)"
                wf, lf = w[i][:].rearrange(flat), low[i][:].rearrange(flat)
                dve.tensor_scalar(lf, wf, mhalf[0:n, i:i + 1], None, ALU.is_lt).then_inc(low_done, 1)
                dve.wait_ge(low_done, i + 1)
                dve.scalar_tensor_tensor(out=tern[i][:, 0].rearrange(flat), in0=wf, scalar=half[0:n, i:i + 1], in1=lf,
                                         op0=ALU.is_gt, op1=ALU.subtract).then_inc(pos_done, 1)
            dve.wait_ge(neg_done, 1)
            for i in range(0, OC, 2):
                spread_in(dve.tensor_copy, 0, m_gate, i)
            dve.wait_ge(neg_done, 3)
            for i in range(0, OC, 2):
                spread_down(dve.tensor_copy, i)

        @block.scalar
        def _(act):
            def copy(out, in_):
                return act.activation(out, in_.bitcast(F32), ACT.Copy)

            for i in range(3):
                act.wait_ge(pos_done, i + 1)
                act.activation(tern[i][:, 1], tern[i][:, 0].bitcast(F32), ACT.Copy, scale=-1.0).then_inc(neg_done, 1)
            act.wait_ge(neg_done, 3)
            for i in range(1, OC, 2):
                spread_in(copy, 0, m_gate, i)
            for i in range(1, OC, 2):
                spread_in(copy, 1, m_up, i)
            for i in range(1, OC, 2):
                spread_down(copy, i)


def stage_octonion(c, m_gate, m_up, m_down, scales, xT_hi, xT_lo):
    nc = c.nc
    n = 2 * OC
    with ExitStack() as st:
        sb, ps, sem = tiles(st, nc)
        g = sb("oc_g", [OHALF, 2, TOK])
        h = sb("oc_h", [OHALF, 2, TOK])
        hT_hi = sb("oc_hT_hi", [OHALF, n, TOK], F32R)
        hT_lo = sb("oc_hT_lo", [OHALF, n, TOK], F32R)
        gu = [ps(f"oc_gu{i}", [OHALF, 2 * TOK]) for i in range(2)]
        out = [ps(f"oc_out{t}", [P, D]) for t in range(TT)]
        gu_ready, g_done, h_done, hi_done, lo_done, out_ready, sum_done = (
            sem(f"oc_{x}") for x in ("gu_ready", "g_done", "h_done", "hi_done", "lo_done", "out_ready", "sum_done"))
        norm = LayerNorm(c, st, "oc", xT_hi, xT_lo)
        block = st.enter_context(nc.Block())

        @block.tensor
        def _(pe):
            norm.tensor(pe)
            pe.wait_ge(norm.done, TT)
            for f in range(n):
                comp, hh = f // 2, f % 2
                if f >= 2:
                    pe.wait_ge(h_done, f - 1)
                for u, m in enumerate((m_gate, m_up)):
                    for k in range(DC):
                        w = m[:, k, comp, hh * OHALF:(hh + 1) * OHALF]
                        dst = gu[f % 2][:, u * TOK:(u + 1) * TOK]
                        pe.matmul(dst, w, xT_hi[:, k, :], start=k == 0, stop=False)
                        last = pe.matmul(dst, w, xT_lo[:, k, :], start=False, stop=k == DC - 1)
                last.then_inc(gu_ready, 1)
            for f in range(n):
                comp, hh = f // 2, f % 2
                pe.wait_ge(lo_done, f + 1)
                for t in range(TT):
                    toks = slice(t * P, (t + 1) * P)
                    w = m_down[:, hh, comp, :]
                    pe.matmul(out[t][:], hT_hi[:, f, toks], w, start=f == 0, stop=False)
                    last = pe.matmul(out[t][:], hT_lo[:, f, toks], w, start=False, stop=f == n - 1)
            last.then_inc(out_ready, 1)

        @block.scalar
        def _(act):
            norm.scalar(act)
            for f in range(n + 1):
                if f < n:
                    act.wait_ge(gu_ready, f + 1)
                    if f >= 2:
                        act.wait_ge(h_done, f - 1)
                    act.activation(g[:, f % 2], gu[f % 2][:, 0:TOK], ACT.Silu,
                                   scale=scales[0:OHALF, 0:1]).then_inc(g_done, 1)
                if f:
                    act.wait_ge(h_done, f)
                    act.activation(hT_hi[:, f - 1], h[:, (f - 1) % 2], ACT.Copy).then_inc(hi_done, 1)

        @block.gpsimd
        def _(pool):
            norm.gpsimd(pool)
            for f in range(n):
                pool.wait_ge(hi_done, f + 1)
                pool.tensor_tensor(hT_lo[:, f], h[:, f % 2], hT_hi[:, f].bitcast(F32), ALU.subtract).then_inc(lo_done, 1)

        @block.vector
        def _(dve):
            norm.vector(dve)
            for f in range(n):
                b = f % 2
                dve.wait_ge(g_done, f + 1)
                if f >= 2:
                    dve.wait_ge(lo_done, f - 1)
                dve.scalar_tensor_tensor(out=h[:, b], in0=gu[b][:, TOK:], scalar=scales[0:OHALF, 1:2], in1=g[:, b],
                                         op0=ALU.mult, op1=ALU.mult).then_inc(h_done, 1)
            dve.wait_ge(out_ready, 1)
            for t in range(TT):
                dve.scalar_tensor_tensor(out=c.x[:, t, :], in0=out[t][:], scalar=scales[:, 2:3], in1=c.x[:, t, :],
                                         op0=ALU.mult, op1=ALU.add).then_inc(sum_done, 1)
            dve.wait_ge(sum_done, TT)


def build(nc, t, out, stop=99):
    c = Ctx()
    c.nc = nc
    with ExitStack() as st:
        sb, ps, sem = tiles(st, nc)
        c.x = sb("x_res", [P, TT, D])
        c.ident = sb("ident", [P, P])
        c.minus_half = sb("minus_half", [P, 8])
        q_dram = nc.dram_tensor("q_scratch", (B, P, KVH, GRP * Q), F32).ap()
        o_dram = nc.dram_tensor("o_scratch", (B, P, KVH, GRP * Q), F32).ap()
        klat_dram = nc.dram_tensor("klat_scratch", (B, P, KVH, Q), F32).ap()
        vlat_dram = nc.dram_tensor("vlat_scratch", (B, Q, KVH * HD), F32).ap()
        stage_constants(c, t["x"])

        def cross(layer, eps, mask):
            tag = f"x{layer}"
            lat = layer == 1
            with ExitStack() as s2:
                sb, _, _ = tiles(s2, nc)
                w_hi = sb(f"{tag}_w_hi", [P, DC, KVCOLS], F32R)
                w_lo = sb(f"{tag}_w_lo", [P, DC, KVCOLS], F32R)
                chunks = context_chunks(nc, s2, tag)
                with ExitStack() as s3:
                    sb, _, _ = tiles(s3, nc)
                    xT_hi = sb(f"{tag}_xT_hi", [P, DC, TOK], F32R)
                    xT_lo = sb(f"{tag}_xT_lo", [P, DC, TOK], F32R)
                    stage_queries(c, f"{tag}_q", chunks, t["ctxT"], t[f"wq{layer}"], t[f"wkv{layer}"], (t[f"qn{layer}"], t[f"kn{layer}"]),
                                  eps, xT_hi, xT_lo, w_hi, w_lo, q_dram, klat_dram if lat else None,
                                  vlat_dram if lat else None)
                stage_context(c, f"{tag}_c", chunks, t["ctxT"], mask, eps, w_hi, w_lo, q_dram, klat_dram if lat else None,
                              vlat_dram if lat else None, o_dram)
            stage_accumulate(c, f"{tag}_o", t[f"wo{layer}"], [P] * (KVH * GRP), o_dram=o_dram)

        if stop in (1, 99):
            with own_semaphores(nc):
                cross(0, 1e-5, t["mask"])

        if stop in (2, 99):
            with own_semaphores(nc), ExitStack() as s2:
                sb, _, _ = tiles(s2, nc)
                aT_hi, aT_lo = sb("aT_hi", [P, SREP, TOK], F32R), sb("aT_lo", [P, SREP, TOK], F32R)
                with ExitStack() as s3:
                    sb, _, _ = tiles(s3, nc)
                    xT_hi, xT_lo = sb("sa_xT_hi", [P, DC, TOK], F32R), sb("sa_xT_lo", [P, DC, TOK], F32R)
                    stage_self_attention(c, t["sa_wq"], t["sa_wkv"], xT_hi, xT_lo, aT_hi, aT_lo)
                stage_accumulate(c, "sa_out", t["sa_wo"], [P] * SREP, aT_hi, aT_lo)

        if stop in (3, 99):
            with own_semaphores(nc), ExitStack() as s2:
                sb, _, _ = tiles(s2, nc)
                F = FFN
                nf = (F + P - 1) // P
                hT_hi, hT_lo = sb("ffn_hT_hi", [P, nf, TOK], F32R), sb("ffn_hT_lo", [P, nf, TOK], F32R)
                with ExitStack() as s3:
                    sb, _, _ = tiles(s3, nc)
                    xT_hi, xT_lo = sb("ffn_xT_hi", [P, DC, TOK], F32R), sb("ffn_xT_lo", [P, DC, TOK], F32R)
                    stage_ffn(c, "ffn", t["ffn_wg"], t["ffn_wu"], F, xT_hi, xT_lo, hT_hi, hT_lo)
                stage_accumulate(c, "ffn_out", t["ffn_wd"], [min(P, F - P * f) for f in range(nf)], hT_hi, hT_lo)

        if stop in (4, 99):
            with own_semaphores(nc):
                cross(1, 1e-6, None)

        if stop in (5, 99):
            with own_semaphores(nc), ExitStack() as s2:
                sb, _, sem = tiles(s2, nc)
                u, sg = sb("m_u", [P, MC, TOK]), sb("m_sg", [P, MC, TOK])
                conv_w, conv_b, dt_bias = sb("m_conv_w", [P, MC, MK]), sb("m_conv_b", [P, MC]), sb("m_dt_bias", [P, MC])
                A, Dp = sb("m_A", [P, MC, MN]), sb("m_Dp", [P, MC])
                with ExitStack() as s3:
                    sb3, _, sem3 = tiles(s3, nc)
                    xT_hi, xT_lo = sb3("mi_xT_hi", [P, DC, TOK], F32R), sb3("mi_xT_lo", [P, DC, TOK], F32R)
                    per_channel = sem3("m_per_channel")
                    with nc.Block() as block:
                        @block.sync
                        def _(sp):
                            for dst, src in ((conv_w, "conv_w"), (conv_b, "conv_b"), (dt_bias, "dt_bias"), (A, "A"),
                                             (Dp, "Dp")):
                                sp.dma_start(dst[:], t[src]).then_inc(per_channel, 16)
                            sp.wait_ge(per_channel, 16 * 5)
                    stage_scan_inputs(c, t["win"], conv_w, conv_b, xT_hi, xT_lo, u, sg)
                yT_hi, yT_lo = sb("m_yT_hi", [P, MC, TOK], F32R), sb("m_yT_lo", [P, MC, TOK], F32R)
                with ExitStack() as s3:
                    sb3, _, _ = tiles(s3, nc)
                    delta, du = sb3("m_delta", [P, MC, TOK]), sb3("m_du", [P, MC, TOK])
                    bc = sb3("m_bc", [P, 2 * MN, TOK])
                    bc_dram = nc.dram_tensor("bc_scratch", (2 * MN, TOK), F32).ap()
                    stage_scan_params(c, t["wx"], t["wdt"], dt_bias, t["scan_lnw"], bc_dram, u, delta, du, bc)
                    stage_scan(c, A, Dp, u, sg, delta, du, bc, yT_hi, yT_lo)
                stage_accumulate(c, "m_out", t["wout"], [P] * MC, yT_hi, yT_lo)

        if stop in (6, 99):
            with own_semaphores(nc), ExitStack() as s2:
                sb, _, _ = tiles(s2, nc)
                m_gate, m_up = (sb(f"o_m_{n}", [P, OC // 2, OC, OHID], F32R) for n in ("gate", "up"))
                m_down = sb("o_m_down", [OHALF, 2, OC, D], F32R)
                scales = sb("o_scales", [P, 3])
                stage_ternary(c, (t["og"], t["ou"], t["od"]), m_gate, m_up, m_down, scales)
                xT_hi, xT_lo = sb("o_xT_hi", [P, DC, TOK], F32R), sb("o_xT_lo", [P, DC, TOK], F32R)
                stage_octonion(c, m_gate, m_up, m_down, scales, xT_hi, xT_lo)
        with ExitStack() as s2:
            _, _, sem = tiles(s2, nc)
            out_done = sem("out_done")
            block = s2.enter_context(nc.Block())

            @block.sync
            def _(sp):
                sp.dma_start(out.rearrange("(t p) d -> p t d", p=P), c.x[:]).then_inc(out_done, 16)
                sp.wait_ge(out_done, 16)


def lay_out(i):
    f = lambda a: np.ascontiguousarray(np.asarray(a))

    def groups(w, cols=COLS):
        k, n = w.shape
        return f(w.reshape(k // P, P, n // cols, cols).transpose(2, 1, 0, 3))

    def rows(w):
        n, d = w.shape
        g = -(-n // (DC * P))
        full = np.zeros((g * DC * P, d), w.dtype)
        full[:n] = w
        return f(full.reshape(g, DC, P, d).transpose(0, 2, 1, 3))

    a = {}
    a["x"] = f(i["x"]).reshape(TOK, D)
    ctx = np.asarray(i["ctx_4096"])
    a["ctxT"] = f(ctx.reshape(B * CHUNKS, P, DC, P).transpose(0, 3, 2, 1))
    a["mask"] = f(i["mask_1x1xSxS2_ff0"]).reshape(Q, KEYS)
    n = lambda k: np.asarray(i[k])
    a["wq0"], a["wq1"] = groups(n("L0_xattn_Wq").T), groups(n("L1_xattn_Wq"))
    a["wkv0"] = np.concatenate([groups(n("L0_xattn_Wk").T), groups(n("L0_xattn_Wv").T)])
    a["wkv1"] = np.concatenate([groups(n("L1_xattn_Wk")), groups(n("L1_xattn_Wv"))])
    a["wo0"], a["wo1"] = rows(n("L0_xattn_Wo").T), rows(n("L1_xattn_Wo"))
    for layer in (0, 1):
        a[f"qn{layer}"], a[f"kn{layer}"] = f(n(f"L{layer}_xattn_q_norm_w")), f(n(f"L{layer}_xattn_k_norm_w"))

    def by_group(w, axis):
        w = np.moveaxis(w, axis, 0)
        w = w.reshape(NKV, SREP, SHD, -1).transpose(1, 0, 2, 3).reshape(D, -1)
        return np.moveaxis(w, 0, axis)

    a["sa_wq"] = groups(by_group(n("L0_attn_wq"), 1))[0]
    a["sa_wkv"] = groups(np.concatenate([n("L0_attn_wk"), n("L0_attn_wv")], 1), 2 * NKV * SHD)[0]
    a["sa_wo"] = rows(by_group(n("L0_attn_wo"), 0))

    def padded(w):
        full = np.zeros((D, -(-w.shape[1] // COLS) * COLS), w.dtype)
        full[:, :w.shape[1]] = w
        return groups(full)

    a["ffn_wg"], a["ffn_wu"] = padded(n("L0_ffn_W_gate").T), padded(n("L0_ffn_W_up").T)
    a["ffn_wd"] = rows(n("L0_ffn_W_down").T)

    def channels(w):
        return f(np.moveaxis(w.reshape(MC, P, *w.shape[1:]), 0, 1))

    a["win"] = groups(n("L1_attn_W_in").T)
    a["conv_w"], a["conv_b"] = channels(n("L1_attn_conv_w")), channels(n("L1_attn_conv_b"))
    a["dt_bias"], a["A"], a["Dp"] = (channels(n(f"L1_attn_{k}")) for k in ("dt_bias", "A", "D_param"))
    a["wx"], a["wdt"] = channels(n("L1_attn_Wx").T), f(n("L1_attn_Wdt").T)
    a["scan_lnw"] = np.concatenate([n("L1_attn_dt_ln_w"), n("L1_attn_b_ln_w"), n("L1_attn_c_ln_w")])
    a["wout"] = rows(n("L1_attn_W_out").T)
    a["og"], a["ou"] = (f(n(f"L1_ffn_w_{k}").transpose(2, 0, 1)) for k in ("gate", "up"))
    a["od"] = f(n("L1_ffn_w_down").reshape(OC, OIN, 2, OHALF).transpose(3, 0, 2, 1))
    return a


def kernel(**inputs):
    import concourse.bacc as bacc
    from concourse.bass_utils import run_bass_kernel_spmd

    nc = bacc.Bacc("TRN2", target_bir_lowering=False, num_devices=1)
    arrays = lay_out(inputs)
    tensors = {k: nc.dram_tensor(k, a.shape, mybir.dt.from_np(a.dtype), kind="ExternalInput").ap()
               for k, a in arrays.items()}
    out = nc.dram_tensor("out", (TOK, D), F32, kind="ExternalOutput").ap()
    build(nc, tensors, out)
    got = run_bass_kernel_spmd(nc, [arrays], core_ids=[0]).results[0]["out"]
    return got.reshape(B, Q, D)
```

```python
from contextlib import ExitStack, contextmanager

import numpy as np
import concourse.bass as bass
from concourse import mybir

F32 = mybir.dt.float32
F32R = mybir.dt.float32r
ALU = mybir.AluOpType
ACT = mybir.ActivationFunctionType
AX = mybir.AxisListType

P = 128
B, Q, D = 8, 32, 512
KEYS = 512
TOK = B * Q
TT = TOK // P
BT = P // Q
DC = D // P
KVH, GRP, HD = 8, 4, 128
COLS = 512
KVCOLS = 2 * KVH * HD
FFN = 1376
CHUNKS = KEYS // P


class Ctx:
    pass


def tiles(stack, nc):
    def sb(name, shape, dt=F32):
        return stack.enter_context(nc.sbuf_tensor(name, shape, dt))

    def ps(name, shape):
        return stack.enter_context(nc.psum_tensor(name, shape, F32))

    def sem(name):
        return nc.alloc_semaphore(name)

    return sb, ps, sem


@contextmanager
def own_semaphores(nc):
    before = nc.snapshot_sems()
    yield
    nc.clear_and_free_semaphores(nc.allocated_since(before))
    nc.all_engine_barrier()


def split_matmul(pe, out, a_hi, a_lo, b_hi, b_lo, first, last):
    pe.matmul(out, a_hi, b_hi, start=first, stop=False)
    pe.matmul(out, a_hi, b_lo, start=False, stop=False)
    return pe.matmul(out, a_lo, b_hi, start=False, stop=last)


class FirstWeights:

    def __init__(self, c, st, tag, src, raw, hi, lo, hi_done, lo_done):
        _, _, sem = tiles(st, c.nc)
        self.src, self.raw, self.hi, self.lo = src, raw, hi, lo
        self.here = [sem(f"{tag}_first_in{k}") for k in range(DC)]
        self.hi_done, self.lo_done = sem(f"{tag}_first_hi"), sem(f"{tag}_first_lo")
        self.all_hi, self.all_lo = hi_done, lo_done

    def sync(self, sp):
        for k in range(DC):
            sp.dma_start(self.raw[:, k], self.src[:, k]).then_inc(self.here[k], 16)

    def scalar(self, act, k):
        act.wait_ge(self.here[k], 16)
        act.activation(self.hi[:, k], self.raw[:, k], ACT.Copy).then_inc(
            self.hi_done if k < DC - 1 else self.all_hi, 1)

    def vector(self, dve, k):
        if k < DC - 1:
            dve.wait_ge(self.hi_done, k + 1)
        else:
            dve.wait_ge(self.all_hi, 1)
        dve.tensor_tensor(self.lo[:, k], self.raw[:, k], self.hi[:, k].bitcast(F32), ALU.subtract).then_inc(
            self.lo_done if k < DC - 1 else self.all_lo, 1)

    def wait(self, pe, k):
        if k < DC - 1:
            pe.wait_ge(self.lo_done, k + 1)
        else:
            pe.wait_ge(self.all_lo, 1)


def stage_constants(c, x_dram):
    nc = c.nc
    with ExitStack() as st:
        sb, ps, sem = tiles(st, nc)
        x_in, ident0, ident1 = sem("x_in"), sem("ident0"), sem("ident1")
        block = st.enter_context(nc.Block())

        @block.sync
        def _(sp):
            sp.dma_start(c.x[:], x_dram.rearrange("(t p) d -> p t d", p=P)).then_inc(x_in, 16)
            sp.wait_ge(x_in, 16)

        @block.gpsimd
        def _(pool):
            pool.memset(c.ident[:], 0.0).then_inc(ident0, 1)
            pool.memset(c.minus_half[:], -0.5)
            pool.wait_ge(ident0, 1)
            pool.affine_select(out=c.ident[:], in_=c.ident[:], compare_op=ALU.not_equal, fill=1.0,
                               base=0, pattern=[[-1, P]], channel_multiplier=1).then_inc(ident1, 1)
            pool.wait_ge(ident1, 1)


class LayerNorm:

    def __init__(self, c, st, tag, xT_hi, xT_lo, banks=None):
        sb, ps, sem = tiles(st, c.nc)
        self.c, self.xT_hi, self.xT_lo = c, xT_hi, xT_lo
        self.stats = sb(f"{tag}_ln_stats", [P, TT, 6])
        self.mv = sb(f"{tag}_ln_mv", [P, TT, 2])
        self.var = sb(f"{tag}_ln_var", [P, TT])
        self.rstd = sb(f"{tag}_ln_rstd", [P, TT])
        self.xn = sb(f"{tag}_ln_xn", [P, TT, D])
        self.xT_ps = banks or [ps(f"{tag}_ln_xT_ps{t}", [P, DC * P]) for t in range(TT)]
        (self.stats_done, self.mv_done, self.var_done, self.rstd_done, self.xn_done, self.xT_ready, self.hi_done,
         self.done) = (sem(f"{tag}_ln_{n}") for n in ("stats_done", "mv_done", "var_done", "rstd_done", "xn_done",
                                                      "xT_ready", "hi_done", "done"))

    def vector(self, dve):
        c = self.c
        for t in range(TT):
            dve.bn_stats(self.stats[:, t, :], c.x[:, t, :]).then_inc(self.stats_done, 1)
        for t in range(TT):
            dve.wait_ge(self.stats_done, t + 1)
            dve.bn_aggr(self.mv[:, t, :], self.stats[:, t, :]).then_inc(self.mv_done, 1)
        dve.wait_ge(self.mv_done, TT)
        dve.tensor_scalar(self.var[:], self.mv[:, :, 1], 1e-5, None, ALU.add).then_inc(self.var_done, 1)
        for t in range(TT):
            dve.wait_ge(self.rstd_done, 1)
            dve.tensor_scalar(self.xn[:, t, :], c.x[:, t, :], self.mv[:, t, 0:1], self.rstd[:, t:t + 1],
                              ALU.subtract, ALU.mult).then_inc(self.xn_done, 1)

    def vector_lo(self, dve, t):
        dve.wait_ge(self.hi_done, t + 1)
        toks = slice(t * P, (t + 1) * P)
        dve.tensor_tensor(self.xT_lo[:, :, toks], self.xT_ps[t][:, 0:DC * P].rearrange("p (c n) -> p c n", c=DC),
                          self.xT_hi[:, :, toks].bitcast(F32), ALU.subtract).then_inc(self.done, 1)

    def gpsimd(self, pool):
        pool.wait_ge(self.var_done, 1)
        pool.tensor_tensor(self.rstd[:], self.var[:], self.c.minus_half[:, 0:TT], ALU.pow).then_inc(self.rstd_done, 1)

    def tensor(self, pe):
        for t in range(TT):
            pe.wait_ge(self.xn_done, t + 1)
            for k in range(DC):
                cols = slice(k * P, (k + 1) * P)
                last = pe.transpose(self.xT_ps[t][:, cols], self.xn[:, t, cols], self.c.ident[:])
            last.then_inc(self.xT_ready, 1)

    def scalar(self, act, t):
        act.wait_ge(self.xT_ready, t + 1)
        act.activation(self.xT_hi[:, :, t * P:(t + 1) * P], self.xT_ps[t][:, 0:DC * P].rearrange("p (c n) -> p c n", c=DC),
                       ACT.Copy).then_inc(self.hi_done, 1)


assert DC == 4 and TT == 2


def first_halves_scalar(act, norm, first):
    first.scalar(act, 0)
    first.scalar(act, 1)
    norm.scalar(act, 0)
    first.scalar(act, 2)
    norm.scalar(act, 1)
    first.scalar(act, 3)


def first_halves_vector(dve, norm, first):
    norm.vector(dve)
    first.vector(dve, 0)
    first.vector(dve, 1)
    norm.vector_lo(dve, 0)
    first.vector(dve, 2)
    norm.vector_lo(dve, 1)
    first.vector(dve, 3)


def stage_queries(c, tag, chunks, ocur, stored, ctxT_dram, wq_dram, wkv_dram, norm_w_dram, eps, xT_hi, xT_lo, w_hi, w_lo,
                  q_dram, klat_dram, vlat_dram):
    nc = c.nc
    with_latents = klat_dram is not None
    q_groups = KVH
    kv_groups = KVCOLS // COLS
    order = [("q", 0)]
    for g in range(1, q_groups):
        order.append(("q", g))
        if g % 2 == 0 or g == q_groups - 1:
            order.append(("kv", g // 2 - 1 if g % 2 == 0 else kv_groups - 1))
    groups = len(order)
    assert groups == q_groups + kv_groups and order[-1][0] == "kv"
    place = {name: at for at, name in enumerate(order)}
    LAG = 2
    RAW, WQ, NP = 4, 3, 4
    ct_raw, ct_hi, ct_lo, ct_in, ct_hi_done, ct_lo_done = chunks
    items = [("q", g, t) for g in range(q_groups) for t in range(TT)]
    if with_latents:
        items += [("k", g, t) for g in range(kv_groups // 2) for t in range(TT)]
        items += [("v", g, t) for g in range(kv_groups // 2, kv_groups) for t in range(TT)]
    n_norm = sum(kind != "v" for kind, _, _ in items)

    with ExitStack() as st:
        sb, ps, sem = tiles(st, nc)
        raw = sb(f"{tag}_raw", [P, RAW, DC, COLS])
        wq_hi = sb(f"{tag}_wq_hi", [P, WQ, DC, COLS], F32R)
        wq_lo = sb(f"{tag}_wq_lo", [P, WQ, DC, COLS], F32R)
        sq = sb(f"{tag}_sq", [P, COLS])
        ss = sb(f"{tag}_ss", [P, 2, GRP])
        ms = sb(f"{tag}_ms", [P, 2, GRP])
        rr = sb(f"{tag}_rr", [P, 2, GRP])
        nrm = sb(f"{tag}_nrm", [P, 2, COLS])
        stg = ocur[:].rearrange("p s j r -> p s (j r)")[:, :, 0:COLS]
        nw = sb(f"{tag}_nw", [P, 2])
        qkw = sb(f"{tag}_qkw", [P, 1])
        proj = [ps(f"{tag}_proj{i}", [P, COLS]) for i in range(NP)]
        turn = [ps(f"{tag}_turn{i}", [P, COLS]) for i in range(2)]
        raw_in = [sem(f"{tag}_raw_in{i}") for i in range(RAW)]
        nw_in, qkw_done = sem(f"{tag}_nw_in"), sem(f"{tag}_qkw_done")
        w_hi_done, w_lo_done = sem(f"{tag}_w_hi_done"), sem(f"{tag}_w_lo_done")
        proj_ready, sq_done, ss_done, ms_done, rr_done, nrm_done, turn_ready, stg_done = (
            sem(f"{tag}_{n}") for n in ("proj_ready", "sq_done", "ss_done", "ms_done", "rr_done", "nrm_done",
                                        "turn_ready", "stg_done"))
        norm = LayerNorm(c, st, tag, xT_hi, xT_lo)
        first = FirstWeights(c, st, tag, wq_dram[0], raw[:, 0], wq_hi[:, 0], wq_lo[:, 0], w_hi_done, w_lo_done)
        block = st.enter_context(nc.Block())

        def weights(kind, g):
            if kind == "q":
                return wq_hi[:, g % WQ], wq_lo[:, g % WQ]
            return w_hi[:, :, g * COLS:(g + 1) * COLS], w_lo[:, :, g * COLS:(g + 1) * COLS]

        def split_by(i):
            return min(groups, i + 1)

        assert all(split_by(TT * g - 1) > place["q", g] for g in range(1, q_groups))
        assert split_by(TT * q_groups - 1) == groups

        @block.sync
        def _(sp):
            first.sync(sp)
            for i, w in enumerate(norm_w_dram):
                sp.dma_start(nw[:, i:i + 1], w.rearrange("(p o) -> p o", o=1)).then_inc(nw_in, 16)

            def load(at):
                kind, g = order[at]
                if at >= RAW:
                    sp.wait_ge(w_lo_done, at - RAW + 1)
                src = wq_dram[g] if kind == "q" else wkv_dram[g]
                sp.dma_start(raw[:, at % RAW], src).then_inc(raw_in[at % RAW], 16)

            for at in range(1, RAW):
                load(at)
            loaded = RAW
            for n in range(2):
                sp.dma_start(ct_raw[:, n], ctxT_dram[n]).then_inc(ct_in[n], 16)
            for i, (kind, g, t) in enumerate(items):
                while loaded < min(groups, split_by(i) + RAW):
                    load(loaded)
                    loaded += 1
                sp.wait_ge(stg_done, i + 1)
                src = stg[:, i % 2, :]
                if kind == "v":
                    cols = slice((g - kv_groups // 2) * COLS, (g - kv_groups // 2 + 1) * COLS)
                    dst = vlat_dram.rearrange("b q n -> (b q) n")[t * P:(t + 1) * P, cols]
                elif kind == "q":
                    dst = q_dram[t * BT:(t + 1) * BT, :, g, :].rearrange("b p n -> p b n")
                    src = src.rearrange("p (b n) -> p b n", b=BT)
                else:
                    dst = klat_dram[t * BT:(t + 1) * BT, :, g * GRP:(g + 1) * GRP, :].rearrange("b p g n -> p b (g n)")
                    src = src.rearrange("p (b n) -> p b n", b=BT)
                sp.dma_start(dst, src).then_inc(stored[i % 2], 16)

        @block.scalar
        def _(act):
            first_halves_scalar(act, norm, first)

            def make_hi(at):
                kind, g = order[at]
                act.wait_ge(raw_in[at % RAW], 16 * (at // RAW + (at % RAW > 0)))
                if kind == "q" and g >= WQ:
                    act.wait_ge(proj_ready, TT * (g - WQ + 1))
                act.activation(weights(kind, g)[0], raw[:, at % RAW], ACT.Copy).then_inc(w_hi_done, 1)

            def square(i):
                act.wait_ge(proj_ready, i + 1)
                if i:
                    act.wait_ge(ss_done, i)
                act.activation(sq[:], proj[i % NP][:], ACT.Square).then_inc(sq_done, 1)

            def turned(i):
                kind, g, t = items[i]
                if i >= 2:
                    act.wait_ge(stored[i % 2], 16 * (i // 2))
                if kind == "v":
                    act.wait_ge(proj_ready, i + 1)
                    act.activation(stg[:, i % 2, :], proj[i % NP][:], ACT.Copy).then_inc(stg_done, 1)
                    return
                act.wait_ge(turn_ready, i + 1)
                out = stg[:, i % 2, :].rearrange("p (b g n) -> p g b n", b=BT, g=GRP)
                src = turn[i % 2][:].rearrange("p (g b n) -> p g b n", b=BT, g=GRP)
                if kind == "q":
                    if i == 0:
                        act.wait_ge(qkw_done, 1)
                    act.activation(out, src, ACT.Copy, scale=qkw[:, 0:1]).then_inc(stg_done, 1)
                else:
                    act.activation(out, src, ACT.Copy).then_inc(stg_done, 1)

            make_hi(1)
            made = 2
            for i in range(n_norm):
                while made < split_by(i):
                    make_hi(made)
                    made += 1
                if i == 4:
                    act.wait_ge(ct_in[0], 16)
                    act.activation(ct_hi[:, 0], ct_raw[:, 0], ACT.Copy).then_inc(ct_hi_done, 1)
                square(i)
                if i >= LAG:
                    turned(i - LAG)
            for i in range(n_norm - LAG, len(items)):
                turned(i)

        @block.vector
        def _(dve):
            first_halves_vector(dve, norm, first)
            dve.wait_ge(nw_in, 32)
            dve.tensor_scalar(qkw[:], nw[:, 0:1], nw[:, 1:2], float(HD) ** -0.5, ALU.mult,
                              ALU.mult).then_inc(qkw_done, 1)

            def make_lo(at):
                kind, g = order[at]
                hi, lo = weights(kind, g)
                dve.wait_ge(w_hi_done, at + 1)
                dve.tensor_tensor(lo, raw[:, at % RAW], hi.bitcast(F32), ALU.subtract).then_inc(w_lo_done, 1)

            make_lo(1)
            made = 2
            for i in range(n_norm):
                dve.wait_ge(sq_done, i + 1)
                dve.tensor_reduce(ss[:, i % 2, :], sq[:].rearrange("p (g n) -> p g n", g=GRP), AX.X,
                                  ALU.add).then_inc(ss_done, 1)
                while made < split_by(i):
                    make_lo(made)
                    made += 1
                dve.wait_ge(rr_done, i + 1)
                if i >= 2:
                    dve.wait_ge(turn_ready, i - 1)
                dve.tensor_tensor(nrm[:, i % 2, :].rearrange("p (g n) -> p g n", g=GRP),
                                  proj[i % NP][:].rearrange("p (g n) -> p g n", g=GRP),
                                  rr[:, i % 2, :].unsqueeze(2).to_broadcast([P, GRP, HD]),
                                  ALU.mult).then_inc(nrm_done, 1)

        @block.gpsimd
        def _(pool):
            norm.gpsimd(pool)
            for i in range(n_norm):
                pool.wait_ge(ss_done, i + 1)
                pool.tensor_scalar(ms[:, i % 2, :], ss[:, i % 2, :], 1.0 / HD, eps, ALU.mult,
                                   ALU.add).then_inc(ms_done, 1)
                pool.wait_ge(ms_done, i + 1)
                if i >= 2:
                    pool.wait_ge(nrm_done, i - 1)
                pool.tensor_tensor(rr[:, i % 2, :], ms[:, i % 2, :], c.minus_half[:, 0:GRP],
                                   ALU.pow).then_inc(rr_done, 1)
                if i == 5:
                    pool.wait_ge(ct_hi_done, 1)
                    pool.tensor_tensor(ct_lo[:, 0], ct_raw[:, 0], ct_hi[:, 0].bitcast(F32),
                                       ALU.subtract).then_inc(ct_lo_done, 1)

        @block.tensor
        def _(pe):
            norm.tensor(pe)
            def turn_rows(m):
                pe.wait_ge(nrm_done, m + 1)
                if m >= 2:
                    pe.wait_ge(stg_done, m - 1)
                for g in range(GRP):
                    last = pe.transpose(turn[m % 2][:, g * P:(g + 1) * P], nrm[:, m % 2, g * P:(g + 1) * P],
                                        c.ident[:])
                last.then_inc(turn_ready, 1)

            for i, (kind, g, t) in enumerate(items):
                name = ("q" if kind == "q" else "kv", g)
                if i < TT:
                    pe.wait_ge(norm.done, i + 1)
                if i:
                    pe.wait_ge(w_lo_done, place[name] + 1)
                if i >= NP:
                    if i - NP < n_norm:
                        pe.wait_ge(nrm_done, i - NP + 1)
                    else:
                        pe.wait_ge(stg_done, i - NP + 1)
                hi, lo = weights(*name)
                for k in range(DC):
                    if i == 0:
                        first.wait(pe, k)
                    toks = slice(t * P, (t + 1) * P)
                    last = split_matmul(pe, proj[i % NP][:], xT_hi[:, k, toks], xT_lo[:, k, toks], hi[:, k], lo[:, k],
                                        k == 0, k == DC - 1)
                last.then_inc(proj_ready, 1)
                if LAG <= i < n_norm + LAG:
                    turn_rows(i - LAG)
            for m in range(len(items) - LAG, n_norm):
                turn_rows(m)


def context_chunks(nc, st, tag):
    sb, _, sem = tiles(st, nc)
    return (sb(f"{tag}_ct_raw", [P, 2, DC, P]), sb(f"{tag}_ct_hi", [P, 2, DC, P], F32R),
            sb(f"{tag}_ct_lo", [P, 2, DC, P], F32R), [sem(f"{tag}_ct_in{i}") for i in range(2)],
            sem(f"{tag}_ct_hi_done"), sem(f"{tag}_ct_lo_done"))


def stage_context(c, tag, chunks, ocur, stored, proj, ctxT_dram, mask_dram, eps, w_hi, w_lo, q_dram, klat_dram, vlat_dram, o_dram):
    nc = c.nc
    with_latents = klat_dram is not None
    with_mask = mask_dram is not None
    NK = KEYS + (Q if with_latents else 0)
    ROWS = GRP * Q
    assert ROWS == P
    HPC = KVH // CHUNKS

    with ExitStack() as st:
        sb, ps, sem = tiles(st, nc)
        ct_raw, ct_hi, ct_lo, ct_in, ct_hi_done, ct_lo_done = chunks
        ksq = sb(f"{tag}_ksq", [P, COLS])
        kss = sb(f"{tag}_kss", [P, 2, GRP])
        kms = sb(f"{tag}_kms", [P, 2, GRP])
        krr = sb(f"{tag}_krr", [P, 2, GRP])
        khat = sb(f"{tag}_khat", [P, 2, COLS])
        kT = sb(f"{tag}_kT", [P, 2, KVH, KEYS])
        vv = sb(f"{tag}_vv", [P, 2, CHUNKS, KVH * HD])
        qcur = sb(f"{tag}_qcur", [P, 2, KVH, ROWS])
        k_hi, k_lo = sb(f"{tag}_k_hi", [P, KEYS], F32R), sb(f"{tag}_k_lo", [P, KEYS], F32R)
        q_hi, q_lo = sb(f"{tag}_q_hi", [P, ROWS], F32R), sb(f"{tag}_q_lo", [P, ROWS], F32R)
        pr = sb(f"{tag}_pr", [P, 2, NK])
        pT = sb(f"{tag}_pT", [P, 2, KEYS])
        nmax = sb(f"{tag}_nmax", [P, 2])
        den = sb(f"{tag}_den", [P, 2])
        rden = sb(f"{tag}_rden", [P, 2])
        if with_mask:
            mask = sb(f"{tag}_mask", [P, KEYS])
            sm = sb(f"{tag}_sm", [P, KEYS])
        if with_latents:
            klat = sb(f"{tag}_klat", [P, 2, KVH, Q])
            vlat = sb(f"{tag}_vlat", [Q, 2, KVH * HD])
            pTlat = sb(f"{tag}_pTlat", [Q, 2, P])
        kp = [ps(f"{tag}_kp{i}", [P, COLS]) for i in range(2)]
        vp = ps(f"{tag}_vp", [P, COLS])
        ktp = ps(f"{tag}_ktp", [P, COLS])
        scp = ps(f"{tag}_scp", [P, 2 * COLS])
        ptp = ps(f"{tag}_ptp", [P, KEYS])
        op = ps(f"{tag}_op", [P, COLS])
        q_in = [sem(f"{tag}_q_in{i}") for i in range(2)]
        o_out = proj.o_out
        m_in = sem(f"{tag}_m_in")
        (k_ready, v_ready, ksq_done, kss_done, kms_done, krr_done, khat_done, ktp_ready,
         kT_done, v_done, s_ready, sm_done, nmax_done, exp_done, rden_done, pn_done, ptp_ready, pT_done, o_ready,
         o_done, head_hi_done, head_lo_done) = (sem(f"{tag}_{n}") for n in (
             "k_ready", "v_ready", "ksq_done", "kss_done", "kms_done", "krr_done",
             "khat_done", "ktp_ready", "kT_done", "v_done", "s_ready", "sm_done", "nmax_done", "exp_done", "rden_done",
             "pn_done", "ptp_ready", "pT_done", "o_ready", "o_done", "head_hi_done", "head_lo_done"))
        block = st.enter_context(nc.Block())
        Q_LOADS = 3 if with_latents else 1
        Q_STORES = TT * (KVH + (KVCOLS // COLS if with_latents else 0))

        def over_batches(eng, run):
            run(0, 0)
            run(0, 1)
            with eng.Fori(1, B // 2) as pair:
                run(pair, 0)
                run(pair, 1)

        def wait(eng, semaphore, value):
            if not (isinstance(value, int) and value <= 0):
                eng.wait_ge(semaphore, value)

        lat_last = vp[0:Q, 0:P]

        def attends(pair, par):
            return not (isinstance(pair, int) and pair == par == 0)

        def chunk_no(pair, par, t):
            return pair * (2 * CHUNKS) + (par * CHUNKS + t)

        def head_no(pair, par, t):
            return pair * (2 * KVH) + (par * KVH + t * HPC - KVH)

        @block.sync
        def _(sp):
            if with_mask:
                for g in range(GRP):
                    sp.dma_start(mask[g * Q:(g + 1) * Q, :], mask_dram).then_inc(m_in, 16)

            def load_chunk(pair, par, t):
                n = chunk_no(pair, par, t)
                wait(sp, ct_lo_done, n - 1)
                sp.dma_start(ct_raw[:, t % 2], ctxT_dram[n]).then_inc(ct_in[t % 2], 16)

            def load_queries(pair, par):
                b = pair * 2 + par
                wait(sp, s_ready, (b - 1) * KVH)
                sp.dma_start(qcur[:, par], q_dram[b]).then_inc(q_in[par], 16)
                if with_latents:
                    wait(sp, o_ready, (b - 1) * KVH)
                    sp.dma_start(klat[:, par], klat_dram[b]).then_inc(q_in[par], 16)
                    sp.dma_start(vlat[:, par], vlat_dram[b]).then_inc(q_in[par], 16)

            def store(pair, par):
                b = pair * 2 + par
                sp.wait_ge(o_done, (b - 1) * KVH)
                sp.dma_start(o_dram[b - 2], ocur[:, par]).then_inc(o_out[par], 16)

            def run(pair, par):
                if attends(pair, par):
                    load_chunk(pair, par, 0)
                    load_chunk(pair, par, 1)
                else:
                    for i in range(2):
                        sp.wait_ge(stored[i], 16 * Q_STORES // 2)
                if not (isinstance(pair, int) and pair == 0):
                    store(pair, par)
                load_queries(pair, par)
                for t in range(2, CHUNKS):
                    load_chunk(pair, par, t)

            over_batches(sp, run)
            for g in range(proj.ahead):
                proj.load(sp, g)
            store(B // 2, 0)
            store(B // 2, 1)

        @block.scalar
        def _(act):
            def make_hi(pair, par, t):
                n = chunk_no(pair, par, t)
                act.wait_ge(ct_in[t % 2], pair * (16 * CHUNKS) + 16 * (par * CHUNKS // 2 + t // 2 + 1))
                wait(act, v_ready, (n - 1) * 2)
                act.activation(ct_hi[:, t % 2], ct_raw[:, t % 2], ACT.Copy).then_inc(ct_hi_done, 1)

            def square(n, j):
                act.wait_ge(k_ready, n * 2 + (j + 1))
                wait(act, kss_done, n * 2 + j)
                act.activation(ksq[:], kp[j][:], ACT.Square).then_inc(ksq_done, 1)

            def keys(n, j, par, t):
                act.wait_ge(ktp_ready, n * 2 + (j + 1))
                act.activation(kT[:, par, j * GRP:(j + 1) * GRP, t * P:(t + 1) * P],
                               ktp[:].rearrange("p (g n) -> p g n", g=GRP), ACT.Copy).then_inc(kT_done, 1)

            def values(n, j, par, t):
                act.wait_ge(v_ready, n * 2 + (j + 1))
                act.activation(vv[:, par, t, j * COLS:(j + 1) * COLS], vp[:], ACT.Copy).then_inc(v_done, 1)

            def exps(h, slot):
                act.wait_ge(nmax_done, h + 1)
                wait(act, ptp_ready, h - 1)
                act.activation(pr[:, slot, :], sm[:] if with_mask else scp[:, 0:NK], ACT.Exp,
                               bias=nmax[:, slot:slot + 1], accum_out=den[:, slot:slot + 1]).then_inc(exp_done, 1)

            def head_hi(h, par, j):
                wait(act, s_ready, h)
                act.activation(k_hi[:], kT[:, par, j, :], ACT.Copy)
                act.activation(q_hi[:], qcur[:, par, j, :], ACT.Copy).then_inc(head_hi_done, 1)

            def run(pair, par):
                attend = attends(pair, par)
                if par == 0 and not isinstance(pair, int):
                    make_hi(pair, 0, 0)
                for t in range(CHUNKS):
                    n, h = chunk_no(pair, par, t), head_no(pair, par, t)
                    if attend:
                        exps(h, 0)
                    if not (t == CHUNKS - 1 and par == 1):
                        make_hi(pair, par, t + 1)
                    square(n, 0)
                    if attend:
                        head_hi(h + 1, 1 - par, t * HPC + 1)
                    square(n, 1)
                    values(n, 0, par, t)
                    keys(n, 0, par, t)
                    if t == CHUNKS - 1:
                        act.wait_ge(q_in[par], pair * (16 * Q_LOADS) + 16 * Q_LOADS)
                        act.wait_ge(kT_done, n * 2 + 1)
                        head_hi(h + 2, par, 0)
                    elif attend:
                        head_hi(h + 2, 1 - par, (t + 1) * HPC)
                    if attend:
                        exps(h + 1, 1)
                    values(n, 1, par, t)
                    keys(n, 1, par, t)

            over_batches(act, run)
            for j in range(KVH):
                exps((B - 1) * KVH + j, j % 2)
                if j == 0:
                    act.wait_ge(k_ready, B * CHUNKS * 2)
                    act.wait_ge(v_ready, B * CHUNKS * 2)
                for at in range(j * proj.ahead * DC // KVH, (j + 1) * proj.ahead * DC // KVH):
                    proj.split_chunk_hi(act, at)

        @block.vector
        def _(dve):
            def key_sums(n, j):
                dve.wait_ge(ksq_done, n * 2 + (j + 1))
                dve.tensor_reduce(kss[:, j, :], ksq[:].rearrange("p (g n) -> p g n", g=GRP), AX.X,
                                  ALU.add).then_inc(kss_done, 1)
                dve.wait_ge(kss_done, n * 2 + (j + 1))
                dve.tensor_scalar(kms[:, j, :], kss[:, j, :], 1.0 / HD, eps, ALU.mult, ALU.add).then_inc(kms_done, 1)

            def key_scale(n, j):
                dve.wait_ge(krr_done, n * 2 + (j + 1))
                wait(dve, ktp_ready, n * 2 + (j - 1))
                dve.tensor_tensor(khat[:, j, :].rearrange("p (g n) -> p g n", g=GRP),
                                  kp[j][:].rearrange("p (g n) -> p g n", g=GRP),
                                  krr[:, j, :].unsqueeze(2).to_broadcast([P, GRP, HD]), ALU.mult).then_inc(khat_done, 1)

            def row_max(h, slot):
                dve.wait_ge(s_ready, h + 1)
                if with_mask:
                    wait(dve, exp_done, h)
                    dve.tensor_tensor(sm[:], scp[:, 0:KEYS], mask[:], ALU.add).then_inc(sm_done, 1)
                    dve.wait_ge(sm_done, h + 1)
                    dve.tensor_reduce(nmax[:, slot:slot + 1], sm[:], AX.X, ALU.max,
                                      negate=True).then_inc(nmax_done, 1)
                else:
                    dve.tensor_reduce(nmax[:, slot:slot + 1], scp[:, 0:NK], AX.X, ALU.max,
                                      negate=True).then_inc(nmax_done, 1)

            def normalise(h, slot):
                dve.wait_ge(exp_done, h + 1)
                dve.reciprocal(rden[:, slot:slot + 1], den[:, slot:slot + 1]).then_inc(rden_done, 1)
                dve.wait_ge(rden_done, h + 1)
                dve.tensor_scalar(pr[:, slot, :], pr[:, slot, :], rden[:, slot:slot + 1], None,
                                  ALU.mult).then_inc(pn_done, 1)

            def probs(h, slot, lat=None):
                dve.wait_ge(ptp_ready, h + 1)
                if with_latents:
                    dve.tensor_copy(pTlat[:, slot, :], op[0:Q, P:2 * P] if lat is None else lat)
                dve.tensor_copy(pT[:, slot, :], ptp[:]).then_inc(pT_done, 1)

            def outputs(h, opar, j):
                dve.wait_ge(o_ready, h + 1)
                dve.tensor_copy(ocur[:, opar, j, :], op[:, 0:P]).then_inc(o_done, 1)

            def run(pair, par):
                attend = attends(pair, par)
                for t in range(CHUNKS):
                    n, h, j = chunk_no(pair, par, t), head_no(pair, par, t), t * HPC
                    if attend:
                        row_max(h, 0)
                        normalise(h, 0)
                        if t:
                            outputs(h - 1, 1 - par, j - 1)
                        elif not (isinstance(h, int) and h == 0):
                            outputs(h - 1, par, KVH - 1)
                    key_sums(n, 0)
                    key_scale(n, 0)
                    if attend:
                        probs(h, 0)
                    key_sums(n, 1)
                    if attend:
                        row_max(h + 1, 1)
                    key_scale(n, 1)
                    if attend:
                        normalise(h + 1, 1)
                        outputs(h, 1 - par, j)
                        probs(h + 1, 1)
                wait(dve, o_out[par], pair * 16)

            if with_mask:
                dve.wait_ge(m_in, 16 * GRP)
            over_batches(dve, run)
            last = (B - 1) * KVH
            for j in range(KVH):
                row_max(last + j, j % 2)
                if j == 0:
                    outputs(last - 1, 0, KVH - 1)
                else:
                    probs(last + j - 1, (j - 1) % 2, lat_last)
                normalise(last + j, j % 2)
                if j >= 2:
                    outputs(last + j - 2, 1, j - 2)
            probs(last + KVH - 1, (KVH - 1) % 2, lat_last)
            outputs(last + KVH - 2, 1, KVH - 2)
            outputs(last + KVH - 1, 1, KVH - 1)

        @block.gpsimd
        def _(pool):
            def make_lo(n, slot):
                pool.wait_ge(ct_hi_done, n + 1)
                pool.tensor_tensor(ct_lo[:, slot], ct_raw[:, slot], ct_hi[:, slot].bitcast(F32),
                                   ALU.subtract).then_inc(ct_lo_done, 1)

            def key_factor(n, j):
                pool.wait_ge(kms_done, n * 2 + (j + 1))
                wait(pool, khat_done, n * 2 + (j - 1))
                pool.tensor_tensor(krr[:, j, :], kms[:, j, :], c.minus_half[:, 0:GRP], ALU.pow).then_inc(krr_done, 1)

            def head_lo(h, par, j):
                pool.wait_ge(head_hi_done, h + 1)
                pool.tensor_tensor(q_lo[:], qcur[:, par, j, :], q_hi[:].bitcast(F32), ALU.subtract)
                pool.tensor_tensor(k_lo[:], kT[:, par, j, :], k_hi[:].bitcast(F32),
                                   ALU.subtract).then_inc(head_lo_done, 1)

            def run(pair, par):
                attend = attends(pair, par)
                if par == 0 and not isinstance(pair, int):
                    make_lo(chunk_no(pair, 0, 0), 0)
                for t in range(CHUNKS):
                    n, h = chunk_no(pair, par, t), head_no(pair, par, t)
                    if not (t == CHUNKS - 1 and par == 1):
                        make_lo(n + 1, (t + 1) % 2)
                    key_factor(n, 0)
                    if attend:
                        head_lo(h + 1, 1 - par, t * HPC + 1)
                    key_factor(n, 1)
                    if t == CHUNKS - 1:
                        head_lo(h + 2, par, 0)
                    elif attend:
                        head_lo(h + 2, 1 - par, (t + 1) * HPC)

            over_batches(pool, run)
            for g in range(proj.ahead):
                proj.split_lo(pool, g)

        @block.tensor
        def _(pe):
            def project_group(out, slot, cols):
                for k in range(DC):
                    last = split_matmul(pe, out, ct_hi[:, slot, k, :], ct_lo[:, slot, k, :], w_hi[:, k, cols],
                                        w_lo[:, k, cols], k == 0, k == DC - 1)
                return last

            def project_k(n, j, slot):
                wait(pe, khat_done, n * 2 + (j - 1))
                project_group(kp[j][:], slot, slice(j * COLS, (j + 1) * COLS)).then_inc(k_ready, 1)

            def project_v(n, j, slot):
                wait(pe, v_done, n * 2 + j)
                cols = slice(KVH * HD + j * COLS, KVH * HD + (j + 1) * COLS)
                project_group(vp[:], slot, cols).then_inc(v_ready, 1)

            def turn_keys(n, j):
                pe.wait_ge(khat_done, n * 2 + (j + 1))
                wait(pe, kT_done, n * 2 + j)
                for g in range(GRP):
                    last = pe.transpose(ktp[:, g * P:(g + 1) * P], khat[:, j, g * P:(g + 1) * P], c.ident[:])
                last.then_inc(ktp_ready, 1)

            def scores(h, j, par, split=True):
                wait(pe, sm_done if with_mask else exp_done, h)
                if split:
                    pe.wait_ge(head_lo_done, h + 1)
                    last = split_matmul(pe, scp[:, 0:KEYS], q_hi[:], q_lo[:], k_hi[:], k_lo[:], True, True)
                else:
                    last = pe.matmul(scp[:, 0:KEYS], qcur[:, par, j, :], kT[:, par, j, :], start=True, stop=True)
                if with_latents:
                    last = pe.matmul(scp[:, KEYS:NK], qcur[:, par, j, :], klat[:, par, j, :], start=True, stop=True)
                last.then_inc(s_ready, 1)

            def turn_probs(h, slot, lat=None):
                pe.wait_ge(pn_done, h + 1)
                wait(pe, pT_done, h)
                if with_latents:
                    if lat is None:
                        wait(pe, o_done, h)
                        lat = op[0:Q, P:2 * P]
                    pe.transpose(lat, pr[:, slot, KEYS:NK], c.ident[:])
                for k in range(CHUNKS):
                    last = pe.transpose(ptp[:, k * P:(k + 1) * P], pr[:, slot, k * P:(k + 1) * P], c.ident[:])
                last.then_inc(ptp_ready, 1)

            def weigh(h, slot, j, par):
                pe.wait_ge(pT_done, h + 1)
                wait(pe, o_done, h)
                for k in range(CHUNKS):
                    last = pe.matmul(op[:, 0:P], vv[:, par, k, j * HD:(j + 1) * HD], pT[:, slot, k * P:(k + 1) * P],
                                     start=k == 0, stop=k == CHUNKS - 1 and not with_latents)
                if with_latents:
                    last = pe.matmul(op[:, 0:P], vlat[:, par, j * HD:(j + 1) * HD], pTlat[:, slot, :],
                                     start=False, stop=True)
                last.then_inc(o_ready, 1)

            def run(pair, par):
                attend = attends(pair, par)
                opar = 1 - par
                if attend:
                    pe.wait_ge(q_in[opar], (pair + par) * (16 * Q_LOADS))
                for t in range(CHUNKS):
                    n, h, j, slot = chunk_no(pair, par, t), head_no(pair, par, t), t * HPC, t % 2
                    if attend:
                        scores(h, j, opar)
                    pe.wait_ge(ct_lo_done, n + 1)
                    project_k(n, 0, slot)
                    if attend and t:
                        weigh(h - 1, 1, j - 1, opar)
                    elif attend and not (isinstance(h, int) and h == 0):
                        weigh(h - 1, 1, KVH - 1, par)
                    project_k(n, 1, slot)
                    if attend:
                        turn_probs(h, 0)
                    project_v(n, 0, slot)
                    turn_keys(n, 0)
                    if attend:
                        scores(h + 1, j + 1, opar)
                    if attend:
                        if t == 0:
                            pe.wait_ge(v_done, n * 2)
                        weigh(h, 0, j, opar)
                    project_v(n, 1, slot)
                    turn_keys(n, 1)
                    if attend:
                        turn_probs(h + 1, 1)

            over_batches(pe, run)
            last = (B - 1) * KVH
            pe.wait_ge(q_in[1], B // 2 * 16 * Q_LOADS)
            pe.wait_ge(kT_done, B * CHUNKS * 2)
            scores(last, 0, 1)
            weigh(last - 1, 1, KVH - 1, 0)
            pe.wait_ge(v_done, B * CHUNKS * 2)
            for j in range(KVH):
                if j + 1 < KVH:
                    scores(last + j + 1, j + 1, 1, split=False)
                turn_probs(last + j, j % 2, lat_last)
                if j:
                    weigh(last + j - 1, (j - 1) % 2, j - 1, 1)
            weigh(last + KVH - 1, (KVH - 1) % 2, KVH - 1, 1)


class Accumulate:

    def __init__(self, c, st, tag, w_dram, rows, a_hi=None, a_lo=None, o_dram=None, weights=None, out=None, ahead=0):
        sb, ps, sem = tiles(st, c.nc)
        self.c, self.w_dram, self.rows, self.a_hi, self.a_lo, self.ahead = c, w_dram, rows, a_hi, a_lo, ahead
        self.groups = (len(rows) + DC - 1) // DC
        self.raw, self.wh, self.wl = weights or (sb(f"{tag}_raw", [P, 2, DC, D]), sb(f"{tag}_wh", [P, 2, DC, D], F32R),
                                                 sb(f"{tag}_wl", [P, 2, DC, D], F32R))
        self.slots = self.wh.shape[1]
        self.tag = tag
        if out:
            self.out = out
        self.w_in = [[sem(f"{tag}_w_in{i}{k}") for k in range(DC)] for i in range(2)]
        self.hi_done, self.lo_done, self.used, self.summed = (sem(f"{tag}_{n}") for n in (
            "hi_done", "lo_done", "used", "summed"))
        self.o_dram = o_dram
        if o_dram is not None:
            self.o_out = [sem(f"{tag}_o_out{i}") for i in range(2)]

    def open(self, st):
        sb, ps, sem = tiles(st, self.c.nc)
        tag = self.tag
        self.out = [ps(f"{tag}_out{t}", [P, D])[:] for t in range(TT)]
        if self.o_dram is not None:
            self.oraw = sb(f"{tag}_oraw", [P, 2, B, GRP * Q])
            self.oh = sb(f"{tag}_oh", [P, 2, GRP, TOK], F32R)
            self.ol = sb(f"{tag}_ol", [P, 2, GRP, TOK], F32R)
            self.oh_done, self.ol_done = sem(f"{tag}_oh_done"), sem(f"{tag}_ol_done")
            self.o_in = [[sem(f"{tag}_o_in{i}{t}") for t in range(TT)] for i in range(2)]

    def by_batch(self, halves, g, t):
        return halves[:, g % 2, :, t * P:(t + 1) * P].rearrange("p g (b n) -> p b g n", b=BT)

    def raw_by_batch(self, g, t):
        return self.oraw[:, g % 2, t * BT:(t + 1) * BT].rearrange("p b (g n) -> p b g n", g=GRP)

    def chunks(self, g):
        return [(g * DC + k, k, n) for k, n in enumerate(self.rows[g * DC:(g + 1) * DC])]

    def load(self, sp, g):
        for at, k, n in self.chunks(g):
            if g >= 2:
                sp.wait_ge(self.lo_done, at - 2 * DC + 1)
            sp.dma_start(self.raw[0:n, g % 2, k, :], self.w_dram[g][0:n, k, :]).then_inc(self.w_in[g % 2][k], 16)

    def split_chunk_hi(self, act, at):
        g, k, n = at // DC, at % DC, self.rows[at]
        act.wait_ge(self.w_in[g % 2][k], 16 * (g // 2 + 1))
        if g >= self.slots:
            act.wait_ge(self.used, g - self.slots + 1)
        act.activation(self.wh[0:n, g % self.slots, k, :], self.raw[0:n, g % 2, k, :], ACT.Copy).then_inc(self.hi_done, 1)

    def split_hi(self, act, g):
        for at, _, _ in self.chunks(g):
            self.split_chunk_hi(act, at)

    def split_lo(self, eng, g):
        for at, k, n in self.chunks(g):
            eng.wait_ge(self.hi_done, at + 1)
            eng.tensor_tensor(self.wl[0:n, g % self.slots, k, :], self.raw[0:n, g % 2, k, :],
                              self.wh[0:n, g % self.slots, k, :].bitcast(F32), ALU.subtract).then_inc(self.lo_done, 1)

    def product(self, pe, chunk, tiles_of=range(TT)):
        g, k = chunk // DC, chunk % DC
        pe.wait_ge(self.lo_done, chunk + 1)
        n, w = self.rows[chunk], (self.wh, self.wl)
        for t in tiles_of:
            toks = slice(t * P, (t + 1) * P)
            if self.o_dram is not None:
                hi, lo = self.oh[:, g % 2, k, toks], self.ol[:, g % 2, k, toks]
            else:
                hi, lo = self.a_hi[0:n, chunk, toks], self.a_lo[0:n, chunk, toks]
            last = split_matmul(pe, self.out[t], hi, lo, w[0][0:n, g % self.slots, k, :], w[1][0:n, g % self.slots, k, :],
                                chunk == 0, chunk == len(self.rows) - 1)
        if chunk in (g * DC + DC - 1, len(self.rows) - 1) and TT - 1 in tiles_of:
            last.then_inc(self.used, 1)

    def sync(self, sp):
        for g in range(self.groups):
            if self.o_dram is not None:
                if g >= 2:
                    sp.wait_ge(self.ol_done, TT * (g - 1))
                for t in range(TT):
                    mine = slice(t * BT, (t + 1) * BT)
                    if g == 0:
                        for i in range(2):
                            sp.wait_ge(self.o_out[i], 16 * BT // 2 * (t + 1))
                    sp.dma_start(self.oraw[:, g % 2, mine],
                                 self.o_dram[mine, :, g, :].rearrange("b p n -> p b n")).then_inc(self.o_in[g % 2][t], 16)
            if g >= self.ahead:
                self.load(sp, g)

    def scalar(self, act):
        for g in range(self.groups):
            if g >= self.ahead:
                self.split_hi(act, g)
            if self.o_dram is not None:
                if g >= 2:
                    act.wait_ge(self.used, g - 1)
                for t in range(TT):
                    act.wait_ge(self.o_in[g % 2][t], 16 * (g // 2 + 1))
                    act.activation(self.by_batch(self.oh, g, t), self.raw_by_batch(g, t), ACT.Copy).then_inc(self.oh_done, 1)

    def vector(self, dve):
        for g in range(self.groups):
            if g >= self.ahead:
                self.split_lo(dve, g)
            if self.o_dram is not None:
                for t in range(TT):
                    dve.wait_ge(self.oh_done, TT * g + t + 1)
                    dve.tensor_tensor(self.by_batch(self.ol, g, t), self.raw_by_batch(g, t),
                                      self.by_batch(self.oh, g, t).bitcast(F32), ALU.subtract).then_inc(self.ol_done, 1)
        self.sum(dve)

    def sum(self, dve):
        dve.wait_ge(self.used, self.groups)
        for t in range(TT):
            dve.tensor_tensor(self.c.x[:, t, :], self.c.x[:, t, :], self.out[t], ALU.add).then_inc(self.summed, 1)
        dve.wait_ge(self.summed, TT)

    def tensor(self, pe):
        for g in range(self.groups):
            if self.o_dram is None:
                for at, _, _ in self.chunks(g):
                    self.product(pe, at)
                continue
            for t in range(TT):
                pe.wait_ge(self.ol_done, TT * g + t + 1)
                for at, _, _ in self.chunks(g):
                    self.product(pe, at, [t])


def stage_accumulate(c, acc):
    with ExitStack() as st:
        acc.open(st)
        block = st.enter_context(c.nc.Block())

        @block.sync
        def _(sp):
            acc.sync(sp)

        @block.scalar
        def _(act):
            acc.scalar(act)

        @block.vector
        def _(dve):
            acc.vector(dve)

        @block.tensor
        def _(pe):
            acc.tensor(pe)


def stage_ffn(c, tag, wg_dram, wu_dram, wd_dram, width, xT_hi, xT_lo, hT_hi, hT_lo):
    nc = c.nc
    chunks = [min(P, width - P * f) for f in range((width + P - 1) // P)]
    n = len(chunks)
    RAW = 4
    per = COLS // P
    loads = 2 * ((n + per - 1) // per)
    with ExitStack() as st:
        sb, ps, sem = tiles(st, nc)
        raw = sb(f"{tag}_raw", [P, RAW, DC, COLS])
        wh = sb(f"{tag}_wh", [P, 4, DC, COLS], F32R)
        wl = sb(f"{tag}_wl", [P, 4, DC, COLS], F32R)
        g = sb(f"{tag}_g", [P, 2, TOK])
        h = sb(f"{tag}_h", [P, 2, TOK])
        gu = [ps(f"{tag}_gu{i}", [P, 2 * TOK]) for i in range(2)]
        w_in = [sem(f"{tag}_w_in{i}") for i in range(RAW)]
        hi_done, lo_done, gu_ready, g_done, h_done, hT_hi_done, hT_lo_done = (
            sem(f"{tag}_{x}") for x in ("hi_done", "lo_done", "gu_ready", "g_done", "h_done", "hT_hi_done",
                                        "hT_lo_done"))
        norm = LayerNorm(c, st, tag, xT_hi, xT_lo)
        down = Accumulate(c, st, f"{tag}_down", wd_dram, chunks, hT_hi, hT_lo)
        down.open(st)
        first = FirstWeights(c, st, tag, wg_dram[0], raw[:, 0], wh[:, 0], wl[:, 0], hi_done, lo_done)
        block = st.enter_context(nc.Block())

        @block.sync
        def _(sp):
            first.sync(sp)
            for q in range(1, loads):
                if q >= RAW:
                    sp.wait_ge(lo_done, q - RAW + 1)
                sp.dma_start(raw[:, q % RAW], (wu_dram if q % 2 else wg_dram)[q // 2]).then_inc(w_in[q % RAW], 16)
            down.sync(sp)

        @block.scalar
        def _(act):
            first_halves_scalar(act, norm, first)

            def make_hi(q):
                act.wait_ge(w_in[q % RAW], 16 * (q // RAW + (q % RAW > 0)))
                if q >= 4:
                    act.wait_ge(gu_ready, per * (q // 2 - 1))
                act.activation(wh[:, q % 4], raw[:, q % RAW], ACT.Copy).then_inc(hi_done, 1)

            for q in range(1, 4):
                make_hi(q)
            for f in range(n + 1):
                if f < n:
                    m = chunks[f]
                    act.wait_ge(gu_ready, f + 1)
                    if f >= 2:
                        act.wait_ge(h_done, f - 1)
                    act.activation(g[0:m, f % 2], gu[f % 2][0:m, 0:TOK], ACT.Silu).then_inc(g_done, 1)
                if f >= 1:
                    m = chunks[f - 1]
                    act.wait_ge(h_done, f)
                    act.activation(hT_hi[0:m, f - 1], h[0:m, (f - 1) % 2], ACT.Copy).then_inc(hT_hi_done, 1)
                if f == per - 1:
                    for q in range(4, loads):
                        make_hi(q)
                if f == 2 * per - 1:
                    down.split_hi(act, 0)
            for part in range(1, down.groups):
                down.split_hi(act, part)

        @block.vector
        def _(dve):
            first_halves_vector(dve, norm, first)

            def make_lo(q):
                dve.wait_ge(hi_done, q + 1)
                dve.tensor_tensor(wl[:, q % 4], raw[:, q % RAW], wh[:, q % 4].bitcast(F32),
                                  ALU.subtract).then_inc(lo_done, 1)

            for q in range(1, 4):
                make_lo(q)
            for f in range(n):
                m, b = chunks[f], f % 2
                dve.wait_ge(g_done, f + 1)
                if f >= 2:
                    dve.wait_ge(hT_lo_done, f - 1)
                dve.tensor_tensor(h[0:m, b], gu[b][0:m, TOK:], g[0:m, b], ALU.mult).then_inc(h_done, 1)
                if f == per - 1:
                    for q in range(4, loads):
                        make_lo(q)
                if f == 2 * per - 1:
                    down.split_lo(dve, 0)
            for part in range(1, down.groups):
                down.split_lo(dve, part)
            down.sum(dve)

        @block.gpsimd
        def _(pool):
            norm.gpsimd(pool)
            for f in range(n):
                m = chunks[f]
                pool.wait_ge(hT_hi_done, f + 1)
                pool.tensor_tensor(hT_lo[0:m, f], h[0:m, f % 2], hT_hi[0:m, f].bitcast(F32),
                                   ALU.subtract).then_inc(hT_lo_done, 1)

        @block.tensor
        def _(pe):
            norm.tensor(pe)
            pe.wait_ge(norm.done, TT)
            for f in range(n):
                m, b = chunks[f], f % 2
                if f >= 2:
                    pe.wait_ge(h_done, f - 1)
                cols = slice(f % per * P, f % per * P + m)
                for u in range(2):
                    q = (2 * (f // per) + u) % 4
                    if f or u:
                        pe.wait_ge(lo_done, 2 * (f // per) + u + 1)
                    for k in range(DC):
                        if f == u == 0:
                            first.wait(pe, k)
                        last = split_matmul(pe, gu[b][0:m, u * TOK:(u + 1) * TOK], wh[:, q, k, cols],
                                            wl[:, q, k, cols], xT_hi[:, k, :], xT_lo[:, k, :], k == 0, k == DC - 1)
                last.then_inc(gu_ready, 1)
            for f in range(n):
                pe.wait_ge(hT_lo_done, f + 1)
                down.product(pe, f)


NH, NKV, SHD = 32, 8, 16
SREP = NH // NKV


def stage_self_attention(c, w_dram, wo_dram, xT_hi, xT_lo, aT_hi, aT_lo):
    nc = c.nc
    HQ = NKV // 2
    NHK = NH * Q
    with ExitStack() as st:
        sb, ps, sem = tiles(st, nc)
        raw = sb("sa_raw", [P, DC, COLS + 2 * NKV * SHD])
        wh = sb("sa_wh", [P, DC, COLS + 2 * NKV * SHD], F32R)
        wl = sb("sa_wl", [P, DC, COLS + 2 * NKV * SHD], F32R)
        qT = sb("sa_qT", [P, SREP, TOK])
        diag8 = sb("sa_diag8", [P, NKV])
        diag4 = sb("sa_diag4", [P, HQ])
        causal = sb("sa_causal", [P, Q])
        kdiag = sb("sa_kdiag", [P, B, NKV, Q])
        vrep = sb("sa_vrep", [P, B, HQ, Q])
        vdiag = sb("sa_vdiag", [P, B, 2, HQ * SHD])
        sm = sb("sa_sm", [P, TT, NHK])
        ex = sb("sa_ex", [P, TT, NHK])
        mx = sb("sa_mx", [P, TT, NH])
        den = sb("sa_den", [P, TT, NH])
        rden = sb("sa_rden", [P, TT, NH])
        pT = sb("sa_pT", [P, TT, NHK])
        o = sb("sa_o", [P, TT, D])
        two = ps("sa_two", [P, 2 * COLS])
        kv = ps("sa_kv", [P, COLS])
        sc = [ps(f"sa_sc{t}", [P, NHK]) for t in range(TT)]
        (hi_done, lo_done, masks, masks0, q_ready, kv_ready, qT_done, kdiag_done, vrep_done, vt_ready, vdiag_done,
         s_ready, sm_done, mx_done, sub_done, ex_done, den_done, rden_done, pt_ready, pT_done, o_ready, o_done,
         at_ready, at_hi_done, at_lo_done) = (sem(f"sa_{n}") for n in (
             "hi_done", "lo_done", "masks", "masks0", "q_ready", "kv_ready", "qT_done", "kdiag_done",
             "vrep_done", "vt_ready", "vdiag_done", "s_ready", "sm_done", "mx_done", "sub_done", "ex_done",
             "den_done", "rden_done", "pt_ready", "pT_done", "o_ready", "o_done", "at_ready",
             "at_hi_done", "at_lo_done"))
        norm = LayerNorm(c, st, "sa", xT_hi, xT_lo, sc)
        proj = Accumulate(c, st, "sa_proj", wo_dram, [P] * SREP, aT_hi, aT_lo,
                          out=[two[:, t * D:(t + 1) * D] for t in range(TT)])
        first = FirstWeights(c, st, "sa", w_dram, raw, wh, wl, hi_done, lo_done)
        block = st.enter_context(nc.Block())

        @block.sync
        def _(sp):
            first.sync(sp)
            proj.sync(sp)

        @block.scalar
        def _(act):
            first_halves_scalar(act, norm, first)
            act.wait_ge(q_ready, 1)
            act.activation(qT[:].rearrange("p g n -> p (g n)"), two[:], ACT.Copy,
                           scale=float(SHD) ** -0.5).then_inc(qT_done, 1)
            act.wait_ge(kdiag_done, 1)
            act.activation(vrep[:], kv[:, TOK:].rearrange("p (b n) -> p b n", b=B).unsqueeze(2)
                           .to_broadcast([P, B, HQ, Q]), ACT.Copy).then_inc(vrep_done, 1)
            proj.scalar(act)
            for t in range(TT):
                act.wait_ge(sub_done, t + 1)
                act.activation(ex[:, t, :], sm[:, t, :], ACT.Exp).then_inc(ex_done, 1)
            for t in range(TT):
                act.wait_ge(pt_ready, t + 1)
                act.activation(pT[:, t, :], sc[t][:], ACT.Copy).then_inc(pT_done, 1)
            for t in range(TT):
                act.wait_ge(at_ready, t + 1)
                act.activation(aT_hi[:, :, t * P:(t + 1) * P], sc[t][:, 0:D].rearrange("p (g n) -> p g n", g=SREP),
                               ACT.Copy).then_inc(at_hi_done, 1)

        @block.gpsimd
        def _(pool):
            norm.gpsimd(pool)
            pool.memset(diag8[:], 1.0)
            pool.memset(diag4[:], 1.0)
            pool.memset(causal[:], 0.0).then_inc(masks0, 1)
            pool.wait_ge(masks0, 1)
            lowest = float(np.finfo(np.float32).min)
            for b in range(BT):
                rows = slice(b * Q, (b + 1) * Q)
                pool.affine_select(out=causal[rows, :], in_=causal[rows, :], compare_op=ALU.is_ge, fill=lowest,
                                   base=0, pattern=[[-1, Q]], channel_multiplier=1).then_inc(masks, 1)
                pool.wait_ge(masks, b + 1)
            at = BT
            for mask, width, cols in ((diag8, SHD, NKV), (diag4, Q, HQ)):
                for low in (True, False):
                    pool.affine_select(out=mask[:], in_=mask[:], compare_op=ALU.is_ge, fill=0.0,
                                       base=0 if low else width - 1, pattern=[[-width if low else width, cols]],
                                       channel_multiplier=1 if low else -1).then_inc(masks, 1)
                    at += 1
                    pool.wait_ge(masks, at)

        @block.vector
        def _(dve):
            first_halves_vector(dve, norm, first)
            dve.wait_ge(kv_ready, 1)
            dve.wait_ge(masks, BT + 4)
            dve.tensor_tensor(kdiag[:], kv[:, 0:TOK].rearrange("p (b n) -> p b n", b=B).unsqueeze(2)
                              .to_broadcast([P, B, NKV, Q]),
                              diag8[:].unsqueeze(1).unsqueeze(3).to_broadcast([P, B, NKV, Q]),
                              ALU.mult).then_inc(kdiag_done, 1)
            proj.split_lo(dve, 0)
            dve.wait_ge(vt_ready, 1)
            dve.tensor_tensor(vdiag[:].rearrange("p b u (j d) -> p (b u) j d", d=SHD),
                              two[:].rearrange("p (a j d) -> p a j d", j=HQ, d=SHD),
                              diag4[:].unsqueeze(1).unsqueeze(3).to_broadcast([P, 2 * B, HQ, SHD]),
                              ALU.mult).then_inc(vdiag_done, 1)
            for t in range(TT):
                s3 = sm[:, t, :].rearrange("p (h n) -> p h n", h=NH)
                dve.wait_ge(s_ready, t + 1)
                dve.tensor_tensor(s3, sc[t][:].rearrange("p (h n) -> p h n", h=NH),
                                  causal[:].unsqueeze(1).to_broadcast([P, NH, Q]), ALU.add).then_inc(sm_done, 1)
                dve.wait_ge(sm_done, t + 1)
                dve.tensor_reduce(mx[:, t, :], s3, AX.X, ALU.max).then_inc(mx_done, 1)
                dve.wait_ge(mx_done, t + 1)
                dve.tensor_tensor(s3, s3, mx[:, t, :].unsqueeze(2).to_broadcast([P, NH, Q]),
                                  ALU.subtract).then_inc(sub_done, 1)
            for t in range(TT):
                dve.wait_ge(ex_done, t + 1)
                dve.tensor_reduce(den[:, t, :], ex[:, t, :].rearrange("p (h n) -> p h n", h=NH), AX.X,
                                  ALU.add).then_inc(den_done, 1)
                dve.wait_ge(den_done, t + 1)
                dve.reciprocal(rden[:, t, :], den[:, t, :]).then_inc(rden_done, 1)
            for t in range(TT):
                dve.wait_ge(o_ready, t + 1)
                dve.wait_ge(rden_done, t + 1)
                dve.tensor_tensor(o[:, t, :].rearrange("p (h d) -> p h d", d=SHD),
                                  two[:, t * D:(t + 1) * D].rearrange("p (h d) -> p h d", d=SHD),
                                  rden[:, t, :].unsqueeze(2).to_broadcast([P, NH, SHD]), ALU.mult).then_inc(o_done, 1)
            for t in range(TT):
                dve.wait_ge(at_hi_done, t + 1)
                dve.tensor_tensor(aT_lo[:, :, t * P:(t + 1) * P], sc[t][:, 0:D].rearrange("p (g n) -> p g n", g=SREP),
                                  aT_hi[:, :, t * P:(t + 1) * P].bitcast(F32), ALU.subtract).then_inc(at_lo_done, 1)
            proj.sum(dve)

        @block.tensor
        def _(pe):
            norm.tensor(pe)
            pe.wait_ge(norm.done, TT)

            def project(out, col):
                for k in range(DC):
                    first.wait(pe, k)
                    cols = slice(col, col + P)
                    last = split_matmul(pe, out, wh[:, k, cols], wl[:, k, cols], xT_hi[:, k, :], xT_lo[:, k, :],
                                        k == 0, k == DC - 1)
                return last

            project(kv[:, 0:TOK], COLS)
            project(kv[:, TOK:], COLS + P).then_inc(kv_ready, 1)
            for g in range(SREP):
                last = project(two[:, g * TOK:(g + 1) * TOK], g * P)
            last.then_inc(q_ready, 1)
            pe.wait_ge(vrep_done, 1)
            pe.wait_ge(qT_done, 1)
            for b in range(B):
                last = pe.transpose(two[:, b * P:(b + 1) * P], vrep[:, b].rearrange("p r n -> p (r n)"), c.ident[:])
            last.then_inc(vt_ready, 1)
            pe.wait_ge(kdiag_done, 1)
            for t in range(TT):
                for b in range(BT):
                    for g in range(SREP):
                        last = pe.matmul(sc[t][b * Q:(b + 1) * Q, g * NKV * Q:(g + 1) * NKV * Q],
                                         qT[:, g, (t * BT + b) * Q:(t * BT + b + 1) * Q],
                                         kdiag[:, t * BT + b].rearrange("p j n -> p (j n)"), start=True, stop=True)
                last.then_inc(s_ready, 1)
            for t in range(TT):
                pe.wait_ge(ex_done, t + 1)
                for a in range(NHK // P):
                    last = pe.transpose(sc[t][:, a * P:(a + 1) * P], ex[:, t, a * P:(a + 1) * P], c.ident[:])
                last.then_inc(pt_ready, 1)
            pe.wait_ge(vdiag_done, 1)
            for t in range(TT):
                pe.wait_ge(pT_done, t + 1)
                for b in range(BT):
                    for a in range(NHK // P):
                        width = HQ * SHD
                        last = pe.matmul(two[b * Q:(b + 1) * Q, t * D + a * width:t * D + (a + 1) * width],
                                         pT[:, t, a * P + b * Q:a * P + (b + 1) * Q], vdiag[:, t * BT + b, a % 2, :],
                                         start=True, stop=True)
                last.then_inc(o_ready, 1)
            for t in range(TT):
                pe.wait_ge(o_done, t + 1)
                for g in range(SREP):
                    last = pe.transpose(sc[t][:, g * P:(g + 1) * P], o[:, t, g * P:(g + 1) * P], c.ident[:])
                last.then_inc(at_ready, 1)
            pe.wait_ge(at_lo_done, TT)
            proj.tensor(pe)


MD, MN, MK, MR = 1024, 16, 4, 32
MC = MD // P
MSP = MR + 2 * MN


def stage_scan_inputs(c, win_dram, small, conv_w, conv_b, xT_hi, xT_lo, u, sg):
    nc = c.nc
    groups = 2 * MD // COLS
    pairs = MC
    per = COLS // (2 * P)
    W = 2 * TOK
    with ExitStack() as st:
        sb, ps, sem = tiles(st, nc)
        raw = sb("mi_raw", [P, groups, DC, COLS])
        wh = sb("mi_wh", [P, groups, DC, COLS], F32R)
        wl = sb("mi_wl", [P, groups, DC, COLS], F32R)
        ux = sb("mi_ux", [P, 2, W])
        acc = sb("mi_acc", [P, 2, W])
        pj = [ps(f"mi_pj{i}", [P, W]) for i in range(4)]
        w_in = [sem(f"mi_w_in{i}") for i in range(groups)]
        hi_done, lo_done, pj_ready, ux_done, conv_done, acc_done, out_done = (
            sem(f"mi_{x}") for x in ("hi_done", "lo_done", "pj_ready", "ux_done", "conv_done", "acc_done",
                                     "out_done"))
        norm = LayerNorm(c, st, "mi", xT_hi, xT_lo)
        first = FirstWeights(c, st, "mi", win_dram[0], raw[:, 0], wh[:, 0], wl[:, 0], hi_done, lo_done)
        small_in = sem("mi_small_in")
        block = st.enter_context(nc.Block())

        @block.sync
        def _(sp):
            first.sync(sp)
            for g in range(1, groups):
                sp.dma_start(raw[:, g], win_dram[g]).then_inc(w_in[g], 16)
                if g == 1:
                    for dst, src in small:
                        sp.dma_start(dst[:], src).then_inc(small_in, 16)

        @block.scalar
        def _(act):
            first_halves_scalar(act, norm, first)

            def make_hi(g):
                act.wait_ge(w_in[g], 16)
                act.activation(wh[:, g], raw[:, g], ACT.Copy).then_inc(hi_done, 1)

            def activate(m):
                act.wait_ge(conv_done, (2 * MK - 1) * (m + 1))
                act.wait_ge(acc_done, m + 1)
                act.activation(u[:, 2 * m:2 * m + 2, :].rearrange("p c n -> p (c n)"), acc[:, m % 2],
                               ACT.Silu).then_inc(out_done, 1)

            make_hi(1)
            for m in range(pairs):
                if 1 <= m < groups - 1:
                    make_hi(m + 1)
                act.wait_ge(pj_ready, m + 1)
                if m >= pairs // 2:
                    act.activation(sg[:, 2 * m - MC:2 * m - MC + 2, :].rearrange("p c n -> p (c n)"), pj[m % 4][:],
                                   ACT.Silu).then_inc(out_done, 1)
                    continue
                if m >= 2:
                    act.wait_ge(acc_done, m - 1)
                act.activation(ux[:, m % 2], pj[m % 4][:], ACT.Copy).then_inc(ux_done, 1)
                if m:
                    activate(m - 1)
                if m == pairs // 2 - 1:
                    activate(m)

        def make_lo(eng, g):
            eng.wait_ge(hi_done, g + 1)
            eng.wait_ge(lo_done, g)
            eng.tensor_tensor(wl[:, g], raw[:, g], wh[:, g].bitcast(F32), ALU.subtract).then_inc(lo_done, 1)

        @block.gpsimd
        def _(pool):
            norm.gpsimd(pool)
            for g in range(2, groups):
                make_lo(pool, g)

        @block.vector
        def _(dve):
            first_halves_vector(dve, norm, first)

            taps = 0
            dve.wait_ge(small_in, 16 * len(small))
            make_lo(dve, 1)
            for m in range(pairs):
                b = m % 2
                gate = m >= pairs // 2
                if not gate:
                    dve.wait_ge(ux_done, m + 1)
                    if m >= 2:
                        dve.wait_ge(out_done, m - 1)
                    for tap in range(MK):
                        if tap:
                            dve.wait_ge(conv_done, taps)
                        for k in range(2):
                            ch = 2 * m + k
                            x3 = ux[:, b, k * TOK:(k + 1) * TOK].rearrange("p (b t) -> p b t", b=B)
                            a3 = acc[:, b, k * TOK:(k + 1) * TOK].rearrange("p (b t) -> p b t", b=B)
                            w = conv_w[:, ch, MK - 1 - tap:MK - tap]
                            if tap == 0:
                                dve.tensor_scalar(a3, x3, w, conv_b[:, ch:ch + 1], ALU.mult,
                                                  ALU.add).then_inc(conv_done, 1)
                            else:
                                last = dve.scalar_tensor_tensor(out=a3[:, :, tap:], in0=x3[:, :, :Q - tap], scalar=w,
                                                                in1=a3[:, :, tap:], op0=ALU.mult, op1=ALU.add)
                                last.then_inc(conv_done if tap < MK - 1 or k == 0 else acc_done, 1)
                            taps += not (tap == MK - 1 and k == 1)

        @block.tensor
        def _(pe):
            norm.tensor(pe)
            pe.wait_ge(norm.done, TT)
            for m in range(pairs):
                g = m // per
                if m:
                    pe.wait_ge(lo_done, g + 1)
                if m >= 4:
                    pe.wait_ge(ux_done, m - 3)
                for half in range(2):
                    col = (m % per * 2 + half) * P
                    for k in range(DC):
                        if m == half == 0:
                            first.wait(pe, k)
                        last = split_matmul(pe, pj[m % 4][:, half * TOK:(half + 1) * TOK], wh[:, g, k, col:col + P],
                                            wl[:, g, k, col:col + P], xT_hi[:, k, :], xT_lo[:, k, :],
                                            k == 0, k == DC - 1)
                last.then_inc(pj_ready, 1)


def stage_scan(c, wx, wdt, lnw, dt_bias, A, Dp, bc_dram, u, sg, yT_hi, yT_lo):
    nc = c.nc
    PARTS = MSP // MN
    W = 2 * TOK
    with ExitStack() as st:
        sb, ps, sem = tiles(st, nc)
        delta, du = sb("m_delta", [P, MC, TOK]), sb("m_du", [P, MC, TOK])
        b_all, c_all = sb("m_b", [P, MN, TOK]), sb("m_c", [P, MN, TOK])
        sq = sb("mp_sq", [P, TT, MSP])
        ss = sb("mp_ss", [P, TT, PARTS])
        s2 = sb("mp_s2", [P, TT])
        ms = sb("mp_ms", [P, TT, PARTS])
        rr = sb("mp_rr", [P, TT, PARTS])
        n1 = sb("mp_n1", [P, TT, MSP])
        n2 = sb("mp_n2", [P, TT, MSP])
        dtT = sb("mp_dtT", [MR, TOK])
        bcT = sb("mp_bcT", [2 * MN, TOK])
        ax = sb("mp_ax", [P, MC, TOK])
        dA = sb("sc_dA", [P, 2, MN, TOK])
        x = sb("sc_x", [P, 2, MN, TOK])
        h = sb("sc_h", [P, 2, MN, TOK])
        y1 = sb("sc_y1", [P, 2, TOK])
        y2 = sb("sc_y2", [P, 2, TOK])
        par = ps("mp_par", [P, TT * MSP])
        turn = ps("mp_turn", [MR, 2 * TOK])
        dl = [ps(f"mp_dl{m}", [P, W]) for m in range(MC // 2)]
        yp = [ps(f"sc_yp{i}", [P, TOK]) for i in range(2)]
        (par_ready, sq_done, ss_done, s2_done, s3_done, ms_done, rr_done, n1_done, n2_done, turn_ready, dtT_done,
         bcT_done, bc_out, b_in, c_in, dl_ready, xb_done, ax_done, e_done, l_done, d_done, du_done) = (
             sem(f"mp_{x}") for x in (
                 "par_ready", "sq_done", "ss_done", "s2_done", "s3_done", "ms_done", "rr_done", "n1_done",
                 "n2_done", "turn_ready", "dtT_done", "bcT_done", "bc_out", "b_in", "c_in", "dl_ready", "xb_done",
                 "ax_done", "e_done", "l_done", "d_done", "du_done"))
        dA_done, reset, x_done, x0_done, h_done, hc_done, y_ready, y1_done, y2_done, hi_done, lo_done = (
            sem(f"sc_{n}") for n in ("dA_done", "reset", "x_done", "x0_done", "h_done", "hc_done", "y_ready",
                                     "y1_done", "y2_done", "hi_done", "lo_done"))
        HALF = MN // 2
        block = st.enter_context(nc.Block())

        @block.sync
        def _(sp):
            sp.wait_ge(bcT_done, 1)
            sp.dma_start(bc_dram, bcT[:]).then_inc(bc_out, 16)
            sp.wait_ge(bc_out, 16)
            sp.dma_start(b_all[:], bc_dram[0:MN].unsqueeze(0).to_broadcast([P, MN, TOK])).then_inc(b_in, 16)
            sp.dma_start(c_all[:], bc_dram[MN:].unsqueeze(0).to_broadcast([P, MN, TOK])).then_inc(c_in, 16)

        @block.tensor
        def _(pe):
            for t in range(TT):
                for k in range(MC):
                    last = pe.matmul(par[:, t * MSP:(t + 1) * MSP], u[:, k, t * P:(t + 1) * P], wx[:, k, :],
                                     start=k == 0, stop=k == MC - 1)
            last.then_inc(par_ready, 1)
            pe.wait_ge(n2_done, 1)
            for t in range(TT):
                pe.transpose(turn[:, t * P:(t + 1) * P], n2[:, t, 0:MR], c.ident[:])
                last = pe.transpose(turn[:, TOK + t * P:TOK + (t + 1) * P], n2[:, t, MR:], c.ident[:])
            last.then_inc(turn_ready, 1)
            pe.wait_ge(dtT_done, 1)
            for ch in range(MC):
                last = pe.matmul(dl[ch // 2][:, ch % 2 * TOK:(ch % 2 + 1) * TOK], wdt[:, ch * P:(ch + 1) * P], dtT[:],
                                 start=True, stop=True)
                if ch % 2:
                    last.then_inc(dl_ready, 1)
            for k in range(MC):
                if k >= 2:
                    pe.wait_ge(y1_done, k - 1)
                for n in range(MN):
                    if n % HALF == 0:
                        pe.wait_ge(hc_done, 2 * k + n // HALF + 1)
                    last = pe.matmul(yp[k % 2][:], c.ident[:], h[:, k % 2, n, :], start=n == 0, stop=n == MN - 1)
                last.then_inc(y_ready, 1)

        @block.scalar
        def _(act):
            act.wait_ge(par_ready, 1)
            act.activation(sq[:].rearrange("p t n -> p (t n)"), par[:], ACT.Square).then_inc(sq_done, 1)
            act.wait_ge(turn_ready, 1)
            act.activation(dtT[:], turn[:, 0:TOK], ACT.Copy).then_inc(dtT_done, 1)
            act.activation(bcT[:], turn[:, TOK:], ACT.Copy).then_inc(bcT_done, 1)
            for m in range(MC // 2):
                act.wait_ge(xb_done, 2 * m + 2)
                act.activation(ax[:, 2 * m:2 * m + 2, :], delta[:, 2 * m:2 * m + 2, :], ACT.Abs).then_inc(ax_done, 1)
            act.wait_ge(ax_done, MC // 2)
            act.activation(ax[:], ax[:], ACT.Exp, scale=-1.0).then_inc(e_done, 1)
            act.wait_ge(e_done, 1)
            for m in range(MC // 2):
                act.activation(ax[:, 2 * m:2 * m + 2, :], ax[:, 2 * m:2 * m + 2, :], ACT.Ln, bias=1.0).then_inc(l_done, 1)

            def make_hi(k):
                act.wait_ge(y2_done, k + 1)
                act.activation(yT_hi[:, k, :], y2[:, k % 2], ACT.Copy).then_inc(hi_done, 1)

            for k in range(MC):
                act.wait_ge(d_done, k // 2 + 1)
                if k >= 2:
                    act.wait_ge(h_done, k - 1)
                for n in range(MN):
                    last = act.activation(dA[:, k % 2, n, :], delta[:, k, :], ACT.Exp, scale=A[:, k, n:n + 1])
                last.then_inc(dA_done, 1)
                if k >= 2:
                    make_hi(k - 2)
            make_hi(MC - 2)
            make_hi(MC - 1)

        @block.gpsimd
        def _(pool):
            pool.wait_ge(s3_done, 1)
            pool.tensor_scalar(ms[:], ss[:], 1.0 / MN, 1e-6, ALU.mult, ALU.add).then_inc(ms_done, 1)
            pool.wait_ge(ms_done, 1)
            pool.tensor_tensor(rr[:].rearrange("p t n -> p (t n)"), ms[:].rearrange("p t n -> p (t n)"),
                               c.minus_half[:, 0:TT * PARTS], ALU.pow).then_inc(rr_done, 1)

            def make_lo(k):
                pool.wait_ge(hi_done, k + 1)
                pool.tensor_tensor(yT_lo[:, k, :], y2[:, k % 2], yT_hi[:, k, :].bitcast(F32),
                                   ALU.subtract).then_inc(lo_done, 1)

            pool.wait_ge(b_in, 16)
            for k in range(MC):
                pool.wait_ge(du_done, k // 2 + 1)
                if k >= 2:
                    pool.wait_ge(h_done, k - 1)
                n = MN if k else HALF
                pool.tensor_tensor(x[:, k % 2, 0:n, :], du[:, k, :].unsqueeze(1).to_broadcast([P, n, TOK]),
                                   b_all[:, 0:n, :], ALU.mult).then_inc(x_done, 1)
                if k >= 3:
                    make_lo(k - 3)
            for k in range(MC - 3, MC):
                make_lo(k)

        @block.vector
        def _(dve):
            dve.wait_ge(sq_done, 1)
            dve.tensor_reduce(ss[:].rearrange("p t n -> p (t n)"), sq[:].rearrange("p t (n k) -> p (t n) k", k=MN), AX.X,
                              ALU.add).then_inc(ss_done, 1)
            dve.wait_ge(ss_done, 1)
            dve.tensor_tensor(s2[:], ss[:, :, 0], ss[:, :, 1], ALU.add).then_inc(s2_done, 1)
            dve.wait_ge(s2_done, 1)
            dve.tensor_scalar(ss[:, :, 0:2], s2[:].unsqueeze(2).to_broadcast([P, TT, 2]), float(MN) / MR, None,
                              ALU.mult).then_inc(s3_done, 1)
            dve.wait_ge(rr_done, 1)
            dve.tensor_tensor(n1[:].rearrange("p t (n k) -> p (t n) k", k=MN),
                              par[:].rearrange("p (n k) -> p n k", k=MN),
                              rr[:].rearrange("p t n -> p (t n)").unsqueeze(2).to_broadcast([P, TT * PARTS, MN]),
                              ALU.mult).then_inc(n1_done, 1)
            dve.wait_ge(n1_done, 1)
            dve.tensor_tensor(n2[:], n1[:], lnw[:].unsqueeze(1).to_broadcast([P, TT, MSP]), ALU.mult).then_inc(n2_done, 1)
            for ch in range(MC):
                dve.wait_ge(dl_ready, ch // 2 + 1)
                dve.tensor_scalar(delta[:, ch, :], dl[ch // 2][:, ch % 2 * TOK:(ch % 2 + 1) * TOK],
                                  dt_bias[:, ch:ch + 1], None, ALU.add).then_inc(xb_done, 1)
            for m in range(MC // 2):
                two = slice(2 * m, 2 * m + 2)
                dve.wait_ge(l_done, m + 1)
                dve.wait_ge(ax_done, m + 1)
                dve.scalar_tensor_tensor(out=delta[:, two, :], in0=delta[:, two, :], scalar=0.0, in1=ax[:, two, :],
                                         op0=ALU.max, op1=ALU.add).then_inc(d_done, 1)
                dve.wait_ge(d_done, m + 1)
                dve.tensor_tensor(du[:, two, :], delta[:, two, :], u[:, two, :], ALU.mult).then_inc(du_done, 1)
            dve.wait_ge(b_in, 16)
            dve.wait_ge(du_done, 1)
            dve.tensor_tensor(x[:, 0, HALF:, :], du[:, 0, :].unsqueeze(1).to_broadcast([P, MN - HALF, TOK]),
                              b_all[:, HALF:, :], ALU.mult).then_inc(x0_done, 1)
            dve.wait_ge(x0_done, 1)
            dve.wait_ge(c_in, 16)

            def finish(k):
                dve.wait_ge(y_ready, k + 1)
                dve.scalar_tensor_tensor(out=y1[:, k % 2], in0=u[:, k, :], scalar=Dp[:, k:k + 1], in1=yp[k % 2][:],
                                         op0=ALU.mult, op1=ALU.add).then_inc(y1_done, 1)
                dve.wait_ge(y1_done, k + 1)
                if k >= 2:
                    dve.wait_ge(lo_done, k - 1)
                dve.tensor_tensor(y2[:, k % 2], y1[:, k % 2], sg[:, k, :], ALU.mult).then_inc(y2_done, 1)

            for k in range(MC):
                b = k % 2
                dve.wait_ge(dA_done, k + 1)
                dve.memset(dA[:, b].rearrange("p n (b t) -> p (n b) t", t=Q)[:, :, 0:1], 0.0).then_inc(reset, 1)
                dve.wait_ge(reset, k + 1)
                dve.wait_ge(x_done, k + 1)
                if k >= 2:
                    dve.wait_ge(y_ready, k - 1)
                dve.tensor_tensor_scan(h[:, b].rearrange("p n t -> p (n t)"), dA[:, b].rearrange("p n t -> p (n t)"),
                                       x[:, b].rearrange("p n t -> p (n t)"), 0.0, ALU.mult,
                                       ALU.add).then_inc(h_done, 1)
                dve.wait_ge(h_done, k + 1)
                for half in (slice(0, HALF), slice(HALF, MN)):
                    dve.tensor_tensor(h[:, b, half], h[:, b, half], c_all[:, half, :], ALU.mult).then_inc(hc_done, 1)
                if k:
                    finish(k - 1)
            finish(MC - 1)


OC = 8
OIN, OHID = D // OC, 1366 // OC
OHALF = OHID // 2


def octonion_signs():
    table = np.zeros((OC, OC, OC), np.int64)
    table[0, 0, 0] = 1
    for i in range(1, OC):
        table[0, i, i] = table[i, 0, i] = 1
        table[i, i, 0] = -1
    for a, b, d in [(1, 2, 3), (1, 4, 5), (1, 7, 6), (2, 4, 6), (2, 5, 7), (3, 4, 7), (3, 6, 5)]:
        for x, y, z in ((a, b, d), (b, d, a), (d, a, b)):
            table[x, y, z], table[y, x, z] = 1, -1
    return [[int(table[i ^ k, i, k]) for k in range(OC)] for i in range(OC)]


class Ternary:

    NAMES = ("gate", "up", "down")
    SHAPES = ([P, OC, OHID], [P, OC, OHID], [OHALF, OC, 2, OIN])
    FLAT = ("p a b -> p (a b)", "p a b -> p (a b)", "p a b c -> p (a b c)")
    COUNT = OC * OHID * OIN

    def __init__(self, c, st, w_drams):
        sb, ps, sem = tiles(st, c.nc)
        self.nc, self.w_drams, self.sign = c.nc, w_drams, octonion_signs()
        self.m_gate, self.m_up = (sb(f"o_m_{n}", [P, OC // 2, OC, OHID], F32R) for n in ("gate", "up"))
        self.m_down = sb("o_m_down", [OHALF, 2, OC, D], F32R)
        self.scales = sb("o_scales", [P, 3])
        self.w = [sb(f"te_w_{n}", s) for n, s in zip(self.NAMES, self.SHAPES)]
        self.low = sb("te_low", [P, OC * OHID])
        self.tern = [sb(f"te_tern_{n}", [s[0], 2, *s[1:]], F32R) for n, s in zip(self.NAMES, self.SHAPES)]
        self.ones = sb("te_ones", [P, P])
        self.sums = sb("te_sums", [P, 3])
        self.half = sb("te_half", [P, 3])
        self.mhalf = sb("te_mhalf", [P, 3])
        self.w_in = [sem(f"te_w_in_{n}") for n in self.NAMES]
        (self.ones_done, self.sum_done, self.total_ready, self.scales_done, self.half_done, self.mhalf_done,
         self.low_done, self.pos_done, self.neg_done, self.spread, self.down_even, self.down_odd) = (sem(f"te_{n}") for n in (
             "ones_done", "sum_done", "total_ready", "scales_done", "half_done", "mhalf_done", "low_done", "pos_done",
             "neg_done", "spread", "down_even", "down_odd"))

    def open(self, st):
        _, ps, _ = tiles(st, self.nc)
        self.total = [ps(f"te_total_{n}", [P, 1]) for n in self.NAMES]

    def sync(self, sp):
        for i in range(2):
            for rows in (slice(0, OIN), slice(OIN, 2 * OIN)):
                sp.dma_start(self.w[i][rows], self.w_drams[i]).then_inc(self.w_in[i], 16)
        sp.dma_start(self.w[2][:], self.w_drams[2]).then_inc(self.w_in[2], 16)

    def tensor(self, pe, i):
        n = (OIN, OIN, OHALF)[i]
        pe.wait_ge(self.ones_done, 1)
        pe.wait_ge(self.sum_done, i + 1)
        pe.matmul(self.total[i][:], self.ones[0:n, :], self.sums[0:n, i:i + 1], start=True,
                  stop=True).then_inc(self.total_ready, 1)

    def spread_in(self, copy, which, m, i):
        rows, chunk = slice(i % 2 * OIN, (i % 2 + 1) * OIN), i // 2
        for k in range(OC):
            neg = int(self.sign[i][k] < 0)
            last = copy(m[rows, chunk, k, :], self.tern[which][rows, neg, i ^ k, :])
        last.then_inc(self.spread, 1)

    def spread_down(self, copy, i):
        for k in range(OC):
            neg = int(self.sign[i][k] < 0)
            last = copy(self.m_down[:, :, i, k * OIN:(k + 1) * OIN], self.tern[2][:, neg, i ^ k, :, :])
        last.then_inc(self.down_odd if i % 2 else self.down_even, 1)

    def gpsimd_ones(self, pool):
        pool.memset(self.ones[:], 1.0).then_inc(self.ones_done, 1)

    def gpsimd(self, pool, i):
        pool.wait_ge(self.neg_done, 2)
        self.spread_in(pool.tensor_copy, 1, self.m_up, i)

    def scalar_sums(self, act):
        for i in range(3):
            n = self.SHAPES[i][0]
            act.wait_ge(self.w_in[i], 16 if i == 2 else 32)
            act.activation(self.tern[i][:, 1].bitcast(F32).rearrange(self.FLAT[i]), self.w[i][:].rearrange(self.FLAT[i]),
                           ACT.Abs, accum_out=self.sums[0:n, i:i + 1]).then_inc(self.sum_done, 1)

    def vector_scales(self, dve, i):
        dve.wait_ge(self.total_ready, i + 1)
        for out, factor, done in ((self.scales, 1.0, self.scales_done), (self.half, 0.5, self.half_done),
                                  (self.mhalf, -0.5, self.mhalf_done)):
            dve.tensor_scalar(out[:, i:i + 1], self.total[i][:], factor / self.COUNT, None, ALU.mult).then_inc(done, 1)
        dve.wait_ge(self.half_done, i + 1)
        dve.wait_ge(self.mhalf_done, i + 1)

    def vector_round(self, dve, i):
        n = self.SHAPES[i][0]
        wf = self.w[i][:].rearrange(self.FLAT[i])
        lf = self.low[0:n, 0:wf.shape[1]]
        if i:
            dve.wait_ge(self.pos_done, i)
        dve.tensor_scalar(lf, wf, self.mhalf[0:n, i:i + 1], None, ALU.is_lt).then_inc(self.low_done, 1)
        dve.wait_ge(self.low_done, i + 1)
        dve.scalar_tensor_tensor(out=self.tern[i][:, 0].rearrange(self.FLAT[i]), in0=wf,
                                 scalar=self.half[0:n, i:i + 1], in1=lf, op0=ALU.is_gt,
                                 op1=ALU.subtract).then_inc(self.pos_done, 1)

    def vector_spread_gate(self, dve):
        dve.wait_ge(self.neg_done, 1)
        for i in range(0, OC, 2):
            self.spread_in(dve.tensor_copy, 0, self.m_gate, i)

    def vector_spread_up(self, dve):
        dve.wait_ge(self.neg_done, 2)
        for i in range(4, OC, 2):
            self.spread_in(dve.tensor_copy, 1, self.m_up, i)

    def down_vector(self, dve, part):
        dve.wait_ge(self.neg_done, 3)
        self.spread_down(dve.tensor_copy, 2 * part)

    def scalar(self, act):
        self.copy = lambda out, in_: act.activation(out, in_.bitcast(F32), ACT.Copy)

        def negate(i):
            act.wait_ge(self.pos_done, i + 1)
            act.activation(self.tern[i][:, 1], self.tern[i][:, 0].bitcast(F32), ACT.Copy,
                           scale=-1.0).then_inc(self.neg_done, 1)
            act.wait_ge(self.neg_done, i + 1)

        negate(0)
        self.spread_in(self.copy, 0, self.m_gate, 1)
        negate(1)
        for i in (3, 5, 7):
            self.spread_in(self.copy, 0, self.m_gate, i)
        for i in (1, 3, 5, 7):
            self.spread_in(self.copy, 1, self.m_up, i)
        negate(2)

    def down_scalar(self, act, part):
        act.wait_ge(self.neg_done, 3)
        self.spread_down(self.copy, 2 * part + 1)


def stage_scan_output(c, acc, ternary, xT_hi, xT_lo):
    with ExitStack() as st:
        norm = LayerNorm(c, st, "oc", xT_hi, xT_lo)
        acc.open(st)
        ternary.open(st)
        block = st.enter_context(c.nc.Block())

        @block.sync
        def _(sp):
            acc.load(sp, 0)
            ternary.sync(sp)
            acc.sync(sp)

        @block.scalar
        def _(act):
            acc.split_hi(act, 0)
            ternary.scalar_sums(act)
            acc.scalar(act)
            ternary.scalar(act)
            for t in range(TT):
                norm.scalar(act, t)

        @block.vector
        def _(dve):
            acc.split_lo(dve, 0)
            for i in range(3):
                ternary.vector_scales(dve, i)
                ternary.vector_round(dve, i)
                if i + 1 < acc.groups:
                    acc.split_lo(dve, i + 1)
            ternary.vector_spread_gate(dve)
            acc.sum(dve)
            norm.vector(dve)
            ternary.vector_spread_up(dve)
            for t in range(TT):
                norm.vector_lo(dve, t)

        @block.gpsimd
        def _(pool):
            ternary.gpsimd_ones(pool)
            ternary.gpsimd(pool, 0)
            norm.gpsimd(pool)
            ternary.gpsimd(pool, 2)

        @block.tensor
        def _(pe):
            at = 0
            for i in range(3):
                ternary.tensor(pe, i)
                for _ in range(2 if i < 2 else MC - 4):
                    acc.product(pe, at)
                    at += 1
            norm.tensor(pe)


def stage_octonion(c, ternary, xT_hi, xT_lo, out_dram):
    nc = c.nc
    NB = 4
    LAG = 3
    n = 2 * OC
    m_gate, m_up, m_down, scales = ternary.m_gate, ternary.m_up, ternary.m_down, ternary.scales
    with ExitStack() as st:
        sb, ps, sem = tiles(st, nc)
        g = sb("oc_g", [OHALF, 2, TOK])
        h = sb("oc_h", [OHALF, 2, TOK])
        hT_hi = sb("oc_hT_hi", [OHALF, n, TOK], F32R)
        hT_lo = sb("oc_hT_lo", [OHALF, n, TOK], F32R)
        gu = [ps(f"oc_gu{i}", [OHALF, 2 * TOK]) for i in range(NB)]
        out = [ps(f"oc_out{t}", [P, D]) for t in range(TT)]
        gu_ready, g_done, h_done, hi_done, lo_done, out_ready, sum_done = (
            sem(f"oc_{x}") for x in ("gu_ready", "g_done", "h_done", "hi_done", "lo_done", "out_ready", "sum_done"))
        out_done = sem("out_done")
        block = st.enter_context(nc.Block())

        @block.sync
        def _(sp):
            for t in range(TT):
                sp.wait_ge(sum_done, t + 1)
                sp.dma_start(out_dram[t * P:(t + 1) * P, :], c.x[:, t, :]).then_inc(out_done, 16)
            sp.wait_ge(out_done, 16 * TT)

        @block.tensor
        def _(pe):
            def down(f):
                comp, hh = f // 2, f % 2
                pe.wait_ge(ternary.down_odd if comp % 2 else ternary.down_even, comp // 2 + 1)
                pe.wait_ge(lo_done, f + 1)
                for t in range(TT):
                    toks = slice(t * P, (t + 1) * P)
                    w = m_down[:, hh, comp, :]
                    pe.matmul(out[t][:], hT_hi[:, f, toks], w, start=f == 0, stop=False)
                    last = pe.matmul(out[t][:], hT_lo[:, f, toks], w, start=False, stop=f == n - 1)
                return last

            for f in range(n):
                comp, hh = f // 2, f % 2
                if f >= NB:
                    pe.wait_ge(h_done, f - NB + 1)
                for u, m in enumerate((m_gate, m_up)):
                    for k in range(DC):
                        w = m[:, k, comp, hh * OHALF:(hh + 1) * OHALF]
                        dst = gu[f % NB][:, u * TOK:(u + 1) * TOK]
                        pe.matmul(dst, w, xT_hi[:, k, :], start=k == 0, stop=False)
                        last = pe.matmul(dst, w, xT_lo[:, k, :], start=False, stop=k == DC - 1)
                last.then_inc(gu_ready, 1)
                if f >= LAG:
                    down(f - LAG)
            for f in range(n - LAG, n):
                last = down(f)
            last.then_inc(out_ready, 1)

        @block.scalar
        def _(act):
            for f in range(n + 1):
                if f < n:
                    act.wait_ge(gu_ready, f + 1)
                    if f >= 2:
                        act.wait_ge(h_done, f - 1)
                    act.activation(g[:, f % 2], gu[f % NB][:, 0:TOK], ACT.Silu,
                                   scale=scales[0:OHALF, 0:1]).then_inc(g_done, 1)
                if f:
                    act.wait_ge(h_done, f)
                    act.activation(hT_hi[:, f - 1], h[:, (f - 1) % 2], ACT.Copy).then_inc(hi_done, 1)
                if f % 2 == 0 and f < OC:
                    ternary.down_scalar(act, f // 2)

        @block.gpsimd
        def _(pool):
            for f in range(n):
                pool.wait_ge(hi_done, f + 1)
                pool.tensor_tensor(hT_lo[:, f], h[:, f % 2], hT_hi[:, f].bitcast(F32), ALU.subtract).then_inc(lo_done, 1)

        @block.vector
        def _(dve):
            for f in range(n):
                b = f % 2
                dve.wait_ge(g_done, f + 1)
                if f >= 2:
                    dve.wait_ge(lo_done, f - 1)
                dve.scalar_tensor_tensor(out=h[:, b], in0=gu[f % NB][:, TOK:], scalar=scales[0:OHALF, 1:2], in1=g[:, b],
                                         op0=ALU.mult, op1=ALU.mult).then_inc(h_done, 1)
                if f % 2 == 0 and f < OC:
                    ternary.down_vector(dve, f // 2)
            dve.wait_ge(out_ready, 1)
            for t in range(TT):
                dve.scalar_tensor_tensor(out=c.x[:, t, :], in0=out[t][:], scalar=scales[:, 2:3], in1=c.x[:, t, :],
                                         op0=ALU.mult, op1=ALU.add).then_inc(sum_done, 1)
            dve.wait_ge(sum_done, TT)


def build(nc, t, out):
    c = Ctx()
    c.nc = nc
    with ExitStack() as st:
        sb, ps, sem = tiles(st, nc)
        c.x = sb("x_res", [P, TT, D])
        c.ident = sb("ident", [P, P])
        c.minus_half = sb("minus_half", [P, 8])
        q_dram = nc.dram_tensor("q_scratch", (B, P, KVH, GRP * Q), F32).ap()
        o_dram = nc.dram_tensor("o_scratch", (B, P, KVH, GRP * Q), F32).ap()
        klat_dram = nc.dram_tensor("klat_scratch", (B, P, KVH, Q), F32).ap()
        vlat_dram = nc.dram_tensor("vlat_scratch", (B, Q, KVH * HD), F32).ap()
        stage_constants(c, t["x"])

        def cross(layer, eps, mask):
            tag = f"x{layer}"
            lat = layer == 1
            with ExitStack() as s2:
                sb, _, _ = tiles(s2, nc)
                w_hi = sb(f"{tag}_w_hi", [P, DC, KVCOLS], F32R)
                w_lo = sb(f"{tag}_w_lo", [P, DC, KVCOLS], F32R)
                chunks = context_chunks(nc, s2, tag)
                ocur = sb(f"{tag}_ocur", [P, 2, KVH, GRP * Q])
                stored = [sem(f"{tag}_stored{i}") for i in range(2)]
                with ExitStack() as s3:
                    sb3, _, _ = tiles(s3, nc)
                    xT_hi = sb3(f"{tag}_xT_hi", [P, DC, TOK], F32R)
                    xT_lo = sb3(f"{tag}_xT_lo", [P, DC, TOK], F32R)
                    stage_queries(c, f"{tag}_q", chunks, ocur, stored, t["ctxT"], t[f"wq{layer}"], t[f"wkv{layer}"],
                                  (t[f"qn{layer}"], t[f"kn{layer}"]), eps, xT_hi, xT_lo, w_hi, w_lo, q_dram,
                                  klat_dram if lat else None, vlat_dram if lat else None)
                assert D == COLS
                slots = [w[:].rearrange("p k (s n) -> p s k n", n=D) for w in (w_hi, w_lo)]
                raw = sb(f"{tag}_o_raw", [P, 2, DC, D])
                proj = Accumulate(c, s2, f"{tag}_o", t[f"wo{layer}"], [P] * (KVH * GRP), o_dram=o_dram,
                                  weights=(raw, *slots), ahead=2)
                stage_context(c, f"{tag}_c", chunks, ocur, stored, proj, t["ctxT"], mask, eps, w_hi, w_lo, q_dram,
                              klat_dram if lat else None, vlat_dram if lat else None, o_dram)
                stage_accumulate(c, proj)

        with own_semaphores(nc):
            cross(0, 1e-5, t["mask"])

            with ExitStack() as s2:
                sb, _, _ = tiles(s2, nc)
                aT_hi, aT_lo = sb("aT_hi", [P, SREP, TOK], F32R), sb("aT_lo", [P, SREP, TOK], F32R)
                with ExitStack() as s3:
                    sb, _, _ = tiles(s3, nc)
                    xT_hi, xT_lo = sb("sa_xT_hi", [P, DC, TOK], F32R), sb("sa_xT_lo", [P, DC, TOK], F32R)
                    stage_self_attention(c, t["sa_w"], t["sa_wo"], xT_hi, xT_lo, aT_hi, aT_lo)

        with own_semaphores(nc):
            with ExitStack() as s2:
                sb, _, _ = tiles(s2, nc)
                F = FFN
                nf = (F + P - 1) // P
                hT_hi, hT_lo = sb("ffn_hT_hi", [P, nf, TOK], F32R), sb("ffn_hT_lo", [P, nf, TOK], F32R)
                with ExitStack() as s3:
                    sb, _, _ = tiles(s3, nc)
                    xT_hi, xT_lo = sb("ffn_xT_hi", [P, DC, TOK], F32R), sb("ffn_xT_lo", [P, DC, TOK], F32R)
                    stage_ffn(c, "ffn", t["ffn_wg"], t["ffn_wu"], t["ffn_wd"], F, xT_hi, xT_lo, hT_hi, hT_lo)

            cross(1, 1e-6, None)

        with ExitStack() as s2:
            sb, _, _ = tiles(s2, nc)
            yT_hi, yT_lo = sb("m_yT_hi", [P, MC, TOK], F32R), sb("m_yT_lo", [P, MC, TOK], F32R)
            with ExitStack() as s3:
                sb, _, _ = tiles(s3, nc)
                u, sg = sb("m_u", [P, MC, TOK]), sb("m_sg", [P, MC, TOK])
                conv_w, conv_b, dt_bias = (sb("m_conv_w", [P, MC, MK]), sb("m_conv_b", [P, MC]),
                                           sb("m_dt_bias", [P, MC]))
                A, Dp = sb("m_A", [P, MC, MN]), sb("m_Dp", [P, MC])
                wx, wdt, lnw = sb("m_wx", [P, MC, MSP]), sb("m_wdt", [MR, MD]), sb("m_lnw", [P, MSP])
                small = [(conv_w, t["conv_w"]), (conv_b, t["conv_b"]), (dt_bias, t["dt_bias"]), (A, t["A"]),
                               (Dp, t["Dp"]), (wx, t["wx"]), (wdt, t["wdt"]),
                               (lnw, t["scan_lnw"].unsqueeze(0).to_broadcast([P, MSP]))]
                with ExitStack() as s4:
                    sb, _, _ = tiles(s4, nc)
                    xT_hi, xT_lo = sb("mi_xT_hi", [P, DC, TOK], F32R), sb("mi_xT_lo", [P, DC, TOK], F32R)
                    stage_scan_inputs(c, t["win"], small, conv_w, conv_b, xT_hi, xT_lo, u, sg)
                bc_dram = nc.dram_tensor("bc_scratch", (2 * MN, TOK), F32).ap()
                stage_scan(c, wx, wdt, lnw, dt_bias, A, Dp, bc_dram, u, sg, yT_hi, yT_lo)
            ternary = Ternary(c, s2, (t["og"], t["ou"], t["od"]))
            sb, _, _ = tiles(s2, nc)
            xT_hi, xT_lo = sb("o_xT_hi", [P, DC, TOK], F32R), sb("o_xT_lo", [P, DC, TOK], F32R)
            with ExitStack() as s3:
                acc = Accumulate(c, s3, "m_out", t["wout"], [P] * MC, yT_hi, yT_lo, ahead=1)
                stage_scan_output(c, acc, ternary, xT_hi, xT_lo)
            stage_octonion(c, ternary, xT_hi, xT_lo, out)


def lay_out(i):
    f = lambda a: np.ascontiguousarray(np.asarray(a))

    def groups(w, cols=COLS):
        k, n = w.shape
        return f(w.reshape(k // P, P, n // cols, cols).transpose(2, 1, 0, 3))

    def rows(w):
        n, d = w.shape
        g = -(-n // (DC * P))
        full = np.zeros((g * DC * P, d), w.dtype)
        full[:n] = w
        return f(full.reshape(g, DC, P, d).transpose(0, 2, 1, 3))

    a = {}
    a["x"] = f(i["x"]).reshape(TOK, D)
    ctx = np.asarray(i["ctx_4096"])
    a["ctxT"] = f(ctx.reshape(B * CHUNKS, P, DC, P).transpose(0, 3, 2, 1))
    a["mask"] = f(i["mask_1x1xSxS2_ff0"]).reshape(Q, KEYS)
    n = lambda k: np.asarray(i[k])
    a["wq0"], a["wq1"] = groups(n("L0_xattn_Wq").T), groups(n("L1_xattn_Wq"))
    a["wkv0"] = np.concatenate([groups(n("L0_xattn_Wk").T), groups(n("L0_xattn_Wv").T)])
    a["wkv1"] = np.concatenate([groups(n("L1_xattn_Wk")), groups(n("L1_xattn_Wv"))])
    a["wo0"], a["wo1"] = rows(n("L0_xattn_Wo").T), rows(n("L1_xattn_Wo"))
    for layer in (0, 1):
        a[f"qn{layer}"], a[f"kn{layer}"] = f(n(f"L{layer}_xattn_q_norm_w")), f(n(f"L{layer}_xattn_k_norm_w"))

    def by_group(w, axis):
        w = np.moveaxis(w, axis, 0)
        w = w.reshape(NKV, SREP, SHD, -1).transpose(1, 0, 2, 3).reshape(D, -1)
        return np.moveaxis(w, 0, axis)

    sa_w = np.concatenate([by_group(n("L0_attn_wq"), 1), n("L0_attn_wk"), n("L0_attn_wv")], 1)
    a["sa_w"] = groups(sa_w, sa_w.shape[1])[0]
    a["sa_wo"] = rows(by_group(n("L0_attn_wo"), 0))

    def padded(w):
        full = np.zeros((D, -(-w.shape[1] // COLS) * COLS), w.dtype)
        full[:, :w.shape[1]] = w
        return groups(full)

    a["ffn_wg"], a["ffn_wu"] = padded(n("L0_ffn_W_gate").T), padded(n("L0_ffn_W_up").T)
    a["ffn_wd"] = rows(n("L0_ffn_W_down").T)

    def channels(w):
        return f(np.moveaxis(w.reshape(MC, P, *w.shape[1:]), 0, 1))

    a["win"] = groups(n("L1_attn_W_in").T)
    a["conv_w"], a["conv_b"] = channels(n("L1_attn_conv_w")), channels(n("L1_attn_conv_b"))
    a["dt_bias"], a["A"], a["Dp"] = (channels(n(f"L1_attn_{k}")) for k in ("dt_bias", "A", "D_param"))
    a["wx"], a["wdt"] = channels(n("L1_attn_Wx").T), f(n("L1_attn_Wdt").T)
    a["scan_lnw"] = np.concatenate([n("L1_attn_dt_ln_w"), n("L1_attn_b_ln_w"), n("L1_attn_c_ln_w")])
    a["wout"] = rows(n("L1_attn_W_out").T)
    a["og"], a["ou"] = (f(n(f"L1_ffn_w_{k}").transpose(2, 0, 1)) for k in ("gate", "up"))
    a["od"] = f(n("L1_ffn_w_down").reshape(OC, OIN, 2, OHALF).transpose(3, 0, 2, 1))
    return a


def kernel(**inputs):
    import concourse.bacc as bacc
    from concourse.bass_utils import run_bass_kernel_spmd

    nc = bacc.Bacc("TRN2", target_bir_lowering=False, num_devices=1)
    arrays = lay_out(inputs)
    tensors = {k: nc.dram_tensor(k, a.shape, mybir.dt.from_np(a.dtype), kind="ExternalInput").ap()
               for k, a in arrays.items()}
    out = nc.dram_tensor("out", (TOK, D), F32, kind="ExternalOutput").ap()
    build(nc, tensors, out)
    got = run_bass_kernel_spmd(nc, [arrays], core_ids=[0]).results[0]["out"]
    return got.reshape(B, Q, D)
```
